# Optimizing a Trainium2 kernel written in Bass

```python
import numpy as np
import jax
import jax.numpy as jnp

def _softmax(x, axis=-1):
    return jax.nn.softmax(x, axis=axis)

def _gelu(x):
    return jax.nn.gelu(x, approximate=True)

def _silu(x):
    return jax.nn.silu(x)

def _sigmoid(x):
    return jax.nn.sigmoid(x)

def _layernorm(x, axis=-1, eps=1e-05):
    m = jnp.mean(x, axis=axis, keepdims=True)
    v = jnp.var(x, axis=axis, keepdims=True)
    return (x - m) / jnp.sqrt(v + eps)

def _scatter_add(tgt, idx, src, axis=0):
    return tgt.at[idx].add(src)

def _segment_sum(src, seg, n):
    return jax.ops.segment_sum(src, seg, n)
kernel_name = 'mk_adj_ffn_d2_adj_r2_d42aa0'

def setup_inputs(seed: int=0):
    np.random.seed(seed)
    _w = jnp.asarray

    def _rec_inputs():
        import jax
        import jax.numpy as jnp
        _gk = jax.random.key(seed)
        x = -0.0005207 + 1.001 * jax.random.normal(jax.random.fold_in(_gk, 1), (8192, 128), jnp.float32)
        _a = jax.random.bernoulli(jax.random.fold_in(_gk, 2), 0.00195312, (8192, 8192))
        _a = jnp.logical_or(_a, jnp.swapaxes(_a, -1, -2))
        _a = jnp.logical_or(_a, jnp.eye(8192, dtype=bool))
        _af = _a.astype(jnp.float32)
        _af = _af * jax.random.uniform(jax.random.fold_in(_gk, 3), (8192, 8192), jnp.float32, 0.05, 5.41998)
        adj = _af
        return (x, adj)
    x, adj = _rec_inputs()

    def _L0_gnn_setup():
        import jax, jax.numpy as jnp
        import numpy as np
        N = 4096
        D = 128
        OUT = 128
        AVG_DEG = 32
        key = jax.random.key(seed)
        k1, k2, k3, k4, k5 = jax.random.split(key, 5)
        node_features = jax.random.normal(k1, (N, D), dtype=jnp.float32)
        edge_features = jax.random.normal(k2, (N, N), dtype=jnp.float32)
        u = jax.random.uniform(k3, (N, N), dtype=jnp.float32)
        adj = jnp.where(u < AVG_DEG / N, 1.0, 0.0).astype(jnp.float32)
        stdv = 1.0 / np.sqrt(OUT)
        weight = jax.random.uniform(k4, (2 * D + 1, OUT), minval=-stdv, maxval=stdv, dtype=jnp.float32)
        bias = jax.random.uniform(k5, (OUT,), minval=-stdv, maxval=stdv, dtype=jnp.float32)
        return {'node_features': node_features, 'edge_features': edge_features, 'adj': adj, 'weight': weight, 'bias': bias}
    _L0_gnn_all = _L0_gnn_setup()
    _L0_gnn_in = {k: v for k, v in _L0_gnn_all.items() if k in ('weight', 'bias')}
    del _L0_gnn_all

    def _L0_ffn_setup():
        import jax, jax.numpy as jnp
        import numpy as np
        NUM_EXPERTS = 8
        TOP_K = 2
        B, S, D = (8, 4096, 128)

        def _moe(tokens, router_w, w1, b1, w2, b2):
            N = tokens.shape[0]
            E = router_w.shape[0]
            logits = tokens.astype(jnp.float32) @ router_w.astype(jnp.float32).T
            probs = jax.nn.softmax(logits, axis=-1)
            rw, re = jax.lax.top_k(probs, TOP_K)
            if TOP_K > 1:
                rw = rw / jnp.maximum(rw.sum(-1, keepdims=True), 1e-12)
            rw = rw.astype(tokens.dtype)
            combine = jnp.zeros((N, E), tokens.dtype).at[jnp.arange(N)[:, None], re].set(rw)
            out = tokens
            for e in range(E):
                h = jax.nn.gelu(tokens @ w1[e] + b1[e], approximate=False)
                y = h @ w2[e] + b2[e]
                out = out + combine[:, e:e + 1] * y
            return out
        key = jax.random.key(seed)
        ks = jax.random.split(key, 4)
        scale = 1.0 / np.sqrt(D).astype(np.float32)
        return {'input_embeddings': jax.random.normal(ks[0], (B, S, D), jnp.float32), 'router_w': jax.random.normal(ks[1], (NUM_EXPERTS, D), jnp.float32) * scale, 'w1': jax.random.normal(ks[2], (NUM_EXPERTS, D, D), jnp.float32) * scale, 'b1': jnp.zeros((NUM_EXPERTS, D), jnp.float32), 'w2': jax.random.normal(ks[3], (NUM_EXPERTS, D, D), jnp.float32) * scale, 'b2': jnp.zeros((NUM_EXPERTS, D), jnp.float32)}
    _L0_ffn_all = _L0_ffn_setup()
    _L0_ffn_in = {k: v for k, v in _L0_ffn_all.items() if k in ('router_w', 'w1', 'b1', 'w2', 'b2')}
    del _L0_ffn_all

    def _L1_gnn_setup():
        import jax, jax.numpy as jnp
        import numpy as np
        N = 4096
        F_IN = 128
        F_OUT = 128
        key = jax.random.key(seed)
        k1, k2, k3, k4 = jax.random.split(key, 4)
        return {'input': jax.random.normal(k1, (N, F_IN), dtype=jnp.float32), 'adj': jax.random.uniform(k2, (N, N), dtype=jnp.float32), 'weight': jax.random.normal(k3, (F_IN, F_OUT), dtype=jnp.float32) * (1.0 / np.sqrt(F_OUT)), 'bias': jax.random.normal(k4, (F_OUT,), dtype=jnp.float32) * (1.0 / np.sqrt(F_OUT))}
    _L1_gnn_all = _L1_gnn_setup()
    _L1_gnn_in = {k: v for k, v in _L1_gnn_all.items() if k in ('weight', 'bias')}
    del _L1_gnn_all

    def _L1_ffn_setup():
        import jax, jax.numpy as jnp
        import numpy as np
        D_MODEL = 128
        EXPERT_DIM = 256
        NUM_EXPERTS = 8
        TOP_K = 2
        SEQ_LEN = 1024
        BATCH = 2
        key = jax.random.key(seed)
        ks = jax.random.split(key, 8)
        s = 0.02
        x = jax.random.normal(ks[0], (SEQ_LEN, BATCH, D_MODEL), dtype=jnp.float32)
        Wg = jax.random.normal(ks[1], (D_MODEL, NUM_EXPERTS), dtype=jnp.float32) * s
        bg = jax.random.normal(ks[2], (NUM_EXPERTS,), dtype=jnp.float32) * s
        bias = jnp.zeros((NUM_EXPERTS,), dtype=jnp.float32)
        W1 = jax.random.normal(ks[3], (NUM_EXPERTS, D_MODEL, EXPERT_DIM), dtype=jnp.float32) * s
        b1 = jax.random.normal(ks[4], (NUM_EXPERTS, EXPERT_DIM), dtype=jnp.float32) * s
        W2 = jax.random.normal(ks[5], (NUM_EXPERTS, EXPERT_DIM, D_MODEL), dtype=jnp.float32) * s
        b2 = jax.random.normal(ks[6], (NUM_EXPERTS, D_MODEL), dtype=jnp.float32) * s
        return {'x': x, 'Wg': Wg, 'bg': bg, 'bias': bias, 'W1': W1, 'b1': b1, 'W2': W2, 'b2': b2}
    _L1_ffn_all = _L1_ffn_setup()
    _L1_ffn_in = {k: v for k, v in _L1_ffn_all.items() if k in ('Wg', 'bg', 'bias', 'W1', 'b1', 'W2', 'b2')}
    del _L1_ffn_all
    return {'x': x, 'adj': adj, 'L0_gnn_weight': _L0_gnn_in['weight'], 'L0_gnn_bias': _L0_gnn_in['bias'], 'L0_ffn_router_w': _L0_ffn_in['router_w'], 'L0_ffn_w1': _L0_ffn_in['w1'], 'L0_ffn_b1': _L0_ffn_in['b1'], 'L0_ffn_w2': _L0_ffn_in['w2'], 'L0_ffn_b2': _L0_ffn_in['b2'], 'L1_gnn_weight': _L1_gnn_in['weight'], 'L1_gnn_bias': _L1_gnn_in['bias'], 'L1_ffn_Wg': _L1_ffn_in['Wg'], 'L1_ffn_bg': _L1_ffn_in['bg'], 'L1_ffn_bias': _L1_ffn_in['bias'], 'L1_ffn_W1': _L1_ffn_in['W1'], 'L1_ffn_b1': _L1_ffn_in['b1'], 'L1_ffn_W2': _L1_ffn_in['W2'], 'L1_ffn_b2': _L1_ffn_in['b2']}

def reference(x, adj, L0_gnn_weight, L0_gnn_bias, L0_ffn_router_w, L0_ffn_w1, L0_ffn_b1, L0_ffn_w2, L0_ffn_b2, L1_gnn_weight, L1_gnn_bias, L1_ffn_Wg, L1_ffn_bg, L1_ffn_bias, L1_ffn_W1, L1_ffn_b1, L1_ffn_W2, L1_ffn_b2):
    import jax
    import jax.numpy as jnp

    def _L0_gnn_ref(node_features, edge_features, adj, weight, bias):
        import jax, jax.numpy as jnp
        import numpy as np
        N = 4096
        D = 128
        OUT = 128
        AVG_DEG = 32
        neighbor_node_features = adj @ node_features
        neighbor_edge_features = jnp.einsum('ij,ji->i', adj, edge_features)[:, None]
        support = jnp.concatenate((node_features, neighbor_node_features, neighbor_edge_features), axis=1)
        return support @ weight + bias

    def _L0_ffn_ref(input_embeddings, router_w, w1, b1, w2, b2):
        import jax, jax.numpy as jnp
        import numpy as np
        NUM_EXPERTS = 8
        TOP_K = 2
        B, S, D = (8, 4096, 128)

        def _moe(tokens, router_w, w1, b1, w2, b2):
            N = tokens.shape[0]
            E = router_w.shape[0]
            logits = tokens.astype(jnp.float32) @ router_w.astype(jnp.float32).T
            probs = jax.nn.softmax(logits, axis=-1)
            rw, re = jax.lax.top_k(probs, TOP_K)
            if TOP_K > 1:
                rw = rw / jnp.maximum(rw.sum(-1, keepdims=True), 1e-12)
            rw = rw.astype(tokens.dtype)
            combine = jnp.zeros((N, E), tokens.dtype).at[jnp.arange(N)[:, None], re].set(rw)
            out = tokens
            for e in range(E):
                h = jax.nn.gelu(tokens @ w1[e] + b1[e], approximate=False)
                y = h @ w2[e] + b2[e]
                out = out + combine[:, e:e + 1] * y
            return out
        b, s, d = input_embeddings.shape
        tokens = input_embeddings.reshape(b * s, d)
        return _moe(tokens, router_w, w1, b1, w2, b2).reshape(b, s, d)

    def _L1_gnn_ref(input, adj, weight, bias):
        import jax, jax.numpy as jnp
        import numpy as np
        N = 4096
        F_IN = 128
        F_OUT = 128
        n = input.shape[0]
        a = adj + jnp.eye(n, dtype=adj.dtype)
        d = jax.lax.rsqrt(jnp.sum(a, axis=1))
        adj_norm = d[:, None] * a * d[None, :]
        support = input @ weight
        out = adj_norm @ support + bias
        return out

    def _L1_ffn_ref(x, Wg, bg, bias, W1, b1, W2, b2):
        import jax, jax.numpy as jnp
        import numpy as np
        D_MODEL = 128
        EXPERT_DIM = 256
        NUM_EXPERTS = 8
        TOP_K = 2
        SEQ_LEN = 1024
        BATCH = 2
        x_flat = x.reshape(-1, D_MODEL)
        gate_logits = x_flat @ Wg + bg + bias
        topk_vals, topk_idx = jax.lax.top_k(gate_logits, TOP_K)
        topk_w = jax.nn.softmax(topk_vals, axis=-1)
        combine = (jax.nn.one_hot(topk_idx, NUM_EXPERTS, dtype=x.dtype) * topk_w[..., None]).sum(axis=1)
        h = jax.nn.relu(jnp.einsum('td,edh->teh', x_flat, W1) + b1)
        y = jnp.einsum('teh,ehd->ted', h, W2) + b2
        out = jnp.einsum('ted,te->td', y, combine)
        return out.reshape(x.shape)
    x = x + _L0_gnn_ref(_layernorm(x, axis=-1), adj, adj, L0_gnn_weight, L0_gnn_bias)
    x = x + _L0_ffn_ref(_layernorm(x, axis=-1)[None], L0_ffn_router_w, L0_ffn_w1, L0_ffn_b1, L0_ffn_w2, L0_ffn_b2)[0]
    x = x + _L1_gnn_ref(_layernorm(x, axis=-1), adj, L1_gnn_weight, L1_gnn_bias)
    x = x + _L1_ffn_ref(_layernorm(x, axis=-1)[None], L1_ffn_Wg, L1_ffn_bg, L1_ffn_bias, L1_ffn_W1, L1_ffn_b1, L1_ffn_W2, L1_ffn_b2)[0]
    return x

_drawn_inputs = setup_inputs


def setup_inputs(seed=0):
    import zlib

    import numpy as np

    out = dict(_drawn_inputs(seed))
    spreads = {'L0_ffn_b1': (0.0, 2.0), 'L0_ffn_b2': (0.0, 0.8), 'L1_ffn_bias': (0.0, 0.8)}
    factors = {'L0_gnn_bias': 8.0,
     'L1_gnn_bias': 8.0,
     'L1_ffn_Wg': 8.0,
     'L1_ffn_bg': 8.0,
     'L1_ffn_W1': 8.0,
     'L1_ffn_b1': 37.874,
     'L1_ffn_W2': 8.0,
     'L1_ffn_b2': 64.0}
    for name, (base, spread) in spreads.items():
        noise = np.random.default_rng([zlib.crc32(name.encode()), seed]).standard_normal(out[name].shape)
        drawn = base * np.exp(spread * noise) if base else spread * noise
        out[name] = jnp.asarray(drawn.astype(out[name].dtype))
    for name, factor in factors.items():
        out[name] = (out[name] * factor).astype(out[name].dtype)
    return out
```

```python
from contextlib import ExitStack

import concourse.bass as bass
from concourse import mybir

F32 = mybir.dt.float32
F32R = mybir.dt.float32r
I32 = mybir.dt.int32
U32 = mybir.dt.uint32
ACT = mybir.ActivationFunctionType
ALU = mybir.AluOpType
AX_X = mybir.AxisListType.X

P = 128
N = 8192
W = 512
PANELS = N // W
BLOCKS = N // P
BPP = W // P
TILE = BPP * W
HALF = TILE // 2
E = 8
EPS = 1e-5

RING1 = 5
RING3 = 4
PAIRS = PANELS // 2 - 1
RANKS = PAIRS + 1


class Chain:

    def __init__(self, eng, sem, start=0):
        self.eng, self.sem, self.base, self.n = eng, sem, start, 0

    def mark(self, ins):
        ins.then_inc(self.sem, 1)
        self.n += 1

    def value(self):
        return self.base + self.n

    def sync(self):
        self.eng.wait_ge(self.sem, self.base + self.n)

    def rebase(self, base):
        self.base, self.n = base, 0


def hold(engine, scrap):
    engine.tensor_tensor(scrap, scrap, scrap, ALU.mult)


def rsqrt_steps(nc, ch, v, r, t):
    ch.sync()
    ch.mark(nc.vector.tensor_scalar(t.bitcast(I32), v.bitcast(I32), 1, None, ALU.arith_shift_right))
    ch.sync()
    ch.mark(nc.vector.tensor_scalar(r.bitcast(I32), t.bitcast(I32), -1.0, float(0x5F3759DF), ALU.mult, ALU.add))
    for _ in range(3):
        newton_step(nc, ch, v, r, t)


def newton_step(nc, ch, v, r, t):
    ch.sync()
    ch.mark(nc.vector.tensor_tensor(t, v, r, ALU.mult))
    ch.sync()
    ch.mark(nc.vector.tensor_tensor(t, t, r, ALU.mult))
    ch.sync()
    ch.mark(nc.vector.tensor_scalar(t, t, -0.5, 1.5, ALU.mult, ALU.add))
    ch.sync()
    ch.mark(nc.vector.tensor_tensor(r, r, t, ALU.mult))


def program(nc, x, adj_tiles, w_gnn0, bias_gnn0, router_t, w1_0, b1_0, w2_0, b2_0,
            w_gnn1, bias_gnn1, gate_w, gate_b, gate_bias, w1_1, b1_1, w2_1, b2_1, out):
    base_dram = nc.dram_tensor("base_dram", [N, P], F32, kind="Internal").ap()
    xb_dram = nc.dram_tensor("xb_dram", [N, P], F32, kind="Internal").ap()
    c0_dram = nc.dram_tensor("c0_dram", [E, N], F32, kind="Internal").ap()
    c1_dram = nc.dram_tensor("c1_dram", [E, N], F32, kind="Internal").ap()

    def rows(t, p):
        return t[bass.ds(p * W, W), :].rearrange("(b p) d -> p b d", p=P)

    def adj_tile(col_panel, row_panel):
        return adj_tiles[bass.ds((col_panel * PANELS + row_panel) * P, P), :]

    with ExitStack() as keep:
        def maker(stack):
            def sb(name, shape, dt=F32):
                return stack.enter_context(nc.sbuf_tensor(name, shape, dt))
            return sb

        def sem(name):
            return keep.enter_context(nc.semaphore(name))

        bank = [keep.enter_context(nc.psum_tensor(f"bank{b}", [P, W], F32)) for b in range(8)]

        sb = maker(keep)
        ident = sb("ident", [P, P])
        ones = sb("ones", [P, 2])
        iota_i = sb("iota_i", [P, E], I32)
        iota_f = sb("iota_f", [P, E])
        w_self = sb("w_self", [P, P])
        w_nbr = sb("w_nbr", [P, P])
        w_last = sb("w_last", [P, P])
        w_edge = sb("w_edge", [P, P])
        bias0 = sb("bias0", [P, P])
        bias1 = sb("bias1", [P, P])
        w_l1 = sb("w_l1", [P, P])
        router = sb("router", [P, E])
        routerH = sb("routerH", [P, E], F32R)
        routerL = sb("routerL", [P, E], F32R)
        gate = sb("gate", [P, E])
        gateH = sb("gateH", [P, E], F32R)
        gateL = sb("gateL", [P, E], F32R)
        gate_row = sb("gate_row", [P, E])
        gate_row2 = sb("gate_row2", [P, E])
        b1s0 = sb("b1s0", [P, E])
        b2s0 = sb("b2s0", [E, P])
        b1s1 = sb("b1s1", [P, E, 2])
        b2s1 = sb("b2s1", [E, P])
        e_rows = sb("e_rows", [P, 9 * BLOCKS])
        scrap_v = sb("scrap_v", [P, 1])
        scrap_p = sb("scrap_p", [P, 1])
        row_sums = sb("row_sums", [P, 2, BPP])
        e_cols = sb("e_cols", [P, BLOCKS + BPP])
        e_cols8 = sb("e_cols8", [P, BLOCKS // 2])
        e_sum = sb("e_sum", [P, BLOCKS])
        rowsum = sb("rowsum", [P, BLOCKS])
        dinv = sb("dinv", [P, BLOCKS])
        mv = sb("mv", [P, BLOCKS, 2])
        rstd = sb("rstd", [P, BLOCKS])
        vpe = sb("vpe", [P, BLOCKS])
        tmp = sb("tmp", [P, BLOCKS])
        mark_u = ExitStack()
        sbu = maker(mark_u)
        w1H0 = sbu("w1H0", [P, E, P], F32R)
        w1L0 = sbu("w1L0", [P, E, P], F32R)
        w2H0 = sbu("w2H0", [P, E, P], F32R)
        w2L0 = sbu("w2L0", [P, E, P], F32R)
        stage = sbu("stage", [P, 2, E * P])
        padu = sbu("padu", [P, 2048])
        mark_u.close()
        raw3 = sb("raw3", [P, RING3, TILE])

        with ExitStack() as st:
            sb = maker(st)
            raw = sb("raw", [P, RING1, TILE])
            hi = sb("hi", [P, 3, HALF], F32R)
            lo = sb("lo", [P, 3, HALF], F32R)
            g0 = sb("g0", [P, BLOCKS, P])
            accT = sb("accT", [P, N])
            with ExitStack() as st0:
                sb0 = maker(st0)
                stats = sb0("stats", [P, BLOCKS, 6])
                nT = sb0("nT", [P, 2, W])
            iwF = sb("iwF", [P, W])
            iwH = sb("iwH", [P, W // 2], F32R)
            iwL = sb("iwL", [P, W // 2], F32R)
            jwH = sb("jwH", [P, 2, W], F32R)
            jwL = sb("jwL", [P, 2, W], F32R)
            prod = sb("prod", [P, 2, TILE])
            accP = sb("accP", [P, TILE])
        with ExitStack() as st:
            sb = maker(st)
            n1H = sb("n1H", [P, N], F32R)
            with ExitStack() as stl:
                n1L = maker(stl)("n1L", [P, N], F32R)
            yT = sb("yT", [P, N])
            xn = sb("xn", [P, BLOCKS, P])
            with ExitStack() as stz:
                sbz = maker(stz)
                accT_place = sbz("accT_place", [P, N])
                sbv = sbz
                stats2 = sbv("stats2", [P, BLOCKS, 6])
                bt = sbv("bt", [P, 4, W])
                nb = sbv("nb", [P, 2, W])
                lg = sbv("lg", [P, BLOCKS, E])
                mx = sbv("mx", [P, BLOCKS, E])
                ix = sbv("ix", [P, BLOCKS, E], U32)
                pr = sbv("pr", [P, BLOCKS, E])
                cw = sbv("cw", [P, BLOCKS, E])
                cts = sbv("cts", [E, 2, W])
            w1H1 = sb("w1H1", [P, E * 2 * P], F32R)
            w1L1 = sb("w1L1", [P, E * 2 * P], F32R)
            w2H1 = sb("w2H1", [P, E * 2 * P], F32R)
            w2L1 = sb("w2L1", [P, E * 2 * P], F32R)
            with ExitStack() as stv:
                sbv = maker(stv)
                h0 = sbv("h0", [P, 4, W])
                hH0 = sbv("hH0", [P, 2, W], F32R)
                hL0 = sbv("hL0", [P, 2, W], F32R)
                cb0 = sbv("cb0", [P, 4, W])
                ct0 = sbv("ct0", [E, W])
            with ExitStack() as stv:
                sbv = maker(stv)
                stats3 = sbv("stats3", [P, BLOCKS, 6])
                nb2 = sbv("nb2", [P, 2, W])
                nT2 = sbv("nT2", [P, 2, W])
                gf = sbv("gf", [P, 2, W])
        with ExitStack() as st:
            sb = maker(st)
            gH = sb("gH", [P, N], F32R)
            gL = sb("gL", [P, N], F32R)
            hi3 = sb("hi3", [P, 4, HALF], F32R)
            lo3 = sb("lo3", [P, 4, HALF], F32R)
            w_place = sb("w_place", [P, 4 * E * 2 * P])
            h1 = sb("h1", [P, 4, W])
            hH1 = sb("hH1", [P, 2, W], F32R)
            hL1 = sb("hL1", [P, 2, W], F32R)
            cb1 = sb("cb1", [P, 4, W])
            n3H = sb("n3H", [P, W], F32R)
            n3L = sb("n3L", [P, W], F32R)
            oT = sb("oT", [P, W])
            x3 = sb("x3", [P, W])
            nb3 = sb("nb3", [P, W])
            xbt = sb("xbt", [P, W])
            ct1 = nb3
            st3 = sb("st3", [P, BPP, 6])
            mv3 = sb("mv3", [P, BPP, 2])
            v3 = sb("v3", [P, BPP])
            r3 = sb("r3", [P, BPP])
            t3 = sb("t3", [P, BPP])
            lg3 = sb("lg3", [P, BPP, E])
            mx3 = sb("mx3", [P, BPP, E])
            ix3 = sb("ix3", [P, BPP, E], U32)
            if3 = sb("if3", [P, BPP, E])
            m13 = sb("m13", [P, BPP, E])
            m23 = sb("m23", [P, BPP, E])
            ex3 = sb("ex3", [P, BPP])
            c3 = sb("c3", [P, BPP, E])

        small_in = sem("small_in")
        experts_in = sem("experts_in")
        x_in = [sem(f"x_in{c}") for c in range(4)]
        ident_zero = sem("ident_zero")
        consts_done = sem("consts_done")
        iota_done = sem("iota_done")
        dve = sem("dve")
        dve_count = [0]
        n0_ready = sem("n0_ready")
        n0_turned = sem("n0_turned")
        nT_ready = sem("nT_ready")
        self_done = sem("self_done")
        base_summed = sem("base_summed")
        base_biased = sem("base_biased")
        base_out = sem("base_out")
        smallH_done = sem("smallH_done")
        weightsH_done = sem("weightsH_done")
        weights_done = sem("weights_done")
        g0_done = sem("g0_done")
        acc_zero = sem("acc_zero")

        with nc.Block() as block:
            @block.sync
            def _(sp):
                for c in range(4):
                    sp.dma_start(accT[:, c * 4 * W:(c + 1) * 4 * W].rearrange("p (b d) -> p b d", d=P),
                                 x[c * 4 * W:(c + 1) * 4 * W, :].rearrange("(b p) d -> p b d", p=P)
                                 ).then_inc(x_in[c], 16)
                for p in range(PANELS):
                    sp.wait_ge(base_biased, p + 1)
                    sp.dma_start(rows(base_dram, p), accT[:, p * W:(p + 1) * W].rearrange("p (b d) -> p b d", d=P)
                                 ).then_inc(base_out, 16)
                sp.wait_ge(base_out, 16 * PANELS)

            @block.scalar
            def _(act):
                loads = [(w_self, w_gnn0[0:P, :]), (w_nbr, w_gnn0[P:2 * P, :]),
                         (w_last, w_gnn0[2 * P - 1, :].partition_broadcast(P)),
                         (w_edge, w_gnn0[2 * P, :].partition_broadcast(P)),
                         (bias0, bias_gnn0.partition_broadcast(P)), (bias1, bias_gnn1.partition_broadcast(P)),
                         (w_l1, w_gnn1), (router, router_t), (gate, gate_w),
                         (gate_row, gate_b.partition_broadcast(P)), (gate_row2, gate_bias.partition_broadcast(P)),
                         (b1s0, b1_0), (b2s0, b2_0), (b1s1, b1_1), (b2s1, b2_1)]
                for dst, src in loads:
                    act.dma_start(dst[:], src).then_inc(small_in, 16)
                for s, w in enumerate((w1_0, w2_0)):
                    act.dma_start(stage[:, s, :].rearrange("p (e n) -> p e n", e=E), w.rearrange("e k n -> k e n")
                                  ).then_inc(experts_in, 16)
                act.wait_ge(small_in, 16 * len(loads))
                nc.scalar.activation(routerH[:], router[:], ACT.Copy).then_inc(smallH_done, 1)
                nc.scalar.activation(gateH[:], gate[:], ACT.Copy).then_inc(smallH_done, 1)
                act.wait_ge(experts_in, 32)
                nc.scalar.activation(w1H0[:].rearrange("p e n -> p (e n)"), stage[:, 0, :], ACT.Copy
                                     ).then_inc(weightsH_done, 1)
                nc.scalar.activation(w2H0[:].rearrange("p e n -> p (e n)"), stage[:, 1, :], ACT.Copy
                                     ).then_inc(weightsH_done, 1)
                for p in range(PANELS):
                    act.wait_ge(n0_turned, p + 1)
                    if p >= 2:
                        act.wait_ge(self_done, p - 1)
                    nc.scalar.activation(nT[:, p % 2, :], bank[p % 2][:], ACT.Copy).then_inc(nT_ready, 1)

            @block.gpsimd
            def _(pool):
                nc.gpsimd.memset(ident[:], 0.0).then_inc(ident_zero, 1)
                nc.gpsimd.iota(iota_i[:], [[1, E]], base=0, channel_multiplier=0).then_inc(iota_done, 1)
                pool.wait_ge(ident_zero, 1)
                nc.gpsimd.affine_select(out=ident[:], in_=ident[:], compare_op=ALU.not_equal, fill=1.0, base=0,
                                        pattern=[[-1, P]], channel_multiplier=1).then_inc(consts_done, 1)
                nc.gpsimd.memset(ones[:], 1.0).then_inc(consts_done, 1)
                nc.gpsimd.memset(scrap_v[:], 0.0).then_inc(consts_done, 1)
                nc.gpsimd.memset(scrap_p[:], 0.0).then_inc(consts_done, 1)
                nc.gpsimd.memset(e_rows[:], 0.0).then_inc(consts_done, 1)
                pool.wait_ge(small_in, 16 * 15)
                for p in range(PANELS):
                    pool.wait_ge(base_summed, p + 1)
                    panel = accT[:, p * W:(p + 1) * W].rearrange("p (b d) -> p b d", d=P)
                    nc.gpsimd.tensor_tensor(panel, panel, bias0[:].unsqueeze(1).to_broadcast([P, BPP, P]), ALU.add
                                            ).then_inc(base_biased, 1)
                pool.wait_ge(base_out, 16 * PANELS)
                nc.gpsimd.memset(accT[:], 0.0).then_inc(acc_zero, 1)

            @block.vector
            def _(v):
                ch = Chain(v, dve)
                v.wait_ge(iota_done, 1)
                ch.mark(nc.vector.tensor_copy(iota_f[:], iota_i[:]))
                for b in range(BLOCKS):
                    if b % 16 == 0:
                        v.wait_ge(x_in[b // 16], 16)
                    ch.mark(nc.vector.bn_stats(stats[:, b, :], accT[:, b * P:(b + 1) * P]))
                ch.sync()
                for b in range(BLOCKS):
                    ch.mark(nc.vector.bn_aggr(mv[:, b, :], stats[:, b, :]))
                ch.sync()
                ch.mark(nc.vector.tensor_scalar(vpe[:], mv[:, :, 1], EPS, None, ALU.add))
                rsqrt_steps(nc, ch, vpe[:], rstd[:], tmp[:])
                ch.sync()
                for b in range(BLOCKS):
                    ins = nc.vector.tensor_scalar(g0[:, b, :], accT[:, b * P:(b + 1) * P], mv[:, b, 0:1],
                                                  rstd[:, b:b + 1], ALU.subtract, ALU.mult)
                    if b % BPP == BPP - 1:
                        ins.then_inc(n0_ready, 1)
                v.wait_ge(smallH_done, 2)
                ch.mark(nc.vector.tensor_tensor(routerL[:], router[:], routerH[:].bitcast(F32), ALU.subtract))
                ch.mark(nc.vector.tensor_tensor(gateL[:], gate[:], gateH[:].bitcast(F32), ALU.subtract))
                ch.mark(nc.vector.tensor_tensor(w_nbr[:], w_nbr[:], w_last[:], ALU.subtract))
                ch.mark(nc.vector.tensor_tensor(gate_row[:], gate_row[:], gate_row2[:], ALU.add))
                for s, (wh, wl) in enumerate(((w1H0, w1L0), (w2H0, w2L0))):
                    v.wait_ge(weightsH_done, s + 1)
                    nc.vector.tensor_tensor(wl[:].rearrange("p e n -> p (e n)"), stage[:, s, :],
                                            wh[:].rearrange("p e n -> p (e n)").bitcast(F32), ALU.subtract
                                            ).then_inc(weights_done, 1)
                for p in range(PANELS):
                    v.wait_ge(self_done, p + 1)
                    nc.vector.tensor_tensor(accT[:, p * W:(p + 1) * W], bank[2 + p % 2][:], accT[:, p * W:(p + 1) * W],
                                            ALU.add).then_inc(base_summed, 1)
                v.wait_ge(n0_turned, PANELS)
                nc.vector.memset(g0[:, :, P - 1:P], 1.0).then_inc(g0_done, 1)
                dve_count[0] = ch.value()

            @block.tensor
            def _(pe):
                pe.wait_ge(consts_done, 5)
                pe.wait_ge(small_in, 16 * 15)
                for p in range(PANELS + 1):
                    if p < PANELS:
                        pe.wait_ge(n0_ready, p + 1)
                        if p >= 2:
                            pe.wait_ge(nT_ready, p - 1)
                        for b in range(BPP):
                            last = nc.tensor.transpose(bank[p % 2][:, b * P:(b + 1) * P], g0[:, p * BPP + b, :], ident[:])
                        last.then_inc(n0_turned, 1)
                    if p >= 1:
                        q = p - 1
                        pe.wait_ge(nT_ready, q + 1)
                        if q >= 2:
                            pe.wait_ge(base_summed, q - 1)
                        for b in range(BPP):
                            last = nc.tensor.matmul(bank[2 + q % 2][:, b * P:(b + 1) * P],
                                                    nT[:, q % 2, b * P:(b + 1) * P], w_self[:], start=True, stop=True)
                        last.then_inc(self_done, 1)

        raw_in = [sem(f"raw_in{s}") for s in range(RING1)]
        hi_done = sem("hi_done")
        lo_done = sem("lo_done")
        split_used = sem("split_used")
        jwH_done = sem("jwH_done")
        jwL_done = sem("jwL_done")
        iwF_done = sem("iwF_done")
        iwH_done = sem("iwH_done")
        iwL_done = sem("iwL_done")
        turned = sem("turned")
        row_tile_done = sem("row_tile_done")
        product_done = sem("product_done")
        product_used = sem("product_used")
        outJ_added = sem("outJ_added")
        outI_added = sem("outI_added")
        rows_kept = sem("rows_kept")
        columns_summed = sem("columns_summed")
        columns_copied = sem("columns_copied")
        PT = bank[0:4]
        OI = bank[4]
        OJ = bank[5:7]
        ES = bank[7]
        MAIN_TILES = PANELS * (2 * PAIRS + 1)
        MAIN_PAIRS = PANELS * PAIRS
        MAIN_RANKS = PANELS * RANKS
        TILES_I = 2 * PAIRS + 1
        USES_I = TILES_I // RING1

        class Pair:

            def __init__(self, i, k):
                self.i, self.k = i, k
                if k <= PAIRS:
                    self.j = (i + k) % PANELS
                    self.q = i * PAIRS + (k - 1)
                    self.r = i * RANKS + (k - 1)
                    self.g = i
                    self.slotA, self.useA = (2 * k - 2) % RING1, i * USES_I + (2 * k - 2) // RING1
                    self.slotB, self.useB = (2 * k - 1) % RING1, i * USES_I + (2 * k - 1) // RING1
                else:
                    self.j = i + k
                    self.q = MAIN_PAIRS + i
                    self.r = MAIN_RANKS + i
                    self.g = PANELS + i
                    n = MAIN_TILES + 2 * i
                    self.slotA, self.useA = n % RING1, n // RING1
                    self.slotB, self.useB = (n + 1) % RING1, (n + 1) // RING1

            @property
            def par(self):
                return self.k % 2 if self.k <= PAIRS else self.i % 2

        FAR = [Pair(i, PAIRS + 1) for i in range(PANELS // 2)]

        def next_pair(a):
            if a.k < PAIRS:
                return Pair(a.i, a.k + 1)
            if a.k == PAIRS:
                return Pair(a.i + 1, 1)
            return FAR[a.i + 1]

        with nc.Block() as block:
            @block.sync
            def _(sp):
                def released(i, m):
                    if isinstance(i, int) and i == PANELS:
                        if m < RING1:
                            i, prev = PANELS - 1, m + TILES_I - RING1
                        else:
                            rank = MAIN_RANKS + (m - RING1) // 2
                            odd = (m - RING1) % 2
                            return rank, odd, not odd
                    elif m >= RING1:
                        prev = m - RING1
                    else:
                        prev = m + TILES_I - RING1
                        rank = i * RANKS + (prev // 2 - RANKS)
                        return (rank, True, True) if prev == TILES_I - 1 else (rank, prev % 2, not prev % 2)
                    rank = i * RANKS + prev // 2
                    return (rank, True, True) if prev == TILES_I - 1 else (rank, prev % 2, not prev % 2)

                def load(i, m, slot, col_panel, row_panel):
                    rank, by_pe, by_dve = released(i, m)
                    if by_pe:
                        sp.wait_ge(row_tile_done, rank + 1 + RANKS)
                    if by_dve:
                        sp.wait_ge(product_done, rank * 4 + 4 + 4 * RANKS)
                    sp.dma_start(raw[:, slot, :], adj_tile(col_panel, row_panel)).then_inc(raw_in[slot], 16)

                with sp.Fori(0, PANELS) as i:
                    for k in range(1, PAIRS + 1):
                        a = Pair(i, k)
                        load(i, 2 * k - 2, a.slotA, a.i, a.j)
                        load(i, 2 * k - 1, a.slotB, a.j, a.i)
                    load(i, TILES_I - 1, RING1 - 1, i, i)
                for a in FAR:
                    load(PANELS, 2 * a.i, a.slotA, a.i, a.j)
                    load(PANELS, 2 * a.i + 1, a.slotB, a.j, a.i)

            @block.scalar
            def _(act):
                act.sem_inc(columns_copied, 1)

                def weights_j(a):
                    act.wait_ge(split_used, a.q * 3 + (2 if a.k == 1 else -1))
                    nc.scalar.activation(jwH[:, a.par, :], g0_flat(a.j, 0, W), ACT.Copy).then_inc(jwH_done, 1)

                def weights_i(a):
                    act.wait_ge(row_tile_done, (a.r - 1) + 1 + RANKS)
                    nc.scalar.activation(iwF[:], g0_flat(a.i, 0, W), ACT.Copy).then_inc(iwF_done, 1)
                    nc.scalar.activation(iwH[:], g0_flat(a.i, 0, W // 2), ACT.Copy).then_inc(iwH_done, 1)

                def g0_flat(panel, start, n):
                    return g0[:].rearrange("p b d -> p (b d)")[:, bass.ds(panel * W + start, n)]

                def split(a):
                    for u, (slot, use, half) in enumerate(((a.slotA, a.useA, 0), (a.slotA, a.useA, 1),
                                                           (a.slotB, a.useB, 0))):
                        act.wait_ge(raw_in[slot], (use + 1) * 16)
                        act.wait_ge(split_used, a.q * 3 + (u + 1))
                        nc.scalar.activation(hi[:, u, :], raw[:, slot, half * HALF:(half + 1) * HALF], ACT.Copy
                                             ).then_inc(hi_done, 1)

                def column_sums(a, flush, dst):
                    act.wait_ge(columns_summed, flush + 1)
                    nc.scalar.activation(dst, ES[:, 0:BPP], ACT.Copy).then_inc(columns_copied, 1)

                act.wait_ge(g0_done, 1)
                split(Pair(0, 1))
                with act.Fori(0, PANELS) as i:
                    weights_j(Pair(i, 1))
                    weights_i(Pair(i, 1))
                    for k in range(1, PAIRS + 1):
                        a = Pair(i, k)
                        if k < PAIRS:
                            weights_j(next_pair(a))
                        split(next_pair(a))
                        if k == 1:
                            column_sums(a, i, e_cols[:, bass.ds(i * BPP, BPP)])
                column_sums(None, PANELS, e_cols[:, PANELS * BPP:(PANELS + 1) * BPP])
                for a in FAR:
                    weights_j(a)
                    weights_i(a)
                    if a.i + 1 < len(FAR):
                        split(next_pair(a))
                    column_sums(a, PANELS + 1 + a.i, e_cols8[:, a.i * BPP:(a.i + 1) * BPP])

            @block.gpsimd
            def _(pool):
                nc.gpsimd.memset(accP[:], 0.0).then_inc(product_used, 1)

                def weights_j(a):
                    pool.wait_ge(jwH_done, a.q + 1)
                    nc.gpsimd.tensor_tensor(jwL[:, a.par, :], g0[:].rearrange("p b d -> p (b d)")[:, bass.ds(a.j * W, W)],
                                            jwH[:, a.par, :].bitcast(F32), ALU.subtract).then_inc(jwL_done, 1)

                def weights_i(a):
                    pool.wait_ge(iwH_done, a.g + 1)
                    nc.gpsimd.tensor_tensor(iwL[:], g0[:].rearrange("p b d -> p (b d)")[:, bass.ds(a.i * W, W // 2)],
                                            iwH[:].bitcast(F32), ALU.subtract).then_inc(iwL_done, 1)

                with pool.Fori(0, PANELS) as i:
                    weights_j(Pair(i, 1))
                    weights_i(Pair(i, 1))
                    for k in range(1, PAIRS + 1):
                        a = Pair(i, k)
                        if k < PAIRS:
                            weights_j(next_pair(a))
                        pool.wait_ge(product_done, a.r * 4 + 4 + 4 * RANKS)
                        pool.wait_ge(product_used, a.q + 1)
                        if k == 1:
                            pool.wait_ge(columns_summed, i + 1)
                            hold(nc.gpsimd, scrap_p[:])
                            ins = nc.gpsimd.tensor_copy(accP[:], prod[:, a.par, :])
                        else:
                            ins = nc.gpsimd.tensor_tensor(accP[:], accP[:], prod[:, a.par, :], ALU.add)
                        ins.then_inc(product_used, 1)
                for a in FAR:
                    weights_j(a)
                    weights_i(a)

            @block.vector
            def _(v):
                v.sem_inc(product_done, 4 * RANKS)
                v.sem_inc(outJ_added, 1)
                v.sem_inc(outI_added, 1)

                def products(r, k, j, tile, par):
                    for m in range(BPP):
                        v.wait_ge(turned, r * 4 + m + 1)
                        nc.vector.tensor_tensor_reduce(
                            prod[:, par, m * W:(m + 1) * W], PT[m][:], tile[:, m * W:(m + 1) * W], 1.0, 0.0,
                            ALU.mult, ALU.add, row_sums[:, par, m:m + 1]).then_inc(product_done, 1)

                def keep_rows(r, k, j, par):
                    v.wait_ge(product_done, r * 4 + 4 + 4 * RANKS)
                    nc.vector.tensor_copy(e_rows[:, bass.ds(j * BPP + k * BLOCKS, BPP)], row_sums[:, par, :]
                                          ).then_inc(rows_kept, 1)

                def split(a):
                    for u, (slot, half) in enumerate(((a.slotA, 0), (a.slotA, 1), (a.slotB, 0))):
                        v.wait_ge(hi_done, a.q * 3 + (u + 1))
                        nc.vector.tensor_tensor(lo[:, u, :], raw[:, slot, half * HALF:(half + 1) * HALF],
                                                hi[:, u, :].bitcast(F32), ALU.subtract).then_inc(lo_done, 1)

                def add_j(a):
                    v.wait_ge(row_tile_done, a.r + 1 + RANKS)
                    v.wait_ge(outJ_added, a.q + 1)
                    v.wait_ge(outI_added, a.g + 1)
                    dst = accT[:, bass.ds(a.j * W, W)]
                    nc.vector.tensor_tensor(dst, OJ[a.par][:], dst, ALU.add).then_inc(outJ_added, 1)

                def add_i(i, g, q_end):
                    v.wait_ge(outJ_added, q_end + 1)
                    dst = accT[:, bass.ds(i * W, W)]
                    nc.vector.tensor_tensor(dst, OI[:], dst, ALU.add).then_inc(outI_added, 1)

                v.wait_ge(acc_zero, 1)
                v.wait_ge(consts_done, 5)
                split(Pair(0, 1))
                with v.Fori(0, PANELS) as i:
                    for k in range(1, PAIRS + 1):
                        a = Pair(i, k)
                        v.wait_ge(product_used, a.q + (1 if k == 1 else 0))
                        products(a.r, k, a.j, raw[:, a.slotA, :], a.par)
                        split(next_pair(a))
                        keep_rows(a.r, k, a.j, a.par)
                        add_j(a)
                    v.wait_ge(product_used, i * PAIRS + PAIRS)
                    products(i * RANKS + PAIRS, 0, i, raw[:, RING1 - 1, :], 0)
                    keep_rows(i * RANKS + PAIRS, 0, i, 0)
                    v.wait_ge(row_tile_done, i * RANKS + RANKS + RANKS)
                    add_i(i, i, i * PAIRS + PAIRS)
                for a in FAR:
                    if a.i < 2:
                        v.wait_ge(product_used, MAIN_PAIRS + 1)
                    else:
                        v.wait_ge(columns_summed, PANELS + 1 + (a.i - 2) + 1)
                    v.wait_ge(rows_kept, a.r)
                    products(a.r, a.k, a.j, raw[:, a.slotA, :], a.par)
                    if a.i + 1 < len(FAR):
                        split(next_pair(a))
                    keep_rows(a.r, a.k, a.j, a.par)
                    add_j(a)
                    add_i(a.i, a.g, a.q + 1)

            @block.tensor
            def _(pe):
                pe.sem_inc(split_used, 3)
                pe.sem_inc(row_tile_done, RANKS)

                def turn(r, slot, use):
                    pe.wait_ge(raw_in[slot], (use + 1) * 16)
                    for m in range(BPP):
                        pe.wait_ge(product_done, r * 4 + (4 * RANKS - 4 + m + 1))
                        for b in range(BPP):
                            last = nc.tensor.transpose(PT[m][:, b * P:(b + 1) * P],
                                                       raw[:, slot, b * W + m * P:b * W + (m + 1) * P], ident[:])
                        last.then_inc(turned, 1)

                def split_half(dst, wh, wl, first_block, unit, start, stop):
                    for b in range(2):
                        blk = slice((first_block + b) * P, (first_block + b + 1) * P)
                        cols = slice(b * W, (b + 1) * W)
                        nc.tensor.matmul(dst[:], wh[:, blk], hi[:, unit, cols], start=start and b == 0, stop=False)
                        nc.tensor.matmul(dst[:], wh[:, blk], lo[:, unit, cols], start=False, stop=False)
                        last = nc.tensor.matmul(dst[:], wl[:, blk], hi[:, unit, cols], start=False,
                                                stop=stop and b == 1)
                    last.then_inc(split_used, 1)

                def plain(dst, slot, blocks, start, stop):
                    for b in blocks:
                        last = nc.tensor.matmul(dst[:], iwF[:, b * P:(b + 1) * P], raw[:, slot, b * W:(b + 1) * W],
                                                start=start and b == blocks[0], stop=stop and b == blocks[-1])
                    last.then_inc(row_tile_done, 1)

                def pair(a, only):
                    turn(a.r, a.slotB, a.useB)
                    pe.wait_ge(jwL_done, a.q + 1)
                    if a.k == 1 or only:
                        pe.wait_ge(outI_added, a.g + 1)
                    for u in range(2):
                        pe.wait_ge(lo_done, a.q * 3 + (u + 1))
                        split_half(OI, jwH[:, a.par, :], jwL[:, a.par, :], 2 * u, u, (a.k == 1 or only) and u == 0,
                                   only and u == 1)
                    pe.wait_ge(iwL_done, a.g + 1)
                    pe.wait_ge(iwF_done, a.g + 1)
                    pe.wait_ge(outJ_added, a.q + (1 if a.k == 1 else 0))
                    pe.wait_ge(lo_done, a.q * 3 + 3)
                    split_half(OJ[a.par], iwH, iwL, 0, 2, True, False)
                    plain(OJ[a.par], a.slotB, [2, 3], False, True)

                def sum_columns(src, flush):
                    pe.wait_ge(columns_copied, flush + 1)
                    for c in range(BPP):
                        for m in range(BPP):
                            last = nc.tensor.matmul(ES[:, c:c + 1], src[:, m * W + c * P:m * W + (c + 1) * P],
                                                    ones[:, 0:1], start=(m == 0), stop=(m == BPP - 1))
                    last.then_inc(columns_summed, 1)

                pe.wait_ge(consts_done, 5)
                with pe.Fori(0, PANELS) as i:
                    for k in range(1, PAIRS + 1):
                        a = Pair(i, k)
                        pair(a, False)
                        if k == 1:
                            pe.wait_ge(product_used, i * PAIRS + 1)
                            sum_columns(accP, i)
                    turn(i * RANKS + PAIRS, RING1 - 1, i * USES_I + USES_I - 1)
                    plain(OI, RING1 - 1, [0, 1, 2, 3], False, True)
                pe.wait_ge(product_used, MAIN_PAIRS + 1)
                sum_columns(accP, PANELS)
                for a in FAR:
                    pair(a, True)
                    pe.wait_ge(product_done, a.r * 4 + 4 + 4 * RANKS)
                    sum_columns(prod[:, a.par, :], PANELS + 1 + a.i)

        e_folded = sem("e_folded")
        base_in = [sem(f"base_in{s}") for s in range(4)]
        nbr_done = sem("nbr_done")
        x1_summed = sem("x1_summed")
        n1_ready = sem("n1_ready")
        n1_turned = sem("n1_turned")
        n1H_done = sem("n1H_done")
        n1L_done = sem("n1L_done")
        xn_done = sem("xn_done")
        logits_done = sem("logits_done")
        shifted = sem("shifted")
        exp_done = sem("exp_done")
        root_in = sem("root_in")
        root_done = sem("root_done")
        c_ready = sem("c_ready")
        c_turned = sem("c_turned")
        ct_ready = sem("ct_ready")
        c_out = [sem(f"c_out{s}") for s in range(2)]
        stage_in = sem("stage_in")
        CHAIN1 = 0

        def bcast(col, n=BLOCKS, m=E):
            return col.to_broadcast([P, n, m])

        with nc.Block() as block:
            @block.sync
            def _(sp):
                sp.dma_start(stage[:].rearrange("p s n -> p (s n)").rearrange("p (e h) -> p e h", e=E),
                             w1_1.rearrange("e k h -> k e h")).then_inc(stage_in, 16)
                for p in range(PANELS):
                    if p >= 4:
                        sp.wait_ge(x1_summed, p - 3)
                    sp.dma_start(bt[:, p % 4, :].rearrange("p (b d) -> p b d", d=P), rows(base_dram, p)
                                 ).then_inc(base_in[p % 4], 16)
                for p in range(PANELS):
                    sp.wait_ge(ct_ready, p + 1)
                    sp.dma_start(c0_dram[:, p * W:(p + 1) * W], cts[:, p % 2, :]).then_inc(c_out[p % 2], 16)
                sp.wait_ge(c_out[0], 8 * PANELS)
                sp.wait_ge(c_out[1], 8 * PANELS)

            @block.scalar
            def _(act):
                act.wait_ge(root_in, 1)
                nc.scalar.activation(dinv[:], rowsum[:], ACT.Sqrt).then_inc(root_done, 1)
                for p in range(PANELS):
                    act.wait_ge(n1_turned, p + 1)
                    nc.scalar.activation(n1H[:, p * W:(p + 1) * W], bank[2 + p % 2][:], ACT.Copy).then_inc(n1H_done, 1)
                act.wait_ge(shifted, 1)
                nc.scalar.activation(pr[:], pr[:], ACT.Exp).then_inc(exp_done, 1)
                for p in range(PANELS):
                    act.wait_ge(c_turned, p + 1)
                    if p >= 2:
                        act.wait_ge(c_out[p % 2], 16 * (p // 2))
                    nc.scalar.activation(cts[:, p % 2, :], bank[4 + p % 2][0:E, :], ACT.Copy).then_inc(ct_ready, 1)

            @block.gpsimd
            def _(pool):
                for p in range(PANELS):
                    pool.wait_ge(n1_ready, p + 1)
                    panel = xn[:, p * BPP:(p + 1) * BPP, :].rearrange("p b d -> p (b d)")
                    nc.gpsimd.tensor_tensor(panel, panel, nb[:, p % 2, :], ALU.add).then_inc(xn_done, 1)

            @block.vector
            def _(v):
                ch = Chain(v, dve, dve_count[0])
                ch.mark(nc.vector.tensor_reduce(e_sum[:], e_rows[:].rearrange("p (k b) -> p b k", b=BLOCKS), AX_X, ALU.add))
                ch.sync()
                ch.mark(nc.vector.tensor_tensor(e_sum[:], e_sum[:], e_cols[:, BPP:], ALU.add))
                ch.sync()
                ch.mark(nc.vector.tensor_tensor(e_sum[:, 0:BLOCKS // 2], e_sum[:, 0:BLOCKS // 2], e_cols8[:], ALU.add))
                for p in range(PANELS):
                    v.wait_ge(base_in[p % 4], 16 * (p // 4 + 1))
                    v.wait_ge(nbr_done, p + 1)
                    panel = xn[:, p * BPP:(p + 1) * BPP, :].rearrange("p b d -> p (b d)")
                    ins = nc.vector.tensor_tensor(panel, bank[p % 2][:], bt[:, p % 4, :], ALU.add)
                    ins.then_inc(x1_summed, 1)
                    v.wait_ge(x1_summed, p + 1)
                    ch.sync()
                    for b in range(p * BPP, (p + 1) * BPP):
                        ch.mark(nc.vector.scalar_tensor_tensor(out=xn[:, b, :], in0=w_edge[:], scalar=e_sum[:, b:b + 1],
                                                               in1=xn[:, b, :], op0=ALU.mult, op1=ALU.add))
                    ch.sync()
                    for b in range(p * BPP, (p + 1) * BPP):
                        ch.mark(nc.vector.bn_stats(stats2[:, b, :], xn[:, b, :]))
                ch.sync()
                nc.vector.tensor_scalar(rowsum[:], bank[7][:, 0:BLOCKS], 1.0, None, ALU.add).then_inc(root_in, 1)
                for b in range(BLOCKS):
                    ch.mark(nc.vector.bn_aggr(mv[:, b, :], stats2[:, b, :]))
                ch.sync()
                ch.mark(nc.vector.tensor_scalar(vpe[:], mv[:, :, 1], EPS, None, ALU.add))
                rsqrt_steps(nc, ch, vpe[:], rstd[:], tmp[:])
                v.wait_ge(root_done, 1)
                ch.mark(nc.vector.reciprocal(dinv[:], dinv[:]))
                newton_step(nc, ch, rowsum[:], dinv[:], tmp[:])
                ch.sync()
                for p in range(PANELS + 1):
                    if p < PANELS:
                        if p >= 2:
                            v.wait_ge(n1_turned, p - 1)
                            v.wait_ge(xn_done, p - 1)
                        for b in range(BPP):
                            blk = p * BPP + b
                            ins = nc.vector.tensor_scalar(nb[:, p % 2, b * P:(b + 1) * P], xn[:, blk, :],
                                                          mv[:, blk, 0:1], rstd[:, blk:blk + 1],
                                                          ALU.subtract, ALU.mult)
                        ins.then_inc(n1_ready, 1)
                    if p >= 1:
                        q = p - 1
                        v.wait_ge(n1H_done, q + 1)
                        nc.vector.tensor_tensor(n1L[:, q * W:(q + 1) * W], bank[2 + q % 2][:],
                                                n1H[:, q * W:(q + 1) * W].bitcast(F32), ALU.subtract
                                                ).then_inc(n1L_done, 1)
                v.wait_ge(logits_done, PANELS)
                ch.mark(nc.vector.tensor_copy(lg[:].rearrange("p b e -> p (b e)"), bank[6][:]))
                ch.sync()
                for b in range(BLOCKS):
                    ch.mark(nc.vector.max(mx[:, b, :], lg[:, b, :]))
                ch.sync()
                for b in range(BLOCKS):
                    ch.mark(nc.vector.max_index(ix[:, b, :], mx[:, b, :], lg[:, b, :]))
                nc.vector.tensor_tensor(pr[:], lg[:], bcast(mx[:, :, 0:1]), ALU.subtract).then_inc(shifted, 1)
                ch.sync()
                v.wait_ge(shifted, 1)
                ch.mark(nc.vector.tensor_copy(mx[:, :, 0:2], ix[:, :, 0:2]))
                ch.sync()
                iota3 = iota_f[:].unsqueeze(1).to_broadcast([P, BLOCKS, E])
                ch.mark(nc.vector.tensor_tensor(lg[:], iota3, bcast(mx[:, :, 0:1]), ALU.is_equal))
                ch.mark(nc.vector.tensor_tensor(cw[:], iota3, bcast(mx[:, :, 1:2]), ALU.is_equal))
                ch.sync()
                ch.mark(nc.vector.tensor_tensor(cw[:], cw[:], lg[:], ALU.add))
                v.wait_ge(exp_done, 1)
                ch.mark(nc.vector.tensor_reduce(vpe[:], pr[:], AX_X, ALU.add))
                ch.sync()
                ch.mark(nc.vector.reciprocal(vpe[:], vpe[:]))
                ch.sync()
                ch.mark(nc.vector.tensor_tensor(pr[:], pr[:], bcast(vpe[:].unsqueeze(2)), ALU.mult))
                ch.sync()
                ch.mark(nc.vector.tensor_tensor(cw[:], cw[:], pr[:], ALU.mult))
                ch.sync()
                ch.mark(nc.vector.tensor_reduce(tmp[:], cw[:], AX_X, ALU.add))
                ch.sync()
                ch.mark(nc.vector.tensor_scalar(tmp[:], tmp[:], 1e-12, None, ALU.max))
                ch.sync()
                ch.mark(nc.vector.reciprocal(tmp[:], tmp[:]))
                ch.sync()
                nc.vector.tensor_tensor(cw[:], cw[:], bcast(tmp[:].unsqueeze(2)), ALU.mult).then_inc(c_ready, 1)
                dve_count[0] = ch.value()

            @block.tensor
            def _(pe):
                for p in range(PANELS):
                    if p >= 2:
                        pe.wait_ge(x1_summed, p - 1)
                    for b in range(BPP):
                        blk = p * BPP + b
                        nc.tensor.matmul(bank[7][:, blk:blk + 1], accT[:, blk * P:(blk + 1) * P], ident[:, P - 1:P],
                                         start=True, stop=True)
                        last = nc.tensor.matmul(bank[p % 2][:, b * P:(b + 1) * P], accT[:, blk * P:(blk + 1) * P],
                                                w_nbr[:], start=True, stop=True)
                    last.then_inc(nbr_done, 1)
                for p in range(PANELS + 1):
                    if p < PANELS:
                        pe.wait_ge(n1_ready, p + 1)
                        if p >= 2:
                            pe.wait_ge(n1L_done, p - 1)
                        for b in range(BPP):
                            last = nc.tensor.transpose(bank[2 + p % 2][:, b * P:(b + 1) * P],
                                                       nb[:, p % 2, b * P:(b + 1) * P], ident[:])
                        last.then_inc(n1_turned, 1)
                    if p >= 1:
                        q = p - 1
                        pe.wait_ge(n1L_done, q + 1)
                        for blk in range(q * BPP, (q + 1) * BPP):
                            cols = slice(blk * P, (blk + 1) * P)
                            dst = bank[6][:, blk * E:(blk + 1) * E]
                            nc.tensor.matmul(dst, n1H[:, cols], routerH[:], start=True, stop=False)
                            nc.tensor.matmul(dst, n1L[:, cols], routerH[:], start=False, stop=False)
                            last = nc.tensor.matmul(dst, n1H[:, cols], routerL[:], start=False, stop=True)
                        last.then_inc(logits_done, 1)
                pe.wait_ge(c_ready, 1)
                for p in range(PANELS):
                    if p >= 2:
                        pe.wait_ge(ct_ready, p - 1)
                    for b in range(BPP):
                        last = nc.tensor.transpose(bank[4 + p % 2][0:E, b * P:(b + 1) * P], cw[:, p * BPP + b, :],
                                                   ident[:])
                    last.then_inc(c_turned, 1)

        W1RAW = stage[:].rearrange("p s n -> p (s n)")
        stageH_done = sem("stageH_done")
        stageL_done = sem("stageL_done")
        cb_in = [sem(f"cb_in{s}") for s in range(4)]
        ct_in = sem("ct_in")
        z_done = sem("z_done")
        gelu_done = sem("gelu_done")
        scaled = sem("scaled")
        hH_done = sem("hH_done")
        hL_done = sem("hL_done")
        y_done = sem("y_done")
        y_copied = sem("y_copied")
        ZB = bank[0:4]
        YB = bank[4]

        with nc.Block() as block:
            @block.sync
            def _(sp):
                def panel(p):
                    sp.wait_ge(y_done, p * E + 1)
                    sp.dma_start(ct0[:], c0_dram[:, bass.ds(p * W, W)]).then_inc(ct_in, 16)
                    for e in range(E):
                        sp.wait_ge(scaled, p * E + (e + 1))
                        sp.dma_start(cb0[:, e % 4, :], c0_dram[e, bass.ds(p * W, W)].partition_broadcast(P)
                                     ).then_inc(cb_in[e % 4], 16)

                with sp.Fori(0, PANELS) as p:
                    panel(p)
                sp.wait_ge(stageL_done, 1)
                sp.dma_start(W1RAW.rearrange("p (e q d) -> p e q d", e=E, q=2),
                             w2_1.rearrange("e (q h) d -> h e q d", q=2)).then_inc(stage_in, 16)

            @block.scalar
            def _(act):
                act.wait_ge(stage_in, 16)
                nc.scalar.activation(w1H1[:], W1RAW, ACT.Copy).then_inc(stageH_done, 1)

                def gelu(p, e):
                    act.wait_ge(z_done, p * E + (e + 1))
                    act.wait_ge(hL_done, p * E + (e + 1))
                    nc.scalar.activation(h0[:, e % 4, :], ZB[e % 4][:], ACT.Gelu, bias=b1s0[:, e:e + 1]
                                         ).then_inc(gelu_done, 1)

                def round_h(p, e):
                    act.wait_ge(scaled, p * E + (e + 5))
                    act.wait_ge(y_done, p * E + (e + 7))
                    nc.scalar.activation(hH0[:, e % 2, :], h0[:, e % 4, :], ACT.Copy).then_inc(hH_done, 1)

                def y_out(p):
                    act.wait_ge(y_done, p * E + 16)
                    nc.scalar.activation(yT[:, bass.ds(p * W, W)], YB[:], ACT.Copy).then_inc(y_copied, 1)

                def panel(p, first=False, last=False):
                    for e in range(E):
                        if e < E - 1:
                            gelu(p, e + 1)
                        elif not last:
                            gelu(p + 1, 0)
                        if e == 1 and not first:
                            y_out(p - 1)
                        round_h(p, e)

                act.sem_inc(gelu_done, 4)
                act.sem_inc(y_copied, 1)
                gelu(0, 0)
                panel(0, first=True)
                with act.Fori(1, PANELS - 1) as p:
                    panel(p)
                panel(PANELS - 1, last=True)
                y_out(PANELS - 1)
                act.wait_ge(stage_in, 32)
                nc.scalar.activation(w2H1[:], W1RAW, ACT.Copy).then_inc(stageH_done, 1)

            @block.gpsimd
            def _(pool):
                pool.sem_inc(scaled, 4)
                with pool.Fori(0, PANELS) as p:
                    for e in range(E):
                        pool.wait_ge(gelu_done, p * E + (e + 5))
                        pool.wait_ge(cb_in[e % 4], (p * 2 + (e // 4 + 1)) * 16)
                        nc.gpsimd.tensor_tensor(h0[:, e % 4, :], h0[:, e % 4, :], cb0[:, e % 4, :], ALU.mult
                                                ).then_inc(scaled, 1)

            @block.vector
            def _(v):
                v.sem_inc(hL_done, 4)
                v.wait_ge(stageH_done, 1)
                nc.vector.tensor_tensor(w1L1[:], W1RAW, w1H1[:].bitcast(F32), ALU.subtract).then_inc(stageL_done, 1)
                with v.Fori(0, PANELS) as p:
                    for e in range(E):
                        v.wait_ge(hH_done, p * E + (e + 1))
                        nc.vector.tensor_tensor(hL0[:, e % 2, :], h0[:, e % 4, :], hH0[:, e % 2, :].bitcast(F32),
                                                ALU.subtract).then_inc(hL_done, 1)
                v.wait_ge(stageH_done, 2)
                nc.vector.tensor_tensor(w2L1[:], W1RAW, w2H1[:].bitcast(F32), ALU.subtract).then_inc(stageL_done, 1)

            @block.tensor
            def _(pe):
                pe.sem_inc(y_done, 8)

                def z(p, e):
                    pe.wait_ge(gelu_done, p * E + (e + 1))
                    cols = bass.ds(p * W, W)
                    nc.tensor.matmul(ZB[e % 4][:], w1H0[:, e, :], n1H[:, cols], start=True, stop=False)
                    nc.tensor.matmul(ZB[e % 4][:], w1H0[:, e, :], n1L[:, cols], start=False, stop=False)
                    nc.tensor.matmul(ZB[e % 4][:], w1L0[:, e, :], n1H[:, cols], start=False, stop=True
                                     ).then_inc(z_done, 1)

                def y(p, e):
                    if e == 0:
                        pe.wait_ge(ct_in, p * 16 + 16)
                        pe.wait_ge(y_copied, p + 1)
                        nc.tensor.matmul(YB[:], b2s0[:], ct0[:], start=True, stop=False)
                    pe.wait_ge(hL_done, p * E + (e + 5))
                    nc.tensor.matmul(YB[:], w2H0[:, e, :], hH0[:, e % 2, :], start=False, stop=False)
                    nc.tensor.matmul(YB[:], w2H0[:, e, :], hL0[:, e % 2, :], start=False, stop=False)
                    nc.tensor.matmul(YB[:], w2L0[:, e, :], hH0[:, e % 2, :], start=False, stop=(e == E - 1)
                                     ).then_inc(y_done, 1)

                def panel(p, last=False):
                    for e in range(E):
                        if e + 3 < E:
                            z(p, e + 3)
                        elif not last:
                            z(p + 1, e + 3 - E)
                        y(p, e)

                for e in range(3):
                    z(0, e)
                with pe.Fori(0, PANELS - 1) as p:
                    panel(p)
                panel(PANELS - 1, last=True)

        yt_turned = sem("yt_turned")
        x2_summed = sem("x2_summed")
        n2_ready = sem("n2_ready")
        xb_biased = sem("xb_biased")
        n2_turned = sem("n2_turned")
        n2T_ready = sem("n2T_ready")
        support_done = sem("support_done")
        g_scaled = sem("g_scaled")
        gH_done = sem("gH_done")
        gL_done = sem("gL_done")
        xb_done = sem("xb_done")
        xb_out = sem("xb_out")
        raw3_in = [sem(f"raw3_in{s}") for s in range(RING3)]

        with nc.Block() as block:
            @block.sync
            def _(sp):
                sp.wait_ge(stageL_done, 2)
                for t in range(RING3):
                    sp.dma_start(raw3[:, t, :], adj_tile(0, t)).then_inc(raw3_in[t], 16)
                for p in range(PANELS):
                    sp.wait_ge(xb_done, p + 1)
                    sp.dma_start(rows(xb_dram, p), xn[:, p * BPP:(p + 1) * BPP, :]).then_inc(xb_out, 16)
                sp.wait_ge(xb_out, 16 * PANELS)

            @block.scalar
            def _(act):
                for p in range(PANELS + 1):
                    if p < PANELS:
                        act.wait_ge(n2_turned, p + 1)
                        if p >= 2:
                            act.wait_ge(support_done, p - 1)
                        nc.scalar.activation(nT2[:, p % 2, :], bank[2 + p % 2][:], ACT.Copy).then_inc(n2T_ready, 1)
                    if p >= 1:
                        q = p - 1
                        act.wait_ge(g_scaled, q + 1)
                        nc.scalar.activation(gH[:, q * W:(q + 1) * W], gf[:, q % 2, :], ACT.Copy).then_inc(gH_done, 1)

            @block.gpsimd
            def _(pool):
                for p in range(PANELS):
                    pool.wait_ge(n2_ready, p + 1)
                    panel = xn[:, p * BPP:(p + 1) * BPP, :]
                    nc.gpsimd.tensor_tensor(panel, panel, bias1[:].unsqueeze(1).to_broadcast([P, BPP, P]), ALU.add
                                            ).then_inc(xb_biased, 1)

            @block.vector
            def _(v):
                ch = Chain(v, dve, dve_count[0])
                for p in range(PANELS):
                    v.wait_ge(yt_turned, p + 1)
                    panel = xn[:, p * BPP:(p + 1) * BPP, :].rearrange("p b d -> p (b d)")
                    nc.vector.tensor_tensor(panel, bank[p % 2][:], panel, ALU.add).then_inc(x2_summed, 1)
                    v.wait_ge(x2_summed, p + 1)
                    for b in range(p * BPP, (p + 1) * BPP):
                        ch.mark(nc.vector.bn_stats(stats3[:, b, :], xn[:, b, :]))
                ch.sync()
                for b in range(BLOCKS):
                    ch.mark(nc.vector.bn_aggr(mv[:, b, :], stats3[:, b, :]))
                ch.sync()
                ch.mark(nc.vector.tensor_scalar(vpe[:], mv[:, :, 1], EPS, None, ALU.add))
                rsqrt_steps(nc, ch, vpe[:], rstd[:], tmp[:])
                ch.sync()
                for p in range(PANELS + 1):
                    if p < PANELS:
                        if p >= 2:
                            v.wait_ge(n2_turned, p - 1)
                        for b in range(BPP):
                            blk = p * BPP + b
                            ins = nc.vector.tensor_scalar(nb2[:, p % 2, b * P:(b + 1) * P], xn[:, blk, :],
                                                          mv[:, blk, 0:1], rstd[:, blk:blk + 1],
                                                          ALU.subtract, ALU.mult)
                        ins.then_inc(n2_ready, 1)
                    if p >= 1:
                        q = p - 1
                        v.wait_ge(support_done, q + 1)
                        if q >= 2:
                            v.wait_ge(gH_done, q - 1)
                            v.wait_ge(xb_done, q - 1)
                        for b in range(BPP):
                            blk = q * BPP + b
                            ins = nc.vector.tensor_scalar(gf[:, q % 2, b * P:(b + 1) * P],
                                                          bank[4 + q % 2][:, b * P:(b + 1) * P],
                                                          dinv[:, blk:blk + 1], None, ALU.mult)
                        ins.then_inc(g_scaled, 1)
                        v.wait_ge(g_scaled, q + 1)
                        v.wait_ge(xb_biased, q + 1)
                        for b in range(BPP):
                            blk = q * BPP + b
                            ins = nc.vector.scalar_tensor_tensor(out=xn[:, blk, :], in0=gf[:, q % 2, b * P:(b + 1) * P],
                                                                 scalar=dinv[:, blk:blk + 1], in1=xn[:, blk, :],
                                                                 op0=ALU.mult, op1=ALU.add)
                        ins.then_inc(xb_done, 1)
                        v.wait_ge(gH_done, q + 1)
                        nc.vector.tensor_tensor(gL[:, q * W:(q + 1) * W], gf[:, q % 2, :],
                                                gH[:, q * W:(q + 1) * W].bitcast(F32), ALU.subtract
                                                ).then_inc(gL_done, 1)
                dve_count[0] = ch.value()

            @block.tensor
            def _(pe):
                for p in range(PANELS):
                    if p >= 2:
                        pe.wait_ge(x2_summed, p - 1)
                    for b in range(BPP):
                        blk = p * BPP + b
                        last = nc.tensor.transpose(bank[p % 2][:, b * P:(b + 1) * P], yT[:, blk * P:(blk + 1) * P],
                                                   ident[:])
                    last.then_inc(yt_turned, 1)
                for p in range(PANELS + 1):
                    if p < PANELS:
                        pe.wait_ge(n2_ready, p + 1)
                        if p >= 2:
                            pe.wait_ge(n2T_ready, p - 1)
                        for b in range(BPP):
                            last = nc.tensor.transpose(bank[2 + p % 2][:, b * P:(b + 1) * P],
                                                       nb2[:, p % 2, b * P:(b + 1) * P], ident[:])
                        last.then_inc(n2_turned, 1)
                    if p >= 1:
                        q = p - 1
                        pe.wait_ge(n2T_ready, q + 1)
                        if q >= 2:
                            pe.wait_ge(g_scaled, q - 1)
                        for b in range(BPP):
                            last = nc.tensor.matmul(bank[4 + q % 2][:, b * P:(b + 1) * P],
                                                    nT2[:, q % 2, b * P:(b + 1) * P], w_l1[:], start=True, stop=True)
                        last.then_inc(support_done, 1)

        hi3_done = sem("hi3_done")
        lo3_done = sem("lo3_done")
        split3_used = sem("split3_used")
        o_copied = sem("o_copied")
        o_turned = sem("o_turned")
        xb3_in = sem("xb3_in")
        x3_done = sem("x3_done")
        n3_ready = sem("n3_ready")
        n3_turned = sem("n3_turned")
        n3H_done = sem("n3H_done")
        n3L_done = sem("n3L_done")
        logits3_done = sem("logits3_done")
        shifted3 = sem("shifted3")
        exp3_done = sem("exp3_done")
        c3_ready = sem("c3_ready")
        c3_turned = sem("c3_turned")
        ct3_ready = sem("ct3_ready")
        c3_out = sem("c3_out")
        cb3_in = [sem(f"cb3_in{s}") for s in range(4)]
        z3_done = sem("z3_done")
        relu_done = sem("relu_done")
        scaled3 = sem("scaled3")
        hH3_done = sem("hH3_done")
        hL3_done = sem("hL3_done")
        y3_done = sem("y3_done")
        y3_copied = sem("y3_copied")
        y3_turned = sem("y3_turned")
        out_ready = sem("out_ready")
        out_stored = sem("out_stored")
        dve3 = sem("dve3")
        OG = bank[5]
        M1 = bank[6]
        M2 = bank[7]
        S = 2 * E
        FIRST_Z, FIRST_Y = 6, 7
        CHAIN3 = 37

        def schedule(t):
            return [2 * (t - FIRST_Y), 2 * (t - FIRST_Y) + 1] if FIRST_Y <= t < FIRST_Y + E else []

        def over_panels(eng, panel):
            panel(0, tiles=True, chain=False, ahead=True)
            with eng.Fori(1, PANELS - 1) as p:
                panel(p, tiles=True, chain=True, ahead=True)
            panel(PANELS - 1, tiles=True, chain=True, ahead=False)
            panel(PANELS, tiles=False, chain=True, ahead=False)

        with nc.Block() as block:
            @block.sync
            def _(sp):
                def load_c(c, e):
                    if e >= 4:
                        sp.wait_ge(scaled3, c * S + (2 * (e - 4) + 2 + 8))
                    else:
                        sp.wait_ge(scaled3, c * S + 8)
                    sp.dma_start(cb1[:, e % 4, :], c1_dram[e, bass.ds(c * W, W)].partition_broadcast(P)
                                 ).then_inc(cb3_in[e % 4], 16)

                def store(c):
                    sp.wait_ge(out_ready, c + 2)
                    sp.dma_start(rows(out, c), x3[:].rearrange("p (b d) -> p b d", d=P)).then_inc(out_stored, 16)

                def panel(p, tiles, chain, ahead):
                    for t in range(PANELS):
                        if tiles and not (isinstance(p, int) and p == 0 and t < RING3):
                            sp.wait_ge(lo3_done, p * (2 * PANELS) + (2 * t + 2))
                            sp.dma_start(raw3[:, t % RING3, :], adj_tile(p, t)).then_inc(raw3_in[t % RING3], 16)
                        if chain and t == 3 and not (isinstance(p, int) and p == 1):
                            store(p - 2)
                        if tiles and t == 6:
                            if not (isinstance(p, int) and p == 0):
                                sp.wait_ge(x3_done, p * 1)
                            sp.dma_start(xbt[:].rearrange("p (b d) -> p b d", d=P), rows(xb_dram, p)).then_inc(xb3_in, 16)
                        if chain and t == 9:
                            sp.wait_ge(ct3_ready, p * 1)
                            sp.dma_start(c1_dram[:, bass.ds((p - 1) * W, W)], ct1[0:E, :]).then_inc(c3_out, 16)
                            sp.wait_ge(c3_out, p * 16)
                            for e in range(4):
                                load_c(p - 1, e)
                        if chain and 11 <= t <= 14:
                            load_c(p - 1, t - 7)

                panel(0, tiles=True, chain=False, ahead=True)
                panel(1, tiles=True, chain=True, ahead=True)
                with sp.Fori(2, PANELS) as p:
                    panel(p, tiles=True, chain=True, ahead=True)
                panel(PANELS, tiles=False, chain=True, ahead=False)
                store(PANELS - 1)
                sp.wait_ge(out_stored, 16 + 16 * PANELS)

            @block.scalar
            def _(act):
                def split(p, t):
                    for h in range(2):
                        act.wait_ge(raw3_in[t % RING3], (p * 4 + (t // RING3 + 1)) * 16)
                        act.wait_ge(split3_used, p * 32 + (2 * t + h + 1))
                        nc.scalar.activation(hi3[:, (2 * t + h) % 4, :], raw3[:, t % RING3, h * HALF:(h + 1) * HALF],
                                             ACT.Copy).then_inc(hi3_done, 1)

                def relu(c, s):
                    act.wait_ge(z3_done, c * S + (s + 1))
                    act.wait_ge(hL3_done, c * S + (s + 1))
                    nc.scalar.activation(h1[:, s % 4, :], ZB[s % 4][:], ACT.Relu, bias=b1s1[:, s // 2, s % 2:s % 2 + 1]
                                         ).then_inc(relu_done, 1)

                def round_h(c, s):
                    act.wait_ge(scaled3, c * S + (s + 9))
                    act.wait_ge(y3_done, c * S + (s + 1))
                    nc.scalar.activation(hH1[:, s % 2, :], h1[:, s % 4, :], ACT.Copy).then_inc(hH3_done, 1)

                def panel(p, tiles, chain, ahead):
                    c = p - 1
                    for t in range(PANELS):
                        if chain and t == 0:
                            act.wait_ge(split3_used, p * 32 + 4)
                            act.wait_ge(y3_turned, c + 1)
                            nc.scalar.activation(oT[:], OG[:], ACT.Copy).then_inc(o_copied, 1)
                        if tiles and t < PANELS - 1:
                            split(p, t + 1)
                        if ahead and t == PANELS - 1:
                            split(p + 1, 0)
                        if not chain:
                            continue
                        if t == 2:
                            act.wait_ge(n3_turned, p * 1)
                            act.wait_ge(y3_done, c * S + 2)
                            nc.scalar.activation(n3H[:], M1[:], ACT.Copy).then_inc(n3H_done, 1)
                        if t == 3:
                            act.wait_ge(shifted3, p * 1)
                            nc.scalar.activation(ex3[:], ex3[:], ACT.Exp).then_inc(exp3_done, 1)
                        if t == 5:
                            act.wait_ge(c3_turned, p * 1)
                            nc.scalar.activation(ct1[0:E, :], M2[0:E, :], ACT.Copy).then_inc(ct3_ready, 1)
                        if t == FIRST_Z:
                            relu(c, 0)
                        for s in schedule(t):
                            if s + 1 < S:
                                relu(c, s + 1)
                            round_h(c, s)
                        if t == FIRST_Y + E - 1:
                            act.wait_ge(y3_done, c * S + (S + 2))
                            nc.scalar.activation(oT[:], YB[:], ACT.Copy).then_inc(y3_copied, 1)

                act.sem_inc(o_copied, 1)
                act.sem_inc(relu_done, 4)
                split(0, 0)
                over_panels(act, panel)

            @block.gpsimd
            def _(pool):
                def panel(c):
                    for s in range(S):
                        pool.wait_ge(relu_done, c * S + (s + 5))
                        pool.wait_ge(cb3_in[(s // 2) % 4], (c * 2 + (s // 8 + 1)) * 16)
                        nc.gpsimd.tensor_tensor(h1[:, s % 4, :], h1[:, s % 4, :], cb1[:, (s // 2) % 4, :], ALU.mult
                                                ).then_inc(scaled3, 1)

                pool.sem_inc(scaled3, 8)
                with pool.Fori(0, PANELS) as c:
                    panel(c)

            @block.vector
            def _(v):
                ch = Chain(v, dve3)

                def split(p, t):
                    for h in range(2):
                        v.wait_ge(hi3_done, p * 32 + (2 * t + h + 1))
                        slot = (2 * t + h) % 4
                        nc.vector.tensor_tensor(lo3[:, slot, :], raw3[:, t % RING3, h * HALF:(h + 1) * HALF],
                                                hi3[:, slot, :].bitcast(F32), ALU.subtract).then_inc(lo3_done, 1)

                def rest_h(c, s):
                    v.wait_ge(hH3_done, c * S + (s + 1))
                    nc.vector.tensor_tensor(hL1[:, s % 2, :], h1[:, s % 4, :], hH1[:, s % 2, :].bitcast(F32),
                                            ALU.subtract).then_inc(hL3_done, 1)

                def rows3(p, c):
                    v.wait_ge(o_turned, p * 1)
                    v.wait_ge(xb3_in, p * 16)
                    v.wait_ge(out_stored, p * 16)
                    for b in range(BPP):
                        blk = slice(b * P, (b + 1) * P)
                        ins = nc.vector.scalar_tensor_tensor(out=x3[:, blk], in0=M1[:, blk],
                                                             scalar=dinv[:, bass.ds(c * BPP + b, 1)],
                                                             in1=xbt[:, blk], op0=ALU.mult, op1=ALU.add)
                    ins.then_inc(x3_done, 1)
                    v.wait_ge(x3_done, p * 1)
                    for b in range(BPP):
                        ch.mark(nc.vector.bn_stats(st3[:, b, :], x3[:, b * P:(b + 1) * P]))
                    ch.sync()
                    hold(nc.vector, scrap_v[:])
                    for b in range(BPP):
                        ch.mark(nc.vector.bn_aggr(mv3[:, b, :], st3[:, b, :]))
                    ch.sync()
                    ch.mark(nc.vector.tensor_scalar(v3[:], mv3[:, :, 1], EPS, None, ALU.add))
                    rsqrt_steps(nc, ch, v3[:], r3[:], t3[:])
                    ch.sync()
                    v.wait_ge(y3_done, c * S + 2)
                    for b in range(BPP):
                        blk = slice(b * P, (b + 1) * P)
                        ins = nc.vector.tensor_scalar(nb3[:, blk], x3[:, blk], mv3[:, b, 0:1], r3[:, b:b + 1],
                                                      ALU.subtract, ALU.mult)
                    ins.then_inc(n3_ready, 1)

                def gates(p):
                    v.wait_ge(logits3_done, p * 1)
                    ch.mark(nc.vector.tensor_tensor(lg3[:], M2[:, 0:BPP * E].rearrange("p (b e) -> p b e", e=E),
                                                    gate_row[:].unsqueeze(1).to_broadcast([P, BPP, E]), ALU.add))
                    ch.sync()
                    hold(nc.vector, scrap_v[:])
                    for b in range(BPP):
                        ch.mark(nc.vector.max(mx3[:, b, :], lg3[:, b, :]))
                    ch.sync()
                    nc.vector.tensor_tensor(ex3[:], mx3[:, :, 1], mx3[:, :, 0], ALU.subtract).then_inc(shifted3, 1)
                    for b in range(BPP):
                        ins = nc.vector.max_index(ix3[:, b, :], mx3[:, b, :], lg3[:, b, :])
                    ch.mark(ins)

                def weights(p):
                    ch.sync()
                    ch.mark(nc.vector.tensor_copy(if3[:, :, 0:2], ix3[:, :, 0:2]))
                    v.wait_ge(exp3_done, p * 1)
                    ch.mark(nc.vector.tensor_scalar(t3[:], ex3[:], 1.0, None, ALU.add))
                    ch.sync()
                    ch.mark(nc.vector.reciprocal(t3[:], t3[:]))
                    ch.sync()
                    ch.mark(nc.vector.tensor_tensor(v3[:], t3[:], ex3[:], ALU.mult))
                    iota3 = iota_f[:].unsqueeze(1).to_broadcast([P, BPP, E])
                    ch.mark(nc.vector.tensor_tensor(m13[:], iota3, bcast(if3[:, :, 0:1], BPP), ALU.is_equal))
                    ch.mark(nc.vector.tensor_tensor(m23[:], iota3, bcast(if3[:, :, 1:2], BPP), ALU.is_equal))
                    ch.sync()
                    ch.mark(nc.vector.tensor_tensor(m13[:], m13[:], bcast(t3[:].unsqueeze(2), BPP), ALU.mult))
                    ch.mark(nc.vector.tensor_tensor(m23[:], m23[:], bcast(v3[:].unsqueeze(2), BPP), ALU.mult))
                    ch.sync()
                    nc.vector.tensor_tensor(c3[:], m13[:], m23[:], ALU.add).then_inc(c3_ready, 1)

                def panel(p, tiles, chain, ahead):
                    c = p - 1
                    if chain:
                        ch.rebase(c * CHAIN3)
                    for t in range(PANELS):
                        if tiles and t < PANELS - 1:
                            split(p, t + 1)
                        if ahead and t == PANELS - 1:
                            split(p + 1, 0)
                        if not chain:
                            continue
                        if t == 0:
                            rows3(p, c)
                        if t == 2:
                            v.wait_ge(n3H_done, p * 1)
                            nc.vector.tensor_tensor(n3L[:], M1[:], n3H[:].bitcast(F32), ALU.subtract).then_inc(n3L_done, 1)
                        if t == 3:
                            gates(p)
                        if t == 4:
                            weights(p)
                        for s in schedule(t):
                            rest_h(c, s)
                        if t == PANELS - 1:
                            v.wait_ge(y3_turned, p + 1)
                            nc.vector.tensor_tensor(x3[:], M1[:], x3[:], ALU.add).then_inc(out_ready, 1)
                    if chain:
                        assert ch.n == CHAIN3, ch.n

                v.sem_inc(lo3_done, 8)
                v.sem_inc(hL3_done, 4)
                v.sem_inc(out_ready, 1)
                v.sem_inc(out_stored, 16)
                v.wait_ge(gL_done, PANELS)
                split(0, 0)
                over_panels(v, panel)

            @block.tensor
            def _(pe):
                def gnn(p, t):
                    for h in range(2):
                        unit = (2 * t + h) % 4
                        pe.wait_ge(lo3_done, p * 32 + (2 * t + h + 9))
                        if t == 0 and h == 0:
                            pe.wait_ge(o_copied, p + 1)
                        for b in range(2):
                            blk = slice((t * BPP + 2 * h + b) * P, (t * BPP + 2 * h + b + 1) * P)
                            cols = slice(b * W, (b + 1) * W)
                            first = t == 0 and h == 0 and b == 0
                            end = t == PANELS - 1 and h == 1 and b == 1
                            nc.tensor.matmul(OG[:], gH[:, blk], hi3[:, unit, cols], start=first, stop=False)
                            nc.tensor.matmul(OG[:], gH[:, blk], lo3[:, unit, cols], start=False, stop=False)
                            last = nc.tensor.matmul(OG[:], gL[:, blk], hi3[:, unit, cols], start=False, stop=end)
                        last.then_inc(split3_used, 1)

                def z(c, s):
                    e, q = s // 2, s % 2
                    pe.wait_ge(relu_done, c * S + (s + 1))
                    blk = slice((e * 2 + q) * P, (e * 2 + q + 1) * P)
                    nc.tensor.matmul(ZB[s % 4][:], w1H1[:, blk], n3H[:], start=True, stop=False)
                    nc.tensor.matmul(ZB[s % 4][:], w1H1[:, blk], n3L[:], start=False, stop=False)
                    nc.tensor.matmul(ZB[s % 4][:], w1L1[:, blk], n3H[:], start=False, stop=True).then_inc(z3_done, 1)

                def y(c, s):
                    blk = slice(s * P, (s + 1) * P)
                    if s == 0:
                        pe.wait_ge(ct3_ready, c + 1)
                        nc.tensor.matmul(YB[:], b2s1[:], ct1[0:E, :], start=True, stop=False)
                    pe.wait_ge(hL3_done, c * S + (s + 5))
                    nc.tensor.matmul(YB[:], w2H1[:, blk], hH1[:, s % 2, :], start=False, stop=False)
                    nc.tensor.matmul(YB[:], w2H1[:, blk], hL1[:, s % 2, :], start=False, stop=False)
                    nc.tensor.matmul(YB[:], w2L1[:, blk], hH1[:, s % 2, :], start=False, stop=(s == S - 1)
                                     ).then_inc(y3_done, 1)

                def turn(src, dst=M1):
                    for b in range(BPP):
                        last = nc.tensor.transpose(dst[:, b * P:(b + 1) * P], src[:, b * P:(b + 1) * P], ident[:])
                    return last

                def panel(p, tiles, chain, ahead):
                    c = p - 1
                    for t in range(PANELS):
                        if tiles:
                            gnn(p, t)
                        if not chain:
                            continue
                        if t == 0:
                            pe.wait_ge(o_copied, p + 1)
                            pe.wait_ge(out_ready, p * 1)
                            turn(oT).then_inc(o_turned, 1)
                        if t == 2:
                            pe.wait_ge(n3_ready, p * 1)
                            turn(nb3).then_inc(n3_turned, 1)
                        if t == 3:
                            pe.wait_ge(n3L_done, p * 1)
                            for b in range(BPP):
                                blk = slice(b * P, (b + 1) * P)
                                dst = M2[:, b * E:(b + 1) * E]
                                nc.tensor.matmul(dst, n3H[:, blk], gateH[:], start=True, stop=False)
                                nc.tensor.matmul(dst, n3L[:, blk], gateH[:], start=False, stop=False)
                                last = nc.tensor.matmul(dst, n3H[:, blk], gateL[:], start=False, stop=True)
                            last.then_inc(logits3_done, 1)
                        if t == 5:
                            pe.wait_ge(c3_ready, p * 1)
                            for b in range(BPP):
                                last = nc.tensor.transpose(M2[0:E, b * P:(b + 1) * P], c3[:, b, :], ident[:])
                            last.then_inc(c3_turned, 1)
                        if t == FIRST_Z:
                            for s in range(3):
                                z(c, s)
                        for s in schedule(t):
                            if s + 3 < S:
                                z(c, s + 3)
                            y(c, s)
                        if t == PANELS - 1:
                            pe.wait_ge(y3_copied, p * 1)
                            turn(oT).then_inc(y3_turned, 1)

                pe.sem_inc(split3_used, 4)
                pe.sem_inc(y3_done, 2)
                pe.sem_inc(y3_turned, 1)
                over_panels(pe, panel)


_OUT = (N, P)


def kernel(**inputs):
    import numpy as _np
    import concourse.bacc as _bacc
    from concourse import mybir as _mybir
    from concourse.bass_utils import run_bass_kernel_spmd as _run

    a = {k: _np.asarray(v) for k, v in inputs.items()}
    tiles = a["adj"].reshape(PANELS, W, PANELS, BPP, P).transpose(0, 2, 4, 3, 1)
    laid = [
        ("x", a["x"]), ("adj_tiles", tiles), ("w_gnn0", a["L0_gnn_weight"]), ("bias_gnn0", a["L0_gnn_bias"]),
        ("router_t", a["L0_ffn_router_w"].T), ("w1_0", a["L0_ffn_w1"]), ("b1_0", a["L0_ffn_b1"].T),
        ("w2_0", a["L0_ffn_w2"]), ("b2_0", a["L0_ffn_b2"]), ("w_gnn1", a["L1_gnn_weight"]),
        ("bias_gnn1", a["L1_gnn_bias"]), ("gate_w", a["L1_ffn_Wg"]), ("gate_b", a["L1_ffn_bg"]),
        ("gate_bias", a["L1_ffn_bias"]), ("w1_1", a["L1_ffn_W1"]),
        ("b1_1", a["L1_ffn_b1"].reshape(E, 2, P).transpose(2, 0, 1)), ("w2_1", a["L1_ffn_W2"]),
        ("b2_1", a["L1_ffn_b2"]),
    ]
    nc = _bacc.Bacc("TRN2", target_bir_lowering=False, num_devices=1)
    arrays, args = {}, []
    for name, v in laid:
        v = _np.ascontiguousarray(v)
        if name == "adj_tiles":
            v = v.reshape(PANELS * PANELS * P, TILE)
        arrays[name] = v
        args.append(nc.dram_tensor(name, v.shape, _mybir.dt.from_np(v.dtype), kind="ExternalInput").ap())
    args.append(nc.dram_tensor("out", _OUT, F32, kind="ExternalOutput").ap())
    program(nc, *args)
    r = _run(nc, [arrays], core_ids=[0])
    return r.results[0]["out"]
```

```python
from contextlib import ExitStack

import concourse.bass as bass
from concourse import mybir

F32 = mybir.dt.float32
F32R = mybir.dt.float32r
I32 = mybir.dt.int32
U32 = mybir.dt.uint32
ACT = mybir.ActivationFunctionType
ALU = mybir.AluOpType
AX_X = mybir.AxisListType.X

P = 128
N = 8192
W = 512
PANELS = N // W
BLOCKS = N // P
BPP = W // P
TILE = BPP * W
HALF = TILE // 2
E = 8
EPS = 1e-5

RING1 = 5
RING3 = 4
PAIRS = PANELS // 2 - 1
RANKS = PAIRS + 1


class Chain:

    def __init__(self, eng, sem, start=0):
        self.eng, self.sem, self.base, self.n = eng, sem, start, 0

    def mark(self, ins):
        ins.then_inc(self.sem, 1)
        self.n += 1

    def value(self):
        return self.base + self.n

    def sync(self):
        self.eng.wait_ge(self.sem, self.base + self.n)

    def rebase(self, base):
        self.base, self.n = base, 0


def hold(engine, scrap):
    engine.tensor_tensor(scrap, scrap, scrap, ALU.mult)


def rsqrt_start(nc, ch, v, r, t):
    ch.sync()
    ch.mark(nc.vector.tensor_scalar(t.bitcast(I32), v.bitcast(I32), 1, None, ALU.arith_shift_right))
    ch.sync()
    ch.mark(nc.vector.tensor_scalar(r.bitcast(I32), t.bitcast(I32), -1.0, float(0x5F3759DF), ALU.mult, ALU.add))


def rsqrt_steps(nc, ch, v, r, t):
    rsqrt_start(nc, ch, v, r, t)
    for _ in range(3):
        newton_step(nc, ch, v, r, t)


def newton_step(nc, ch, v, r, t):
    ch.sync()
    ch.mark(nc.vector.tensor_tensor(t, v, r, ALU.mult))
    ch.sync()
    ch.mark(nc.vector.tensor_tensor(t, t, r, ALU.mult))
    ch.sync()
    ch.mark(nc.vector.tensor_scalar(t, t, -0.5, 1.5, ALU.mult, ALU.add))
    ch.sync()
    ch.mark(nc.vector.tensor_tensor(r, r, t, ALU.mult))


def program(nc, x, adj_tiles, w_gnn0, bias_gnn0, router_t, w1_0, b1_0, w2_0, b2_0,
            w_gnn1, bias_gnn1, gate_w, gate_b, gate_bias, w1_1, b1_1, w2_1, b2_1, out):
    xb_dram = nc.dram_tensor("xb_dram", [N, P], F32, kind="Internal").ap()
    c0_dram = nc.dram_tensor("c0_dram", [E, N], F32, kind="Internal").ap()
    c1_dram = nc.dram_tensor("c1_dram", [PANELS * E, W], F32, kind="Internal").ap()

    def rows(t, p):
        return t[bass.ds(p * W, W), :].rearrange("(b p) d -> p b d", p=P)

    def adj_tile(col_panel, row_panel):
        return adj_tiles[bass.ds((col_panel * PANELS + row_panel) * P, P), :]

    with ExitStack() as keep:
        def maker(stack):
            def sb(name, shape, dt=F32):
                return stack.enter_context(nc.sbuf_tensor(name, shape, dt))
            return sb

        def sem(name):
            return keep.enter_context(nc.semaphore(name))

        bank = [keep.enter_context(nc.psum_tensor(f"bank{b}", [P, W], F32)) for b in range(8)]

        sb = maker(keep)
        ident = sb("ident", [P, P])
        ones = sb("ones", [P, 2])
        iota_i = sb("iota_i", [P, E], I32)
        iota_f = sb("iota_f", [P, E])
        router = sb("router", [P, E])
        routerH = sb("routerH", [P, E], F32R)
        routerL = sb("routerL", [P, E], F32R)
        gate = sb("gate", [P, E])
        gateH = sb("gateH", [P, E], F32R)
        gateL = sb("gateL", [P, E], F32R)
        gate_row = sb("gate_row", [P, E])
        gate_row2 = sb("gate_row2", [P, E])
        b1s0 = sb("b1s0", [P, E])
        b2s0 = sb("b2s0", [E, P])
        b1s1 = sb("b1s1", [P, E, 2])
        b2s1 = sb("b2s1", [E, P])
        scrap_v = sb("scrap_v", [P, 1])
        scrap_p = sb("scrap_p", [P, 1])
        dinv = sb("dinv", [P, BLOCKS])
        mark_u = ExitStack()
        sbu = maker(mark_u)
        w1H0 = sbu("w1H0", [P, E, P], F32R)
        w1L0 = sbu("w1L0", [P, E, P], F32R)
        w2H0 = sbu("w2H0", [P, E, P], F32R)
        w2L0 = sbu("w2L0", [P, E, P], F32R)
        stage = sbu("stage", [P, 2, E * P])
        w_self = sbu("w_self", [P, P])
        w_nbr = sbu("w_nbr", [P, P])
        w_last = sbu("w_last", [P, P])
        w_edge = sbu("w_edge", [P, P])
        bias0 = sbu("bias0", [P, P])
        bias1 = sbu("bias1", [P, P])
        w_l1 = sbu("w_l1", [P, P])
        e_rows = sbu("e_rows", [P, 9 * BLOCKS])
        e_cols = sbu("e_cols", [P, BLOCKS + BPP])
        e_cols8 = sbu("e_cols8", [P, BLOCKS // 2])
        row_sums = sbu("row_sums", [P, 2, BPP])
        e_sum = sbu("e_sum", [P, BLOCKS])
        rowsum = sbu("rowsum", [P, BLOCKS])
        mv = sbu("mv", [P, BLOCKS, 2])
        rstd = sbu("rstd", [P, BLOCKS])
        vpe = sbu("vpe", [P, BLOCKS])
        tmp = sbu("tmp", [P, BLOCKS])
        mark_u.close()
        raw3 = sb("raw3", [P, RING3, TILE])

        with ExitStack() as st:
            sb = maker(st)
            raw = sb("raw", [P, RING1, TILE])
            hi = sb("hi", [P, 3, HALF], F32R)
            lo = sb("lo", [P, 3, HALF], F32R)
            g0 = sb("g0", [P, BLOCKS, P])
            accT = sb("accT", [P, N])
            with ExitStack() as st0:
                sb0 = maker(st0)
                stats = sb0("stats", [P, BLOCKS, 6])
                w_last_self = sb0("w_last_self", [P, P])
            iwF = sb("iwF", [P, W])
            iwH = sb("iwH", [P, W // 2], F32R)
            iwL = sb("iwL", [P, W // 2], F32R)
            jwH = sb("jwH", [P, 2, W], F32R)
            jwL = sb("jwL", [P, 2, W], F32R)
            prod = sb("prod", [P, 2, TILE])
            accP = sb("accP", [P, TILE])
        with ExitStack() as st:
            sb = maker(st)
            n1H = sb("n1H", [P, N], F32R)
            with ExitStack() as stl:
                n1L = maker(stl)("n1L", [P, N], F32R)
            yT = sb("yT", [P, N])
            xn = sb("xn", [P, BLOCKS, P])
            with ExitStack() as stz:
                sbz = maker(stz)
                accT_place = sbz("accT_place", [P, N])
                sbv = sbz
                stats2 = sbv("stats2", [P, BLOCKS, 6])
                bt = sbv("bt", [P, 4, W])
                nb = sbv("nb", [P, 2, W])
                lg = sbv("lg", [P, BLOCKS, E])
                mx = sbv("mx", [P, BLOCKS, E])
                ix = sbv("ix", [P, BLOCKS, E], U32)
                pr = sbv("pr", [P, BLOCKS, E])
                cw = sbv("cw", [P, BLOCKS, E])
                cts = sbv("cts", [E, 2, W])
                nTa = sbv("nTa", [P, 2, W])
            w1H1 = sb("w1H1", [P, E * 2 * P], F32R)
            w1L1 = sb("w1L1", [P, E * 2 * P], F32R)
            w2H1 = sb("w2H1", [P, E * 2 * P], F32R)
            w2L1 = sb("w2L1", [P, E * 2 * P], F32R)
            with ExitStack() as stv:
                sbv = maker(stv)
                h0 = sbv("h0", [P, 4, W])
                hH0 = sbv("hH0", [P, 2, W], F32R)
                hL0 = sbv("hL0", [P, 2, W], F32R)
                cb0 = sbv("cb0", [P, 4, W])
                ct0 = sbv("ct0", [E, W])
            with ExitStack() as stv:
                sbv = maker(stv)
                stats3 = sbv("stats3", [P, BLOCKS, 6])
                nb2 = sbv("nb2", [P, 2, W])
                nT2 = sbv("nT2", [P, 2, W])
                gf = sbv("gf", [P, 2, W])
        with ExitStack() as st:
            sb = maker(st)
            gH = sb("gH", [P, N], F32R)
            gL = sb("gL", [P, N], F32R)
            hi3 = sb("hi3", [P, 4, HALF], F32R)
            lo3 = sb("lo3", [P, 4, HALF], F32R)
            w_place = sb("w_place", [P, 4 * E * 2 * P])
            h1 = sb("h1", [P, 4, W])
            hH1 = sb("hH1", [P, 2, W], F32R)
            hL1 = sb("hL1", [P, 2, W], F32R)
            cb1 = sb("cb1", [P, 4, W])
            n3H = sb("n3H", [P, 2, W], F32R)
            n3L = sb("n3L", [P, 2, W], F32R)
            oT = sb("oT", [P, W])
            outb = oT
            yTb = sb("yTb", [P, W])
            x3 = sb("x3", [P, 2, W])
            nb3 = sb("nb3", [P, W])
            xbt = nb3
            ct1 = sb("ct1", [E, W])
            st3 = sb("st3", [P, BPP, 6])
            mv3 = sb("mv3", [P, BPP, 2])
            v3 = sb("v3", [P, BPP])
            r3 = sb("r3", [P, BPP])
            t3 = sb("t3", [P, BPP])
            lg3 = sb("lg3", [P, BPP, E])
            mx3 = sb("mx3", [P, BPP, E])
            ix3 = sb("ix3", [P, BPP, E], U32)
            if3 = sb("if3", [P, BPP, E])
            m13 = sb("m13", [P, BPP, E])
            m23 = sb("m23", [P, BPP, E])
            ex3 = sb("ex3", [P, BPP])
            c3 = sb("c3", [P, BPP, E])

        small_in = sem("small_in")
        experts_in = sem("experts_in")
        x_in = [sem(f"x_in{c}") for c in range(4)]
        ident_zero = sem("ident_zero")
        consts_done = sem("consts_done")
        iota_done = sem("iota_done")
        dve = sem("dve")
        dve_count = [0]
        n0_ready = sem("n0_ready")
        smallH_done = sem("smallH_done")
        weightsH_done = sem("weightsH_done")
        weights_done = sem("weights_done")
        g0_done = sem("g0_done")
        acc_zero = sem("acc_zero")

        with nc.Block() as block:
            @block.sync
            def _(sp):
                for c in range(4):
                    sp.dma_start(accT[:, c * 4 * W:(c + 1) * 4 * W].rearrange("p (b d) -> p b d", d=P),
                                 x[c * 4 * W:(c + 1) * 4 * W, :].rearrange("(b p) d -> p b d", p=P)
                                 ).then_inc(x_in[c], 16)

            @block.scalar
            def _(act):
                loads = [(w_self, w_gnn0[0:P, :]), (w_last_self, w_gnn0[P - 1, :].partition_broadcast(P)), (w_nbr, w_gnn0[P:2 * P, :]),
                         (w_last, w_gnn0[2 * P - 1, :].partition_broadcast(P)),
                         (w_edge, w_gnn0[2 * P, :].partition_broadcast(P)),
                         (bias0, bias_gnn0.partition_broadcast(P)), (bias1, bias_gnn1.partition_broadcast(P)),
                         (w_l1, w_gnn1), (router, router_t), (gate, gate_w),
                         (gate_row, gate_b.partition_broadcast(P)), (gate_row2, gate_bias.partition_broadcast(P)),
                         (b1s0, b1_0), (b2s0, b2_0), (b1s1, b1_1), (b2s1, b2_1)]
                for dst, src in loads:
                    act.dma_start(dst[:], src).then_inc(small_in, 16)
                for s, w in enumerate((w1_0, w2_0)):
                    act.dma_start(stage[:, s, :].rearrange("p (e n) -> p e n", e=E), w.rearrange("e k n -> k e n")
                                  ).then_inc(experts_in, 16)
                act.wait_ge(small_in, 16 * len(loads))
                nc.scalar.activation(routerH[:], router[:], ACT.Copy).then_inc(smallH_done, 1)
                nc.scalar.activation(gateH[:], gate[:], ACT.Copy).then_inc(smallH_done, 1)
                act.wait_ge(experts_in, 32)
                nc.scalar.activation(w1H0[:].rearrange("p e n -> p (e n)"), stage[:, 0, :], ACT.Copy
                                     ).then_inc(weightsH_done, 1)
                nc.scalar.activation(w2H0[:].rearrange("p e n -> p (e n)"), stage[:, 1, :], ACT.Copy
                                     ).then_inc(weightsH_done, 1)

            @block.gpsimd
            def _(pool):
                nc.gpsimd.memset(ident[:], 0.0).then_inc(ident_zero, 1)
                nc.gpsimd.iota(iota_i[:], [[1, E]], base=0, channel_multiplier=0).then_inc(iota_done, 1)
                pool.wait_ge(ident_zero, 1)
                nc.gpsimd.affine_select(out=ident[:], in_=ident[:], compare_op=ALU.not_equal, fill=1.0, base=0,
                                        pattern=[[-1, P]], channel_multiplier=1).then_inc(consts_done, 1)
                nc.gpsimd.memset(ones[:], 1.0).then_inc(consts_done, 1)
                nc.gpsimd.memset(scrap_v[:], 0.0).then_inc(consts_done, 1)
                nc.gpsimd.memset(scrap_p[:], 0.0).then_inc(consts_done, 1)
                nc.gpsimd.memset(e_rows[:], 0.0).then_inc(consts_done, 1)
                for c in range(4):
                    pool.wait_ge(n0_ready, 4 * (c + 1))
                    nc.gpsimd.memset(accT[:, c * 4 * W:(c + 1) * 4 * W], 0.0).then_inc(acc_zero, 1)

            @block.vector
            def _(v):
                ch = Chain(v, dve)
                v.wait_ge(iota_done, 1)
                ch.mark(nc.vector.tensor_copy(iota_f[:], iota_i[:]))
                for b in range(BLOCKS):
                    if b % 16 == 0:
                        v.wait_ge(x_in[b // 16], 16)
                    ch.mark(nc.vector.bn_stats(stats[:, b, :], accT[:, b * P:(b + 1) * P]))
                ch.sync()
                for b in range(BLOCKS):
                    ch.mark(nc.vector.bn_aggr(mv[:, b, :], stats[:, b, :]))
                ch.sync()
                ch.mark(nc.vector.tensor_scalar(vpe[:], mv[:, :, 1], EPS, None, ALU.add))
                rsqrt_steps(nc, ch, vpe[:], rstd[:], tmp[:])
                ch.sync()
                for b in range(BLOCKS):
                    ins = nc.vector.tensor_scalar(g0[:, b, :], accT[:, b * P:(b + 1) * P], mv[:, b, 0:1],
                                                  rstd[:, b:b + 1], ALU.subtract, ALU.mult)
                    if b % BPP == BPP - 1:
                        ins.then_inc(n0_ready, 1)
                v.wait_ge(smallH_done, 2)
                ch.mark(nc.vector.tensor_tensor(routerL[:], router[:], routerH[:].bitcast(F32), ALU.subtract))
                ch.mark(nc.vector.tensor_tensor(gateL[:], gate[:], gateH[:].bitcast(F32), ALU.subtract))
                v.wait_ge(small_in, 16 * 16)
                ch.mark(nc.vector.tensor_tensor(w_self[:], w_self[:], w_last_self[:], ALU.subtract))
                ch.mark(nc.vector.tensor_tensor(w_nbr[:], w_nbr[:], w_last[:], ALU.subtract))
                ch.mark(nc.vector.tensor_tensor(gate_row[:], gate_row[:], gate_row2[:], ALU.add))
                for s, (wh, wl) in enumerate(((w1H0, w1L0), (w2H0, w2L0))):
                    v.wait_ge(weightsH_done, s + 1)
                    nc.vector.tensor_tensor(wl[:].rearrange("p e n -> p (e n)"), stage[:, s, :],
                                            wh[:].rearrange("p e n -> p (e n)").bitcast(F32), ALU.subtract
                                            ).then_inc(weights_done, 1)
                v.wait_ge(n0_ready, PANELS)
                nc.vector.memset(g0[:, :, P - 1:P], 1.0).then_inc(g0_done, 1)
                dve_count[0] = ch.value()

        raw_in = [sem(f"raw_in{s}") for s in range(RING1)]
        hi_done = sem("hi_done")
        lo_done = sem("lo_done")
        split_used = sem("split_used")
        jwH_done = sem("jwH_done")
        jwL_done = sem("jwL_done")
        iwF_done = sem("iwF_done")
        iwH_done = sem("iwH_done")
        iwL_done = sem("iwL_done")
        turned = sem("turned")
        row_tile_done = sem("row_tile_done")
        product_done = sem("product_done")
        product_used = sem("product_used")
        outJ_added = sem("outJ_added")
        outI_added = sem("outI_added")
        rows_kept = sem("rows_kept")
        columns_summed = sem("columns_summed")
        columns_copied = sem("columns_copied")
        PT = bank[0:4]
        OI = bank[4]
        OJ = bank[5:7]
        ES = bank[7]
        MAIN_TILES = PANELS * (2 * PAIRS + 1)
        MAIN_PAIRS = PANELS * PAIRS
        MAIN_RANKS = PANELS * RANKS
        TILES_I = 2 * PAIRS + 1
        USES_I = TILES_I // RING1

        class Pair:

            def __init__(self, i, k):
                self.i, self.k = i, k
                if k <= PAIRS:
                    self.j = (i + k) % PANELS
                    self.q = i * PAIRS + (k - 1)
                    self.r = i * RANKS + (k - 1)
                    self.g = i
                    self.slotA, self.useA = (2 * k - 2) % RING1, i * USES_I + (2 * k - 2) // RING1
                    self.slotB, self.useB = (2 * k - 1) % RING1, i * USES_I + (2 * k - 1) // RING1
                else:
                    self.j = i + k
                    self.q = MAIN_PAIRS + i
                    self.r = MAIN_RANKS + i
                    self.g = PANELS + i
                    n = MAIN_TILES + 2 * i
                    self.slotA, self.useA = n % RING1, n // RING1
                    self.slotB, self.useB = (n + 1) % RING1, (n + 1) // RING1

            @property
            def par(self):
                return self.k % 2 if self.k <= PAIRS else self.i % 2

        FAR = [Pair(i, PAIRS + 1) for i in range(PANELS // 2)]

        def next_pair(a):
            if a.k < PAIRS:
                return Pair(a.i, a.k + 1)
            if a.k == PAIRS:
                return Pair(a.i + 1, 1)
            return FAR[a.i + 1]

        with nc.Block() as block:
            @block.sync
            def _(sp):
                def released(i, m):
                    if isinstance(i, int) and i == PANELS:
                        if m < RING1:
                            i, prev = PANELS - 1, m + TILES_I - RING1
                        else:
                            rank = MAIN_RANKS + (m - RING1) // 2
                            odd = (m - RING1) % 2
                            return rank, odd, not odd
                    elif m >= RING1:
                        prev = m - RING1
                    else:
                        prev = m + TILES_I - RING1
                        rank = i * RANKS + (prev // 2 - RANKS)
                        return (rank, True, True) if prev == TILES_I - 1 else (rank, prev % 2, not prev % 2)
                    rank = i * RANKS + prev // 2
                    return (rank, True, True) if prev == TILES_I - 1 else (rank, prev % 2, not prev % 2)

                def load(i, m, slot, col_panel, row_panel):
                    rank, by_pe, by_dve = released(i, m)
                    if by_pe:
                        sp.wait_ge(row_tile_done, rank + 1 + RANKS)
                    if by_dve:
                        sp.wait_ge(product_done, rank * 4 + 4 + 4 * RANKS)
                    sp.dma_start(raw[:, slot, :], adj_tile(col_panel, row_panel)).then_inc(raw_in[slot], 16)

                with sp.Fori(0, PANELS) as i:
                    for k in range(1, PAIRS + 1):
                        a = Pair(i, k)
                        load(i, 2 * k - 2, a.slotA, a.i, a.j)
                        load(i, 2 * k - 1, a.slotB, a.j, a.i)
                    load(i, TILES_I - 1, RING1 - 1, i, i)
                for a in FAR:
                    load(PANELS, 2 * a.i, a.slotA, a.i, a.j)
                    load(PANELS, 2 * a.i + 1, a.slotB, a.j, a.i)

            @block.scalar
            def _(act):
                act.sem_inc(columns_copied, 1)

                def weights_j(a):
                    act.wait_ge(split_used, a.q * 3 + (2 if a.k == 1 else -1))
                    nc.scalar.activation(jwH[:, a.par, :], g0_flat(a.j, 0, W), ACT.Copy).then_inc(jwH_done, 1)

                def weights_i(a):
                    act.wait_ge(row_tile_done, (a.r - 1) + 1 + RANKS)
                    nc.scalar.activation(iwF[:], g0_flat(a.i, 0, W), ACT.Copy).then_inc(iwF_done, 1)
                    nc.scalar.activation(iwH[:], g0_flat(a.i, 0, W // 2), ACT.Copy).then_inc(iwH_done, 1)

                def g0_flat(panel, start, n):
                    return g0[:].rearrange("p b d -> p (b d)")[:, bass.ds(panel * W + start, n)]

                def split(a):
                    for u, (slot, use, half) in enumerate(((a.slotA, a.useA, 0), (a.slotA, a.useA, 1),
                                                           (a.slotB, a.useB, 0))):
                        act.wait_ge(raw_in[slot], (use + 1) * 16)
                        act.wait_ge(split_used, a.q * 3 + (u + 1))
                        nc.scalar.activation(hi[:, u, :], raw[:, slot, half * HALF:(half + 1) * HALF], ACT.Copy
                                             ).then_inc(hi_done, 1)

                def column_sums(a, flush, dst):
                    act.wait_ge(columns_summed, flush + 1)
                    nc.scalar.activation(dst, ES[:, 0:BPP], ACT.Copy).then_inc(columns_copied, 1)

                act.wait_ge(g0_done, 1)
                split(Pair(0, 1))
                with act.Fori(0, PANELS) as i:
                    weights_j(Pair(i, 1))
                    weights_i(Pair(i, 1))
                    for k in range(1, PAIRS + 1):
                        a = Pair(i, k)
                        if k < PAIRS:
                            weights_j(next_pair(a))
                        split(next_pair(a))
                        if k == 1:
                            column_sums(a, i, e_cols[:, bass.ds(i * BPP, BPP)])
                column_sums(None, PANELS, e_cols[:, PANELS * BPP:(PANELS + 1) * BPP])
                for a in FAR:
                    weights_j(a)
                    weights_i(a)
                    if a.i + 1 < len(FAR):
                        split(next_pair(a))
                    column_sums(a, PANELS + 1 + a.i, e_cols8[:, a.i * BPP:(a.i + 1) * BPP])

            @block.gpsimd
            def _(pool):
                nc.gpsimd.memset(accP[:], 0.0).then_inc(product_used, 1)

                def weights_j(a):
                    pool.wait_ge(jwH_done, a.q + 1)
                    nc.gpsimd.tensor_tensor(jwL[:, a.par, :], g0[:].rearrange("p b d -> p (b d)")[:, bass.ds(a.j * W, W)],
                                            jwH[:, a.par, :].bitcast(F32), ALU.subtract).then_inc(jwL_done, 1)

                def weights_i(a):
                    pool.wait_ge(iwH_done, a.g + 1)
                    nc.gpsimd.tensor_tensor(iwL[:], g0[:].rearrange("p b d -> p (b d)")[:, bass.ds(a.i * W, W // 2)],
                                            iwH[:].bitcast(F32), ALU.subtract).then_inc(iwL_done, 1)

                with pool.Fori(0, PANELS) as i:
                    weights_j(Pair(i, 1))
                    weights_i(Pair(i, 1))
                    for k in range(1, PAIRS + 1):
                        a = Pair(i, k)
                        if k < PAIRS:
                            weights_j(next_pair(a))
                        pool.wait_ge(product_done, a.r * 4 + 4 + 4 * RANKS)
                        pool.wait_ge(product_used, a.q + 1)
                        if k == 1:
                            pool.wait_ge(columns_summed, i + 1)
                            hold(nc.gpsimd, scrap_p[:])
                            ins = nc.gpsimd.tensor_copy(accP[:], prod[:, a.par, :])
                        else:
                            ins = nc.gpsimd.tensor_tensor(accP[:], accP[:], prod[:, a.par, :], ALU.add)
                        ins.then_inc(product_used, 1)
                for a in FAR:
                    weights_j(a)
                    weights_i(a)

            @block.vector
            def _(v):
                v.sem_inc(product_done, 4 * RANKS)
                v.sem_inc(outJ_added, 1)
                v.sem_inc(outI_added, 1)

                def products(r, k, j, tile, par):
                    for m in range(BPP):
                        v.wait_ge(turned, r * 4 + m + 1)
                        nc.vector.tensor_tensor_reduce(
                            prod[:, par, m * W:(m + 1) * W], PT[m][:], tile[:, m * W:(m + 1) * W], 1.0, 0.0,
                            ALU.mult, ALU.add, row_sums[:, par, m:m + 1]).then_inc(product_done, 1)

                def keep_rows(r, k, j, par):
                    v.wait_ge(product_done, r * 4 + 4 + 4 * RANKS)
                    nc.vector.tensor_copy(e_rows[:, bass.ds(j * BPP + k * BLOCKS, BPP)], row_sums[:, par, :]
                                          ).then_inc(rows_kept, 1)

                def split(a):
                    for u, (slot, half) in enumerate(((a.slotA, 0), (a.slotA, 1), (a.slotB, 0))):
                        v.wait_ge(hi_done, a.q * 3 + (u + 1))
                        nc.vector.tensor_tensor(lo[:, u, :], raw[:, slot, half * HALF:(half + 1) * HALF],
                                                hi[:, u, :].bitcast(F32), ALU.subtract).then_inc(lo_done, 1)

                def add_j(a):
                    v.wait_ge(row_tile_done, a.r + 1 + RANKS)
                    v.wait_ge(outJ_added, a.q + 1)
                    v.wait_ge(outI_added, a.g + 1)
                    dst = accT[:, bass.ds(a.j * W, W)]
                    nc.vector.tensor_tensor(dst, OJ[a.par][:], dst, ALU.add).then_inc(outJ_added, 1)

                def add_i(i, g, q_end):
                    v.wait_ge(outJ_added, q_end + 1)
                    dst = accT[:, bass.ds(i * W, W)]
                    nc.vector.tensor_tensor(dst, OI[:], dst, ALU.add).then_inc(outI_added, 1)

                v.wait_ge(acc_zero, 4)
                v.wait_ge(consts_done, 5)
                split(Pair(0, 1))
                with v.Fori(0, PANELS) as i:
                    for k in range(1, PAIRS + 1):
                        a = Pair(i, k)
                        v.wait_ge(product_used, a.q + (1 if k == 1 else 0))
                        products(a.r, k, a.j, raw[:, a.slotA, :], a.par)
                        split(next_pair(a))
                        keep_rows(a.r, k, a.j, a.par)
                        add_j(a)
                    v.wait_ge(product_used, i * PAIRS + PAIRS)
                    products(i * RANKS + PAIRS, 0, i, raw[:, RING1 - 1, :], 0)
                    keep_rows(i * RANKS + PAIRS, 0, i, 0)
                    v.wait_ge(row_tile_done, i * RANKS + RANKS + RANKS)
                    add_i(i, i, i * PAIRS + PAIRS)
                for a in FAR:
                    if a.i < 2:
                        v.wait_ge(product_used, MAIN_PAIRS + 1)
                    else:
                        v.wait_ge(columns_summed, PANELS + 1 + (a.i - 2) + 1)
                    v.wait_ge(rows_kept, a.r)
                    products(a.r, a.k, a.j, raw[:, a.slotA, :], a.par)
                    if a.i + 1 < len(FAR):
                        split(next_pair(a))
                    keep_rows(a.r, a.k, a.j, a.par)
                    add_j(a)
                    add_i(a.i, a.g, a.q + 1)

            @block.tensor
            def _(pe):
                pe.sem_inc(split_used, 3)
                pe.sem_inc(row_tile_done, RANKS)

                def turn(r, slot, use):
                    pe.wait_ge(raw_in[slot], (use + 1) * 16)
                    for m in range(BPP):
                        pe.wait_ge(product_done, r * 4 + (4 * RANKS - 4 + m + 1))
                        for b in range(BPP):
                            last = nc.tensor.transpose(PT[m][:, b * P:(b + 1) * P],
                                                       raw[:, slot, b * W + m * P:b * W + (m + 1) * P], ident[:])
                        last.then_inc(turned, 1)

                def split_half(dst, wh, wl, first_block, unit, start, stop):
                    for b in range(2):
                        blk = slice((first_block + b) * P, (first_block + b + 1) * P)
                        cols = slice(b * W, (b + 1) * W)
                        nc.tensor.matmul(dst[:], wh[:, blk], hi[:, unit, cols], start=start and b == 0, stop=False)
                        nc.tensor.matmul(dst[:], wh[:, blk], lo[:, unit, cols], start=False, stop=False)
                        last = nc.tensor.matmul(dst[:], wl[:, blk], hi[:, unit, cols], start=False,
                                                stop=stop and b == 1)
                    last.then_inc(split_used, 1)

                def plain(dst, slot, blocks, start, stop):
                    for b in blocks:
                        last = nc.tensor.matmul(dst[:], iwF[:, b * P:(b + 1) * P], raw[:, slot, b * W:(b + 1) * W],
                                                start=start and b == blocks[0], stop=stop and b == blocks[-1])
                    last.then_inc(row_tile_done, 1)

                def pair(a, only):
                    turn(a.r, a.slotB, a.useB)
                    pe.wait_ge(jwL_done, a.q + 1)
                    if a.k == 1 or only:
                        pe.wait_ge(outI_added, a.g + 1)
                    for u in range(2):
                        pe.wait_ge(lo_done, a.q * 3 + (u + 1))
                        split_half(OI, jwH[:, a.par, :], jwL[:, a.par, :], 2 * u, u, (a.k == 1 or only) and u == 0,
                                   only and u == 1)
                    pe.wait_ge(iwL_done, a.g + 1)
                    pe.wait_ge(iwF_done, a.g + 1)
                    pe.wait_ge(outJ_added, a.q + (1 if a.k == 1 else 0))
                    pe.wait_ge(lo_done, a.q * 3 + 3)
                    split_half(OJ[a.par], iwH, iwL, 0, 2, True, False)
                    plain(OJ[a.par], a.slotB, [2, 3], False, True)

                def sum_columns(src, flush):
                    pe.wait_ge(columns_copied, flush + 1)
                    for c in range(BPP):
                        for m in range(BPP):
                            last = nc.tensor.matmul(ES[:, c:c + 1], src[:, m * W + c * P:m * W + (c + 1) * P],
                                                    ones[:, 0:1], start=(m == 0), stop=(m == BPP - 1))
                    last.then_inc(columns_summed, 1)

                pe.wait_ge(consts_done, 5)
                with pe.Fori(0, PANELS) as i:
                    for k in range(1, PAIRS + 1):
                        a = Pair(i, k)
                        pair(a, False)
                        if k == 1:
                            pe.wait_ge(product_used, i * PAIRS + 1)
                            sum_columns(accP, i)
                    turn(i * RANKS + PAIRS, RING1 - 1, i * USES_I + USES_I - 1)
                    plain(OI, RING1 - 1, [0, 1, 2, 3], False, True)
                pe.wait_ge(product_used, MAIN_PAIRS + 1)
                sum_columns(accP, PANELS)
                for a in FAR:
                    pair(a, True)
                    pe.wait_ge(product_done, a.r * 4 + 4 + 4 * RANKS)
                    sum_columns(prod[:, a.par, :], PANELS + 1 + a.i)

        e_folded = sem("e_folded")
        x_again = [sem(f"x_again{s}") for s in range(4)]
        x_biased = sem("x_biased")
        g0_turned = sem("g0_turned")
        nTa_ready = sem("nTa_ready")
        nbr_done = sem("nbr_done")
        x1_summed = sem("x1_summed")
        n1_ready = sem("n1_ready")
        n1_turned = sem("n1_turned")
        n1H_done = sem("n1H_done")
        n1L_done = sem("n1L_done")
        xn_done = sem("xn_done")
        logits_done = sem("logits_done")
        shifted = sem("shifted")
        exp_done = sem("exp_done")
        root_in = sem("root_in")
        root_done = sem("root_done")
        c_ready = sem("c_ready")
        c_turned = sem("c_turned")
        ct_ready = sem("ct_ready")
        c_out = [sem(f"c_out{s}") for s in range(2)]
        stage_in = sem("stage_in")
        CHAIN1 = 0

        def bcast(col, n=BLOCKS, m=E):
            return col.to_broadcast([P, n, m])

        with nc.Block() as block:
            @block.sync
            def _(sp):
                sp.dma_start(stage[:].rearrange("p s n -> p (s n)").rearrange("p (e h) -> p e h", e=E),
                             w1_1.rearrange("e k h -> k e h")).then_inc(stage_in, 16)
                for p in range(PANELS):
                    if p >= 4:
                        sp.wait_ge(x1_summed, p - 3)
                    sp.dma_start(bt[:, p % 4, :].rearrange("p (b d) -> p b d", d=P), rows(x, p)
                                 ).then_inc(x_again[p % 4], 16)
                for p in range(PANELS):
                    sp.wait_ge(ct_ready, p + 1)
                    sp.dma_start(c0_dram[:, p * W:(p + 1) * W], cts[:, p % 2, :]).then_inc(c_out[p % 2], 16)
                sp.wait_ge(c_out[0], 8 * PANELS)
                sp.wait_ge(c_out[1], 8 * PANELS)

            @block.scalar
            def _(act):
                for p in range(PANELS):
                    act.wait_ge(g0_turned, p + 1)
                    if p >= 2:
                        act.wait_ge(nbr_done, p - 1)
                    nc.scalar.activation(nTa[:, p % 2, :], bank[4 + p % 2][:], ACT.Copy).then_inc(nTa_ready, 1)
                act.wait_ge(root_in, 1)
                nc.scalar.activation(dinv[:], rowsum[:], ACT.Sqrt).then_inc(root_done, 1)
                for p in range(PANELS):
                    act.wait_ge(n1_turned, p + 1)
                    nc.scalar.activation(n1H[:, p * W:(p + 1) * W], bank[2 + p % 2][:], ACT.Copy).then_inc(n1H_done, 1)
                act.wait_ge(shifted, 1)
                nc.scalar.activation(pr[:], pr[:], ACT.Exp).then_inc(exp_done, 1)
                for p in range(PANELS):
                    act.wait_ge(c_turned, p + 1)
                    if p >= 2:
                        act.wait_ge(c_out[p % 2], 16 * (p // 2))
                    nc.scalar.activation(cts[:, p % 2, :], bank[4 + p % 2][0:E, :], ACT.Copy).then_inc(ct_ready, 1)

            @block.gpsimd
            def _(pool):
                for p in range(PANELS):
                    pool.wait_ge(x_again[p % 4], 16 * (p // 4 + 1))
                    panel = bt[:, p % 4, :].rearrange("p (b d) -> p b d", d=P)
                    nc.gpsimd.tensor_tensor(panel, panel, bias0[:].unsqueeze(1).to_broadcast([P, BPP, P]), ALU.add
                                            ).then_inc(x_biased, 1)
                for p in range(PANELS):
                    pool.wait_ge(n1_ready, p + 1)
                    panel = xn[:, p * BPP:(p + 1) * BPP, :].rearrange("p b d -> p (b d)")
                    nc.gpsimd.tensor_tensor(panel, panel, nb[:, p % 2, :], ALU.add).then_inc(xn_done, 1)

            @block.vector
            def _(v):
                ch = Chain(v, dve, dve_count[0])
                ch.mark(nc.vector.tensor_reduce(e_sum[:], e_rows[:].rearrange("p (k b) -> p b k", b=BLOCKS), AX_X, ALU.add))
                ch.sync()
                ch.mark(nc.vector.tensor_tensor(e_sum[:], e_sum[:], e_cols[:, BPP:], ALU.add))
                ch.sync()
                ch.mark(nc.vector.tensor_tensor(e_sum[:, 0:BLOCKS // 2], e_sum[:, 0:BLOCKS // 2], e_cols8[:], ALU.add))
                for p in range(PANELS):
                    v.wait_ge(x_biased, p + 1)
                    v.wait_ge(nbr_done, p + 1)
                    panel = xn[:, p * BPP:(p + 1) * BPP, :].rearrange("p b d -> p (b d)")
                    ins = nc.vector.tensor_tensor(panel, bank[p % 2][:], bt[:, p % 4, :], ALU.add)
                    ins.then_inc(x1_summed, 1)
                    v.wait_ge(x1_summed, p + 1)
                    ch.sync()
                    for b in range(p * BPP, (p + 1) * BPP):
                        ch.mark(nc.vector.scalar_tensor_tensor(out=xn[:, b, :], in0=w_edge[:], scalar=e_sum[:, b:b + 1],
                                                               in1=xn[:, b, :], op0=ALU.mult, op1=ALU.add))
                    ch.sync()
                    for b in range(p * BPP, (p + 1) * BPP):
                        ch.mark(nc.vector.bn_stats(stats2[:, b, :], xn[:, b, :]))
                ch.sync()
                nc.vector.tensor_scalar(rowsum[:], bank[7][:, 0:BLOCKS], 1.0, None, ALU.add).then_inc(root_in, 1)
                for b in range(BLOCKS):
                    ch.mark(nc.vector.bn_aggr(mv[:, b, :], stats2[:, b, :]))
                ch.sync()
                ch.mark(nc.vector.tensor_scalar(vpe[:], mv[:, :, 1], EPS, None, ALU.add))
                rsqrt_steps(nc, ch, vpe[:], rstd[:], tmp[:])
                v.wait_ge(root_done, 1)
                ch.mark(nc.vector.reciprocal(dinv[:], dinv[:]))
                newton_step(nc, ch, rowsum[:], dinv[:], tmp[:])
                ch.sync()
                for p in range(PANELS + 1):
                    if p < PANELS:
                        if p >= 2:
                            v.wait_ge(n1_turned, p - 1)
                            v.wait_ge(xn_done, p - 1)
                        for b in range(BPP):
                            blk = p * BPP + b
                            ins = nc.vector.tensor_scalar(nb[:, p % 2, b * P:(b + 1) * P], xn[:, blk, :],
                                                          mv[:, blk, 0:1], rstd[:, blk:blk + 1],
                                                          ALU.subtract, ALU.mult)
                        ins.then_inc(n1_ready, 1)
                    if p >= 1:
                        q = p - 1
                        v.wait_ge(n1H_done, q + 1)
                        nc.vector.tensor_tensor(n1L[:, q * W:(q + 1) * W], bank[2 + q % 2][:],
                                                n1H[:, q * W:(q + 1) * W].bitcast(F32), ALU.subtract
                                                ).then_inc(n1L_done, 1)
                v.wait_ge(logits_done, PANELS)
                ch.mark(nc.vector.tensor_copy(lg[:].rearrange("p b e -> p (b e)"), bank[6][:]))
                ch.sync()
                for b in range(BLOCKS):
                    ch.mark(nc.vector.max(mx[:, b, :], lg[:, b, :]))
                ch.sync()
                for b in range(BLOCKS):
                    ch.mark(nc.vector.max_index(ix[:, b, :], mx[:, b, :], lg[:, b, :]))
                nc.vector.tensor_tensor(pr[:], lg[:], bcast(mx[:, :, 0:1]), ALU.subtract).then_inc(shifted, 1)
                ch.sync()
                v.wait_ge(shifted, 1)
                ch.mark(nc.vector.tensor_copy(mx[:, :, 0:2], ix[:, :, 0:2]))
                ch.sync()
                iota3 = iota_f[:].unsqueeze(1).to_broadcast([P, BLOCKS, E])
                ch.mark(nc.vector.tensor_tensor(lg[:], iota3, bcast(mx[:, :, 0:1]), ALU.is_equal))
                ch.mark(nc.vector.tensor_tensor(cw[:], iota3, bcast(mx[:, :, 1:2]), ALU.is_equal))
                ch.sync()
                ch.mark(nc.vector.tensor_tensor(cw[:], cw[:], lg[:], ALU.add))
                v.wait_ge(exp_done, 1)
                ch.mark(nc.vector.tensor_reduce(vpe[:], pr[:], AX_X, ALU.add))
                ch.sync()
                ch.mark(nc.vector.reciprocal(vpe[:], vpe[:]))
                ch.sync()
                ch.mark(nc.vector.tensor_tensor(pr[:], pr[:], bcast(vpe[:].unsqueeze(2)), ALU.mult))
                ch.sync()
                ch.mark(nc.vector.tensor_tensor(cw[:], cw[:], pr[:], ALU.mult))
                ch.sync()
                ch.mark(nc.vector.tensor_reduce(tmp[:], cw[:], AX_X, ALU.add))
                ch.sync()
                ch.mark(nc.vector.tensor_scalar(tmp[:], tmp[:], 1e-12, None, ALU.max))
                ch.sync()
                ch.mark(nc.vector.reciprocal(tmp[:], tmp[:]))
                ch.sync()
                nc.vector.tensor_tensor(cw[:], cw[:], bcast(tmp[:].unsqueeze(2)), ALU.mult).then_inc(c_ready, 1)
                dve_count[0] = ch.value()

            @block.tensor
            def _(pe):
                for p in range(PANELS + 1):
                    if p < PANELS:
                        if p >= 2:
                            pe.wait_ge(nTa_ready, p - 1)
                        for b in range(BPP):
                            last = nc.tensor.transpose(bank[4 + p % 2][:, b * P:(b + 1) * P], g0[:, p * BPP + b, :],
                                                       ident[:])
                        last.then_inc(g0_turned, 1)
                    if p >= 1:
                        q = p - 1
                        pe.wait_ge(nTa_ready, q + 1)
                        if q >= 2:
                            pe.wait_ge(x1_summed, q - 1)
                        for b in range(BPP):
                            blk = q * BPP + b
                            agg = accT[:, blk * P:(blk + 1) * P]
                            dst = bank[q % 2][:, b * P:(b + 1) * P]
                            nc.tensor.matmul(bank[7][:, blk:blk + 1], agg, ident[:, P - 1:P], start=True, stop=True)
                            nc.tensor.matmul(dst, agg, w_nbr[:], start=True, stop=False)
                            last = nc.tensor.matmul(dst, nTa[:, q % 2, b * P:(b + 1) * P], w_self[:],
                                                    start=False, stop=True)
                        last.then_inc(nbr_done, 1)
                for p in range(PANELS + 1):
                    if p < PANELS:
                        pe.wait_ge(n1_ready, p + 1)
                        if p >= 2:
                            pe.wait_ge(n1L_done, p - 1)
                        for b in range(BPP):
                            last = nc.tensor.transpose(bank[2 + p % 2][:, b * P:(b + 1) * P],
                                                       nb[:, p % 2, b * P:(b + 1) * P], ident[:])
                        last.then_inc(n1_turned, 1)
                    if p >= 1:
                        q = p - 1
                        pe.wait_ge(n1L_done, q + 1)
                        for blk in range(q * BPP, (q + 1) * BPP):
                            cols = slice(blk * P, (blk + 1) * P)
                            dst = bank[6][:, blk * E:(blk + 1) * E]
                            nc.tensor.matmul(dst, n1H[:, cols], routerH[:], start=True, stop=False)
                            nc.tensor.matmul(dst, n1L[:, cols], routerH[:], start=False, stop=False)
                            last = nc.tensor.matmul(dst, n1H[:, cols], routerL[:], start=False, stop=True)
                        last.then_inc(logits_done, 1)
                pe.wait_ge(c_ready, 1)
                for p in range(PANELS):
                    if p >= 2:
                        pe.wait_ge(ct_ready, p - 1)
                    for b in range(BPP):
                        last = nc.tensor.transpose(bank[4 + p % 2][0:E, b * P:(b + 1) * P], cw[:, p * BPP + b, :],
                                                   ident[:])
                    last.then_inc(c_turned, 1)

        W1RAW = stage[:].rearrange("p s n -> p (s n)")
        stageH_done = sem("stageH_done")
        stageL_done = sem("stageL_done")
        cb_in = [sem(f"cb_in{s}") for s in range(4)]
        ct_in = sem("ct_in")
        z_done = sem("z_done")
        gelu_done = sem("gelu_done")
        scaled = sem("scaled")
        hH_done = sem("hH_done")
        hL_done = sem("hL_done")
        y_done = sem("y_done")
        y_copied = sem("y_copied")
        ZB = bank[0:4]
        YB = bank[4]

        with nc.Block() as block:
            @block.sync
            def _(sp):
                def panel(p):
                    sp.wait_ge(y_done, p * E + 1)
                    sp.dma_start(ct0[:], c0_dram[:, bass.ds(p * W, W)]).then_inc(ct_in, 16)
                    for e in range(E):
                        sp.wait_ge(scaled, p * E + (e + 1))
                        sp.dma_start(cb0[:, e % 4, :], c0_dram[e, bass.ds(p * W, W)].partition_broadcast(P)
                                     ).then_inc(cb_in[e % 4], 16)

                with sp.Fori(0, PANELS) as p:
                    panel(p)
                sp.wait_ge(stageL_done, 1)
                sp.dma_start(W1RAW.rearrange("p (e q d) -> p e q d", e=E, q=2),
                             w2_1.rearrange("e (q h) d -> h e q d", q=2)).then_inc(stage_in, 16)

            @block.scalar
            def _(act):
                act.wait_ge(stage_in, 16)
                nc.scalar.activation(w1H1[:], W1RAW, ACT.Copy).then_inc(stageH_done, 1)

                def gelu(p, e):
                    act.wait_ge(z_done, p * E + (e + 1))
                    act.wait_ge(hL_done, p * E + (e + 1))
                    nc.scalar.activation(h0[:, e % 4, :], ZB[e % 4][:], ACT.Gelu, bias=b1s0[:, e:e + 1]
                                         ).then_inc(gelu_done, 1)

                def round_h(p, e):
                    act.wait_ge(scaled, p * E + (e + 5))
                    act.wait_ge(y_done, p * E + (e + 7))
                    nc.scalar.activation(hH0[:, e % 2, :], h0[:, e % 4, :], ACT.Copy).then_inc(hH_done, 1)

                def y_out(p):
                    act.wait_ge(y_done, p * E + 16)
                    nc.scalar.activation(yT[:, bass.ds(p * W, W)], YB[:], ACT.Copy).then_inc(y_copied, 1)

                def panel(p, first=False, last=False):
                    for e in range(E):
                        if e < E - 2:
                            gelu(p, e + 2)
                        elif not last:
                            gelu(p + 1, e + 2 - E)
                        if e == 1 and not first:
                            y_out(p - 1)
                        round_h(p, e)

                act.sem_inc(gelu_done, 4)
                act.sem_inc(y_copied, 1)
                gelu(0, 0)
                gelu(0, 1)
                panel(0, first=True)
                with act.Fori(1, PANELS - 1) as p:
                    panel(p)
                panel(PANELS - 1, last=True)
                y_out(PANELS - 1)
                act.wait_ge(stage_in, 32)
                nc.scalar.activation(w2H1[:], W1RAW, ACT.Copy).then_inc(stageH_done, 1)

            @block.gpsimd
            def _(pool):
                pool.sem_inc(scaled, 4)
                with pool.Fori(0, PANELS) as p:
                    for e in range(E):
                        pool.wait_ge(gelu_done, p * E + (e + 5))
                        pool.wait_ge(cb_in[e % 4], (p * 2 + (e // 4 + 1)) * 16)
                        nc.gpsimd.tensor_tensor(h0[:, e % 4, :], h0[:, e % 4, :], cb0[:, e % 4, :], ALU.mult
                                                ).then_inc(scaled, 1)

            @block.vector
            def _(v):
                v.sem_inc(hL_done, 4)
                v.wait_ge(stageH_done, 1)
                nc.vector.tensor_tensor(w1L1[:], W1RAW, w1H1[:].bitcast(F32), ALU.subtract).then_inc(stageL_done, 1)
                with v.Fori(0, PANELS) as p:
                    for e in range(E):
                        v.wait_ge(hH_done, p * E + (e + 1))
                        nc.vector.tensor_tensor(hL0[:, e % 2, :], h0[:, e % 4, :], hH0[:, e % 2, :].bitcast(F32),
                                                ALU.subtract).then_inc(hL_done, 1)
                v.wait_ge(stageH_done, 2)
                nc.vector.tensor_tensor(w2L1[:], W1RAW, w2H1[:].bitcast(F32), ALU.subtract).then_inc(stageL_done, 1)

            @block.tensor
            def _(pe):
                pe.sem_inc(y_done, 8)

                def z(p, e):
                    pe.wait_ge(gelu_done, p * E + (e + 1))
                    cols = bass.ds(p * W, W)
                    nc.tensor.matmul(ZB[e % 4][:], w1H0[:, e, :], n1H[:, cols], start=True, stop=False)
                    nc.tensor.matmul(ZB[e % 4][:], w1H0[:, e, :], n1L[:, cols], start=False, stop=False)
                    nc.tensor.matmul(ZB[e % 4][:], w1L0[:, e, :], n1H[:, cols], start=False, stop=True
                                     ).then_inc(z_done, 1)

                def y(p, e):
                    if e == 0:
                        pe.wait_ge(ct_in, p * 16 + 16)
                        pe.wait_ge(y_copied, p + 1)
                        nc.tensor.matmul(YB[:], b2s0[:], ct0[:], start=True, stop=False)
                    pe.wait_ge(hL_done, p * E + (e + 5))
                    nc.tensor.matmul(YB[:], w2H0[:, e, :], hH0[:, e % 2, :], start=False, stop=False)
                    nc.tensor.matmul(YB[:], w2H0[:, e, :], hL0[:, e % 2, :], start=False, stop=False)
                    nc.tensor.matmul(YB[:], w2L0[:, e, :], hH0[:, e % 2, :], start=False, stop=(e == E - 1)
                                     ).then_inc(y_done, 1)

                def panel(p, last=False):
                    for e in range(E):
                        if e + 3 < E:
                            z(p, e + 3)
                        elif not last:
                            z(p + 1, e + 3 - E)
                        y(p, e)

                for e in range(3):
                    z(0, e)
                with pe.Fori(0, PANELS - 1) as p:
                    panel(p)
                panel(PANELS - 1, last=True)

        yt_turned = sem("yt_turned")
        x2_summed = sem("x2_summed")
        n2_ready = sem("n2_ready")
        xb_biased = sem("xb_biased")
        n2_turned = sem("n2_turned")
        n2T_ready = sem("n2T_ready")
        support_done = sem("support_done")
        g_scaled = sem("g_scaled")
        gH_done = sem("gH_done")
        gL_done = sem("gL_done")
        xb_done = sem("xb_done")
        xb_out = sem("xb_out")
        raw3_in = [sem(f"raw3_in{s}") for s in range(RING3)]

        with nc.Block() as block:
            @block.sync
            def _(sp):
                sp.wait_ge(stageL_done, 2)
                for t in range(RING3 - 1):
                    sp.dma_start(raw3[:, t, :], adj_tile(0, t)).then_inc(raw3_in[t], 16)
                for p in range(PANELS):
                    sp.wait_ge(xb_done, p + 1)
                    sp.dma_start(rows(xb_dram, p), xn[:, p * BPP:(p + 1) * BPP, :]).then_inc(xb_out, 16)
                sp.wait_ge(xb_out, 16 * PANELS)

            @block.scalar
            def _(act):
                for p in range(PANELS + 1):
                    if p < PANELS:
                        act.wait_ge(n2_turned, p + 1)
                        if p >= 2:
                            act.wait_ge(support_done, p - 1)
                        nc.scalar.activation(nT2[:, p % 2, :], bank[2 + p % 2][:], ACT.Copy).then_inc(n2T_ready, 1)
                    if p >= 1:
                        q = p - 1
                        act.wait_ge(g_scaled, q + 1)
                        nc.scalar.activation(gH[:, q * W:(q + 1) * W], gf[:, q % 2, :], ACT.Copy).then_inc(gH_done, 1)

            @block.gpsimd
            def _(pool):
                for p in range(PANELS):
                    pool.wait_ge(n2_ready, p + 1)
                    panel = xn[:, p * BPP:(p + 1) * BPP, :]
                    nc.gpsimd.tensor_tensor(panel, panel, bias1[:].unsqueeze(1).to_broadcast([P, BPP, P]), ALU.add
                                            ).then_inc(xb_biased, 1)

            @block.vector
            def _(v):
                ch = Chain(v, dve, dve_count[0])
                for p in range(PANELS):
                    v.wait_ge(yt_turned, p + 1)
                    panel = xn[:, p * BPP:(p + 1) * BPP, :].rearrange("p b d -> p (b d)")
                    nc.vector.tensor_tensor(panel, bank[p % 2][:], panel, ALU.add).then_inc(x2_summed, 1)
                    v.wait_ge(x2_summed, p + 1)
                    for b in range(p * BPP, (p + 1) * BPP):
                        ch.mark(nc.vector.bn_stats(stats3[:, b, :], xn[:, b, :]))
                ch.sync()
                for b in range(BLOCKS):
                    ch.mark(nc.vector.bn_aggr(mv[:, b, :], stats3[:, b, :]))
                ch.sync()
                ch.mark(nc.vector.tensor_scalar(vpe[:], mv[:, :, 1], EPS, None, ALU.add))
                rsqrt_steps(nc, ch, vpe[:], rstd[:], tmp[:])
                ch.sync()
                for p in range(PANELS + 1):
                    if p < PANELS:
                        if p >= 2:
                            v.wait_ge(n2_turned, p - 1)
                        for b in range(BPP):
                            blk = p * BPP + b
                            ins = nc.vector.tensor_scalar(nb2[:, p % 2, b * P:(b + 1) * P], xn[:, blk, :],
                                                          mv[:, blk, 0:1], rstd[:, blk:blk + 1],
                                                          ALU.subtract, ALU.mult)
                        ins.then_inc(n2_ready, 1)
                    if p >= 1:
                        q = p - 1
                        v.wait_ge(support_done, q + 1)
                        if q >= 2:
                            v.wait_ge(gH_done, q - 1)
                            v.wait_ge(xb_done, q - 1)
                        for b in range(BPP):
                            blk = q * BPP + b
                            ins = nc.vector.tensor_scalar(gf[:, q % 2, b * P:(b + 1) * P],
                                                          bank[4 + q % 2][:, b * P:(b + 1) * P],
                                                          dinv[:, blk:blk + 1], None, ALU.mult)
                        ins.then_inc(g_scaled, 1)
                        v.wait_ge(g_scaled, q + 1)
                        v.wait_ge(xb_biased, q + 1)
                        for b in range(BPP):
                            blk = q * BPP + b
                            ins = nc.vector.scalar_tensor_tensor(out=xn[:, blk, :], in0=gf[:, q % 2, b * P:(b + 1) * P],
                                                                 scalar=dinv[:, blk:blk + 1], in1=xn[:, blk, :],
                                                                 op0=ALU.mult, op1=ALU.add)
                        ins.then_inc(xb_done, 1)
                        v.wait_ge(gH_done, q + 1)
                        nc.vector.tensor_tensor(gL[:, q * W:(q + 1) * W], gf[:, q % 2, :],
                                                gH[:, q * W:(q + 1) * W].bitcast(F32), ALU.subtract
                                                ).then_inc(gL_done, 1)
                dve_count[0] = ch.value()

            @block.tensor
            def _(pe):
                for p in range(PANELS):
                    if p >= 2:
                        pe.wait_ge(x2_summed, p - 1)
                    for b in range(BPP):
                        blk = p * BPP + b
                        last = nc.tensor.transpose(bank[p % 2][:, b * P:(b + 1) * P], yT[:, blk * P:(blk + 1) * P],
                                                   ident[:])
                    last.then_inc(yt_turned, 1)
                for p in range(PANELS + 1):
                    if p < PANELS:
                        pe.wait_ge(n2_ready, p + 1)
                        if p >= 2:
                            pe.wait_ge(n2T_ready, p - 1)
                        for b in range(BPP):
                            last = nc.tensor.transpose(bank[2 + p % 2][:, b * P:(b + 1) * P],
                                                       nb2[:, p % 2, b * P:(b + 1) * P], ident[:])
                        last.then_inc(n2_turned, 1)
                    if p >= 1:
                        q = p - 1
                        pe.wait_ge(n2T_ready, q + 1)
                        if q >= 2:
                            pe.wait_ge(g_scaled, q - 1)
                        for b in range(BPP):
                            last = nc.tensor.matmul(bank[4 + q % 2][:, b * P:(b + 1) * P],
                                                    nT2[:, q % 2, b * P:(b + 1) * P], w_l1[:], start=True, stop=True)
                        last.then_inc(support_done, 1)

        hi3_done = sem("hi3_done")
        lo3_done = sem("lo3_done")
        split3_used = sem("split3_used")
        o_copied = sem("o_copied")
        o_turned = sem("o_turned")
        xb3_in = sem("xb3_in")
        x3_done = sem("x3_done")
        n3_ready = sem("n3_ready")
        n3_turned = sem("n3_turned")
        n3H_done = sem("n3H_done")
        n3L_done = sem("n3L_done")
        logits3_done = sem("logits3_done")
        shifted3 = sem("shifted3")
        exp3_done = sem("exp3_done")
        c3_ready = sem("c3_ready")
        c3_turned = sem("c3_turned")
        ct3_ready = sem("ct3_ready")
        c3_out = sem("c3_out")
        cb3_in = [sem(f"cb3_in{s}") for s in range(4)]
        z3_done = sem("z3_done")
        relu_done = sem("relu_done")
        scaled3 = sem("scaled3")
        hH3_done = sem("hH3_done")
        hL3_done = sem("hL3_done")
        y3_done = sem("y3_done")
        y3_copied = sem("y3_copied")
        y3_turned = sem("y3_turned")
        out_ready = sem("out_ready")
        out_stored = sem("out_stored")
        dve3 = sem("dve3")
        ZB = bank[0:2]
        YB = bank[2:4]
        OG = bank[4:6]
        M1 = bank[6]
        M2 = bank[7]
        S = 2 * E
        CHAIN3 = 37
        LAST = PANELS + 2
        assert S == PANELS

        def chains(p):
            return min(p, PANELS) if isinstance(p, int) else p

        def active(p):
            return dict(tiles=p < PANELS, chain=1 <= p <= PANELS, ffn=2 <= p <= PANELS + 1, fin=3 <= p,
                        ahead=p < PANELS - 1)

        def over_panels(eng, panel):
            for p in range(4):
                panel(p, p % 2, **active(p))
            with eng.Fori(4, PANELS - 2, 2) as p:
                panel(p, 0, **active(4))
                panel(p + 1, 1, **active(5))
            for p in range(PANELS - 2, LAST + 1):
                panel(p, p % 2, **active(p))

        with nc.Block() as block:
            @block.sync
            def _(sp):
                def load_c(c, e):
                    if e == 0:
                        sp.wait_ge(c3_out, (c + 1) * 16)
                    else:
                        sp.wait_ge(scaled3, c * S + (2 * (e - 4) + 2 + 8))
                    sp.dma_start(cb1[:, e % 4, :], c1_dram[bass.ds(c * E + e, 1), :].to_broadcast([P, W])
                                 ).then_inc(cb3_in[e % 4], 16)

                def panel(p, odd, tiles, chain, ffn, fin, ahead):
                    for t in range(PANELS):
                        if tiles and not (isinstance(p, int) and p == 0 and t < RING3 - 1):
                            sp.wait_ge(lo3_done, p * (2 * PANELS) + (2 * t + 2))
                            sp.dma_start(raw3[:, t % RING3, :], adj_tile(p, t)).then_inc(raw3_in[t % RING3], 16)
                        if ffn and t == 1:
                            sp.wait_ge(ct3_ready, p - 1)
                            sp.dma_start(c1_dram[bass.ds((p - 2) * E, E), :], ct1[:]).then_inc(c3_out, 16)
                        if ffn and t == 2:
                            load_c(p - 2, 0)
                        if ffn and t % 2 and t >= 3:
                            load_c(p - 2, (t - 1) // 2)
                        if fin and t == 6:
                            sp.wait_ge(out_ready, p - 2)
                            sp.dma_start(rows(out, p - 3), outb[:].rearrange("p (b d) -> p b d", d=P)
                                         ).then_inc(out_stored, 16)
                        if tiles and t == 12:
                            if not (isinstance(p, int) and p == 0):
                                sp.wait_ge(n3_turned, p * 1)
                            sp.dma_start(xbt[:].rearrange("p (b d) -> p b d", d=P), rows(xb_dram, p)
                                         ).then_inc(xb3_in, 16)

                over_panels(sp, panel)
                sp.wait_ge(out_stored, 16 + 16 * PANELS)

            @block.scalar
            def _(act):
                def split(p, t):
                    for h in range(2):
                        act.wait_ge(raw3_in[t % RING3], (p * 4 + (t // RING3 + 1)) * 16)
                        act.wait_ge(split3_used, p * 32 + (2 * t + h + 1))
                        nc.scalar.activation(hi3[:, (2 * t + h) % 4, :], raw3[:, t % RING3, h * HALF:(h + 1) * HALF],
                                             ACT.Copy).then_inc(hi3_done, 1)

                def relu(c, s):
                    act.wait_ge(z3_done, c * S + (s + 1))
                    act.wait_ge(hL3_done, c * S + (s + 1))
                    nc.scalar.activation(h1[:, s % 4, :], ZB[s % 2][:], ACT.Relu, bias=b1s1[:, s // 2, s % 2:s % 2 + 1]
                                         ).then_inc(relu_done, 1)

                def round_h(c, s):
                    act.wait_ge(scaled3, c * S + (s + 9))
                    act.wait_ge(y3_done, c * S + (s + 1))
                    nc.scalar.activation(hH1[:, s % 2, :], h1[:, s % 4, :], ACT.Copy).then_inc(hH3_done, 1)

                def panel(p, odd, tiles, chain, ffn, fin, ahead):
                    c = p - 1
                    for t in range(PANELS):
                        if chain and t == 8:
                            act.wait_ge(n3_turned, p * 1)
                            nc.scalar.activation(n3H[:, 1 - odd, :], M1[:], ACT.Copy).then_inc(n3H_done, 1)
                        if chain and t == 13:
                            act.wait_ge(c3_turned, p * 1)
                            nc.scalar.activation(ct1[:], M2[0:E, :], ACT.Copy).then_inc(ct3_ready, 1)
                        if tiles and t < PANELS - 1:
                            split(p, t + 1)
                        if ahead and t == PANELS - 1:
                            split(p + 1, 0)
                        if chain and t == 11:
                            act.wait_ge(shifted3, p * 1)
                            nc.scalar.activation(ex3[:], ex3[:], ACT.Exp).then_inc(exp3_done, 1)
                        if ffn and t + 2 < S:
                            relu(p - 2, t + 2)
                        if chain and t + 2 >= S:
                            relu(c, t + 2 - S)
                        if ffn:
                            round_h(p - 2, t)
                        if chain and t == 0:
                            act.wait_ge(split3_used, p * 32 + 4)
                            if fin:
                                act.wait_ge(out_stored, (p - 2) * 16)
                            nc.scalar.activation(oT[:], OG[1 - odd][:], ACT.Copy).then_inc(o_copied, 1)
                        if fin and t == 0:
                            act.wait_ge(y3_done, (p - 2) * S + 2)
                            nc.scalar.activation(yTb[:], YB[1 - odd][:], ACT.Copy).then_inc(y3_copied, 1)

                act.sem_inc(o_copied, 1)
                act.sem_inc(y3_copied, 1)
                act.sem_inc(relu_done, 4)
                split(0, 0)
                over_panels(act, panel)

            @block.gpsimd
            def _(pool):
                pool.sem_inc(scaled3, 8)
                with pool.Fori(0, PANELS) as c:
                    for s in range(S):
                        pool.wait_ge(relu_done, c * S + (s + 5))
                        pool.wait_ge(cb3_in[(s // 2) % 4], (c * 2 + (s // 8 + 1)) * 16)
                        nc.gpsimd.tensor_tensor(h1[:, s % 4, :], h1[:, s % 4, :], cb1[:, (s // 2) % 4, :], ALU.mult
                                                ).then_inc(scaled3, 1)

            @block.vector
            def _(v):
                ch = Chain(v, dve3)

                def split(p, t):
                    for h in range(2):
                        v.wait_ge(hi3_done, p * 32 + (2 * t + h + 1))
                        slot = (2 * t + h) % 4
                        nc.vector.tensor_tensor(lo3[:, slot, :], raw3[:, t % RING3, h * HALF:(h + 1) * HALF],
                                                hi3[:, slot, :].bitcast(F32), ALU.subtract).then_inc(lo3_done, 1)

                def rest_h(c, s):
                    v.wait_ge(hH3_done, c * S + (s + 1))
                    nc.vector.tensor_tensor(hL1[:, s % 2, :], h1[:, s % 4, :], hH1[:, s % 2, :].bitcast(F32),
                                            ALU.subtract).then_inc(hL3_done, 1)

                def finish(p, f, odd):
                    v.wait_ge(y3_turned, f + 1)
                    v.wait_ge(o_turned, chains(p))
                    if isinstance(p, int) and p > PANELS:
                        v.wait_ge(out_stored, (p - 2) * 16)
                    nc.vector.tensor_tensor(outb[:], M2[:], x3[:, 1 - odd, :], ALU.add).then_inc(out_ready, 1)

                def rows3(p, c, odd, fin):
                    v.wait_ge(o_turned, p * 1)
                    v.wait_ge(xb3_in, p * 16)
                    if fin:
                        v.wait_ge(out_ready, p - 2)
                    for b in range(BPP):
                        blk = slice(b * P, (b + 1) * P)
                        ins = nc.vector.scalar_tensor_tensor(out=x3[:, 1 - odd, blk], in0=M1[:, blk],
                                                             scalar=dinv[:, bass.ds(c * BPP + b, 1)],
                                                             in1=xbt[:, blk], op0=ALU.mult, op1=ALU.add)
                    ins.then_inc(x3_done, 1)

                def stats_rows3(p, odd):
                    v.wait_ge(x3_done, p * 1)
                    hold(nc.vector, scrap_v[:])
                    for b in range(BPP):
                        ch.mark(nc.vector.bn_stats(st3[:, b, :], x3[:, 1 - odd, b * P:(b + 1) * P]))
                    ch.sync()
                    hold(nc.vector, scrap_v[:])
                    for b in range(BPP):
                        ch.mark(nc.vector.bn_aggr(mv3[:, b, :], st3[:, b, :]))
                    ch.sync()
                    ch.mark(nc.vector.tensor_scalar(v3[:], mv3[:, :, 1], EPS, None, ALU.add))

                def norm3(c, odd):
                    ch.sync()
                    for b in range(BPP):
                        blk = slice(b * P, (b + 1) * P)
                        ins = nc.vector.tensor_scalar(nb3[:, blk], x3[:, 1 - odd, blk], mv3[:, b, 0:1], r3[:, b:b + 1],
                                                      ALU.subtract, ALU.mult)
                    ins.then_inc(n3_ready, 1)

                def gates(p):
                    v.wait_ge(logits3_done, p * 1)
                    ch.mark(nc.vector.tensor_tensor(lg3[:], M2[:, 0:BPP * E].rearrange("p (b e) -> p b e", e=E),
                                                    gate_row[:].unsqueeze(1).to_broadcast([P, BPP, E]), ALU.add))
                    ch.sync()
                    hold(nc.vector, scrap_v[:])
                    for b in range(BPP):
                        ch.mark(nc.vector.max(mx3[:, b, :], lg3[:, b, :]))
                    ch.sync()
                    nc.vector.tensor_tensor(ex3[:], mx3[:, :, 1], mx3[:, :, 0], ALU.subtract).then_inc(shifted3, 1)
                    for b in range(BPP):
                        ins = nc.vector.max_index(ix3[:, b, :], mx3[:, b, :], lg3[:, b, :])
                    ch.mark(ins)

                def weights(p):
                    ch.sync()
                    ch.mark(nc.vector.tensor_copy(if3[:, :, 0:2], ix3[:, :, 0:2]))
                    v.wait_ge(exp3_done, p * 1)
                    ch.mark(nc.vector.tensor_scalar(t3[:], ex3[:], 1.0, None, ALU.add))
                    ch.sync()
                    ch.mark(nc.vector.reciprocal(t3[:], t3[:]))
                    ch.sync()
                    ch.mark(nc.vector.tensor_tensor(v3[:], t3[:], ex3[:], ALU.mult))
                    iota3 = iota_f[:].unsqueeze(1).to_broadcast([P, BPP, E])
                    ch.mark(nc.vector.tensor_tensor(m13[:], iota3, bcast(if3[:, :, 0:1], BPP), ALU.is_equal))
                    ch.mark(nc.vector.tensor_tensor(m23[:], iota3, bcast(if3[:, :, 1:2], BPP), ALU.is_equal))
                    ch.sync()
                    ch.mark(nc.vector.tensor_tensor(m13[:], m13[:], bcast(t3[:].unsqueeze(2), BPP), ALU.mult))
                    ch.mark(nc.vector.tensor_tensor(m23[:], m23[:], bcast(v3[:].unsqueeze(2), BPP), ALU.mult))
                    ch.sync()
                    nc.vector.tensor_tensor(c3[:], m13[:], m23[:], ALU.add).then_inc(c3_ready, 1)

                def panel(p, odd, tiles, chain, ffn, fin, ahead):
                    c = p - 1
                    if chain:
                        ch.rebase(c * CHAIN3)
                    for t in range(PANELS):
                        if tiles and t < PANELS - 1:
                            split(p, t + 1)
                        if ahead and t == PANELS - 1:
                            split(p + 1, 0)
                        if ffn:
                            rest_h(p - 2, t)
                        if fin and t == 2:
                            finish(p, p - 3, odd)
                        if chain and t == 2:
                            rows3(p, c, odd, fin)
                        if chain and t == 3:
                            stats_rows3(p, odd)
                        if chain and t == 4:
                            rsqrt_start(nc, ch, v3[:], r3[:], t3[:])
                            newton_step(nc, ch, v3[:], r3[:], t3[:])
                        if chain and t == 5:
                            newton_step(nc, ch, v3[:], r3[:], t3[:])
                            newton_step(nc, ch, v3[:], r3[:], t3[:])
                        if chain and t == 6:
                            norm3(c, odd)
                        if chain and t == 8:
                            v.wait_ge(n3H_done, p * 1)
                            nc.vector.tensor_tensor(n3L[:, 1 - odd, :], M1[:], n3H[:, 1 - odd, :].bitcast(F32),
                                                    ALU.subtract).then_inc(n3L_done, 1)
                        if chain and t == 10:
                            gates(p)
                        if chain and t == 11:
                            weights(p)
                    if chain:
                        assert ch.n == CHAIN3, ch.n

                v.sem_inc(lo3_done, 8)
                v.sem_inc(hL3_done, 4)
                v.sem_inc(out_stored, 16)
                v.wait_ge(gL_done, PANELS)
                split(0, 0)
                over_panels(v, panel)

            @block.tensor
            def _(pe):
                def gnn(p, t, odd):
                    for h in range(2):
                        unit = (2 * t + h) % 4
                        pe.wait_ge(lo3_done, p * 32 + (2 * t + h + 9))
                        if t == 0 and h == 0 and not (isinstance(p, int) and p < 2):
                            pe.wait_ge(o_copied, p * 1)
                        for b in range(2):
                            blk = slice((t * BPP + 2 * h + b) * P, (t * BPP + 2 * h + b + 1) * P)
                            cols = slice(b * W, (b + 1) * W)
                            first = t == 0 and h == 0 and b == 0
                            end = t == PANELS - 1 and h == 1 and b == 1
                            nc.tensor.matmul(OG[odd][:], gH[:, blk], hi3[:, unit, cols], start=first, stop=False)
                            nc.tensor.matmul(OG[odd][:], gH[:, blk], lo3[:, unit, cols], start=False, stop=False)
                            last = nc.tensor.matmul(OG[odd][:], gL[:, blk], hi3[:, unit, cols], start=False, stop=end)
                        last.then_inc(split3_used, 1)

                def z(c, s, par):
                    pe.wait_ge(relu_done, c * S + (s + 3))
                    pe.wait_ge(n3L_done, c + 1)
                    blk = slice(s * P, (s + 1) * P)
                    nc.tensor.matmul(ZB[s % 2][:], w1H1[:, blk], n3H[:, par, :], start=True, stop=False)
                    nc.tensor.matmul(ZB[s % 2][:], w1H1[:, blk], n3L[:, par, :], start=False, stop=False)
                    nc.tensor.matmul(ZB[s % 2][:], w1L1[:, blk], n3H[:, par, :], start=False, stop=True
                                     ).then_inc(z3_done, 1)

                def y(c, s, par):
                    blk = slice(s * P, (s + 1) * P)
                    if s == 0:
                        pe.wait_ge(ct3_ready, c + 1)
                        if not (isinstance(c, int) and c < 1):
                            pe.wait_ge(y3_copied, c * 1)
                        nc.tensor.matmul(YB[par][:], b2s1[:], ct1[:], start=True, stop=False)
                    pe.wait_ge(hL3_done, c * S + (s + 5))
                    nc.tensor.matmul(YB[par][:], w2H1[:, blk], hH1[:, s % 2, :], start=False, stop=False)
                    nc.tensor.matmul(YB[par][:], w2H1[:, blk], hL1[:, s % 2, :], start=False, stop=False)
                    nc.tensor.matmul(YB[par][:], w2L1[:, blk], hH1[:, s % 2, :], start=False, stop=(s == S - 1)
                                     ).then_inc(y3_done, 1)

                def turn(src, dst):
                    for b in range(BPP):
                        last = nc.tensor.transpose(dst[:, b * P:(b + 1) * P], src[:, b * P:(b + 1) * P], ident[:])
                    return last

                def panel(p, odd, tiles, chain, ffn, fin, ahead):
                    c = p - 1
                    for t in range(PANELS):
                        if tiles:
                            gnn(p, t, odd)
                        if fin and t == 1:
                            pe.wait_ge(y3_copied, p - 1)
                            pe.wait_ge(ct3_ready, chains(p - 1))
                            turn(yTb, M2).then_inc(y3_turned, 1)
                        if chain and t == 1:
                            pe.wait_ge(o_copied, p + 1)
                            turn(oT, M1).then_inc(o_turned, 1)
                        if chain and t == 7:
                            pe.wait_ge(n3_ready, p * 1)
                            turn(nb3, M1).then_inc(n3_turned, 1)
                        if chain and t == 9:
                            pe.wait_ge(n3L_done, p * 1)
                            if not (isinstance(p, int) and p < 3):
                                pe.wait_ge(out_ready, p - 2)
                            for b in range(BPP):
                                blk = slice(b * P, (b + 1) * P)
                                dst = M2[:, b * E:(b + 1) * E]
                                nc.tensor.matmul(dst, n3H[:, 1 - odd, blk], gateH[:], start=True, stop=False)
                                nc.tensor.matmul(dst, n3L[:, 1 - odd, blk], gateH[:], start=False, stop=False)
                                last = nc.tensor.matmul(dst, n3H[:, 1 - odd, blk], gateL[:], start=False, stop=True)
                            last.then_inc(logits3_done, 1)
                        if chain and t == 12:
                            pe.wait_ge(c3_ready, p * 1)
                            for b in range(BPP):
                                last = nc.tensor.transpose(M2[0:E, b * P:(b + 1) * P], c3[:, b, :], ident[:])
                            last.then_inc(c3_turned, 1)
                        if ffn and t + 3 < S:
                            z(p - 2, t + 3, odd)
                        if chain and t + 3 >= S:
                            z(c, t + 3 - S, 1 - odd)
                        if ffn:
                            y(p - 2, t, odd)

                pe.sem_inc(split3_used, 4)
                pe.sem_inc(y3_done, 2)
                over_panels(pe, panel)


_OUT = (N, P)


def kernel(**inputs):
    import numpy as _np
    import concourse.bacc as _bacc
    from concourse import mybir as _mybir
    from concourse.bass_utils import run_bass_kernel_spmd as _run

    a = {k: _np.asarray(v) for k, v in inputs.items()}
    tiles = a["adj"].reshape(PANELS, W, PANELS, BPP, P).transpose(0, 2, 4, 3, 1)
    laid = [
        ("x", a["x"]), ("adj_tiles", tiles), ("w_gnn0", a["L0_gnn_weight"]), ("bias_gnn0", a["L0_gnn_bias"]),
        ("router_t", a["L0_ffn_router_w"].T), ("w1_0", a["L0_ffn_w1"]), ("b1_0", a["L0_ffn_b1"].T),
        ("w2_0", a["L0_ffn_w2"]), ("b2_0", a["L0_ffn_b2"]), ("w_gnn1", a["L1_gnn_weight"]),
        ("bias_gnn1", a["L1_gnn_bias"]), ("gate_w", a["L1_ffn_Wg"]), ("gate_b", a["L1_ffn_bg"]),
        ("gate_bias", a["L1_ffn_bias"]), ("w1_1", a["L1_ffn_W1"]),
        ("b1_1", a["L1_ffn_b1"].reshape(E, 2, P).transpose(2, 0, 1)), ("w2_1", a["L1_ffn_W2"]),
        ("b2_1", a["L1_ffn_b2"]),
    ]
    nc = _bacc.Bacc("TRN2", target_bir_lowering=False, num_devices=1)
    arrays, args = {}, []
    for name, v in laid:
        v = _np.ascontiguousarray(v)
        if name == "adj_tiles":
            v = v.reshape(PANELS * PANELS * P, TILE)
        arrays[name] = v
        args.append(nc.dram_tensor(name, v.shape, _mybir.dt.from_np(v.dtype), kind="ExternalInput").ap())
    args.append(nc.dram_tensor("out", _OUT, F32, kind="ExternalOutput").ap())
    program(nc, *args)
    r = _run(nc, [arrays], core_ids=[0])
    return r.results[0]["out"]
```

```python
from contextlib import ExitStack

import concourse.bass as bass
from concourse import mybir

F32 = mybir.dt.float32
F32R = mybir.dt.float32r
I32 = mybir.dt.int32
U32 = mybir.dt.uint32
ACT = mybir.ActivationFunctionType
ALU = mybir.AluOpType
AX_X = mybir.AxisListType.X

P = 128
N = 8192
W = 512
PANELS = N // W
BLOCKS = N // P
BPP = W // P
TILE = BPP * W
HALF = TILE // 2
E = 8
EPS = 1e-5

RING1 = 5
RING3 = 4
PAIRS = PANELS // 2 - 1
RANKS = PAIRS + 1


class Chain:

    def __init__(self, eng, sem, start=0):
        self.eng, self.sem, self.base, self.n = eng, sem, start, 0

    def mark(self, ins):
        ins.then_inc(self.sem, 1)
        self.n += 1

    def value(self):
        return self.base + self.n

    def sync(self):
        self.eng.wait_ge(self.sem, self.base + self.n)

    def rebase(self, base):
        self.base, self.n = base, 0


def hold(engine, scrap):
    engine.tensor_tensor(scrap, scrap, scrap, ALU.mult)


def rsqrt_start(nc, ch, v, r, t):
    ch.sync()
    ch.mark(nc.vector.tensor_scalar(t.bitcast(I32), v.bitcast(I32), 1, None, ALU.arith_shift_right))
    ch.sync()
    ch.mark(nc.vector.tensor_scalar(r.bitcast(I32), t.bitcast(I32), -1.0, float(0x5F3759DF), ALU.mult, ALU.add))


def rsqrt_steps(nc, ch, v, r, t):
    rsqrt_start(nc, ch, v, r, t)
    for _ in range(3):
        newton_step(nc, ch, v, r, t)


def newton_step(nc, ch, v, r, t):
    ch.sync()
    ch.mark(nc.vector.tensor_tensor(t, v, r, ALU.mult))
    ch.sync()
    ch.mark(nc.vector.tensor_tensor(t, t, r, ALU.mult))
    ch.sync()
    ch.mark(nc.vector.tensor_scalar(t, t, -0.5, 1.5, ALU.mult, ALU.add))
    ch.sync()
    ch.mark(nc.vector.tensor_tensor(r, r, t, ALU.mult))


def program(nc, x, adj_tiles, w_gnn0, bias_gnn0, router_t, w1_0, b1_0, w2_0, b2_0,
            w_gnn1, bias_gnn1, gate_w, gate_b, gate_bias, w1_1, b1_1, w2_1, b2_1, out):
    xb_dram = nc.dram_tensor("xb_dram", [N, P], F32, kind="Internal").ap()
    sums_dram = nc.dram_tensor("sums_dram", [BLOCKS, P], F32, kind="Internal").ap()
    c0_dram = nc.dram_tensor("c0_dram", [BLOCKS * E, P], F32, kind="Internal").ap()
    c1_dram = nc.dram_tensor("c1_dram", [PANELS * E, W], F32, kind="Internal").ap()

    def rows(t, p):
        return t[bass.ds(p * W, W), :].rearrange("(b p) d -> p b d", p=P)

    def adj_tile(col_panel, row_panel):
        return adj_tiles[bass.ds((col_panel * PANELS + row_panel) * P, P), :]

    with ExitStack() as keep:
        def maker(stack):
            def sb(name, shape, dt=F32):
                return stack.enter_context(nc.sbuf_tensor(name, shape, dt))
            return sb

        def sem(name):
            return keep.enter_context(nc.semaphore(name))

        bank = [keep.enter_context(nc.psum_tensor(f"bank{b}", [P, W], F32)) for b in range(8)]

        sb = maker(keep)
        ident = sb("ident", [P, P])
        ones = sb("ones", [P, 2])
        iota_i = sb("iota_i", [P, E], I32)
        iota_f = sb("iota_f", [P, E])
        router = sb("router", [P, E])
        routerHL = sb("routerHL", [P, 2 * E], F32R)
        gate = sb("gate", [P, E])
        gateHL = sb("gateHL", [P, 2 * E], F32R)
        gate_row = sb("gate_row", [P, E])
        gate_row2 = sb("gate_row2", [P, E])
        b1s0 = sb("b1s0", [P, E])
        b2s0 = sb("b2s0", [E, P])
        b1s1 = sb("b1s1", [P, E, 2])
        b2s1 = sb("b2s1", [E, P])
        scrap_v = sb("scrap_v", [P, 1])
        scrap_p = sb("scrap_p", [P, 1])
        dinv = sb("dinv", [P, BLOCKS])
        mark_u = ExitStack()
        sbu = maker(mark_u)
        w1H0 = sbu("w1H0", [P, E, P], F32R)
        w1L0 = sbu("w1L0", [P, E, P], F32R)
        w2H0 = sbu("w2H0", [P, E, P], F32R)
        w2L0 = sbu("w2L0", [P, E, P], F32R)
        stage = sbu("stage", [P, 2, E * P])
        w_self = sbu("w_self", [P, P])
        w_nbr = sbu("w_nbr", [P, P])
        w_last = sbu("w_last", [P, P])
        w_edge = sbu("w_edge", [P, P])
        bias0 = sbu("bias0", [P, P])
        bias1 = sbu("bias1", [P, P])
        w_l1 = sbu("w_l1", [P, P])
        with ExitStack() as ste:
            e_rows = maker(ste)("e_rows", [P, 9 * BLOCKS])
        stats3 = sbu("stats3", [P, BLOCKS, 6])
        e_rows_rest = sbu("e_rows_rest", [P, 9 * BLOCKS - 6 * BLOCKS])
        e_cols = sbu("e_cols", [P, BLOCKS + BPP])
        e_cols8 = sbu("e_cols8", [P, BLOCKS // 2])
        row_sums = sbu("row_sums", [P, 2, BPP])
        e_sum = sbu("e_sum", [P, BLOCKS])
        rowsum = sbu("rowsum", [P, BLOCKS])
        mv = sbu("mv", [P, BLOCKS, 2])
        rstd = sbu("rstd", [P, BLOCKS])
        vpe = sbu("vpe", [P, BLOCKS])
        tmp = sbu("tmp", [P, BLOCKS])
        mark_u.close()
        raw3 = sb("raw3", [P, RING3, TILE])

        with ExitStack() as st:
            sb = maker(st)
            raw = sb("raw", [P, RING1, TILE])
            hi = sb("hi", [P, 3, HALF], F32R)
            lo = sb("lo", [P, 3, HALF], F32R)
            g0 = sb("g0", [P, BLOCKS, P])
            accT = sb("accT", [P, N])
            with ExitStack() as st0:
                sb0 = maker(st0)
                stats = sb0("stats", [P, BLOCKS, 6])
                shift0 = sb0("shift0", [P, BLOCKS])
            iwF = sb("iwF", [P, 2, W])
            iwH = sb("iwH", [P, 2, W // 2], F32R)
            iwL = sb("iwL", [P, 2, W // 2], F32R)
            jwH = sb("jwH", [P, 2, W], F32R)
            jwL = sb("jwL", [P, 2, W], F32R)
            prod = sb("prod", [P, 2, TILE])
            accP = sb("accP", [P, W])
            w_last_self = sb("w_last_self", [P, P])
        with ExitStack() as st:
            sb = maker(st)
            n1H = sb("n1H", [P, N], F32R)
            n1L = sb("n1L", [P, N], F32R)
            xn = sb("xn", [P, BLOCKS, P])
            with ExitStack() as stz:
                sbz = maker(stz)
                accT_place = sbz("accT_place", [P, N])
                sbv = sbz
                stats2 = sbv("stats2", [P, BLOCKS, 6])
                bt = sbv("bt", [P, 4, W])
                nb = sbv("nb", [P, 4, W])
                lg = sbv("lg", [P, BLOCKS, E])
                mx = sbv("mx", [P, BLOCKS, E])
                ix = sbv("ix", [P, BLOCKS, E], U32)
                pr = sbv("pr", [P, BLOCKS, E])
                cw = sbv("cw", [P, BLOCKS, E])
                cwT = sbv("cwT", [P, W])
                sums_by_block = sbv("sums_by_block", [BLOCKS, P])
                nTa = sbv("nTa", [P, 2, W])
            w1H1 = sb("w1H1", [P, E * 2 * P], F32R)
            w1L1 = sb("w1L1", [P, E * 2 * P], F32R)
            w2H1 = sb("w2H1", [P, E * 2 * P], F32R)
            w2L1 = sb("w2L1", [P, E * 2 * P], F32R)
            with ExitStack() as stv:
                sbv = maker(stv)
                h0 = sbv("h0", [P, E, W])
                hH0 = sbv("hH0", [P, 2, W], F32R)
                hL0 = sbv("hL0", [P, 2, W], F32R)
                cb0 = sbv("cb0", [P, E, W])
                ct0 = sbv("ct0", [E, W])
                yTa = sbv("yTa", [P, W])
            with ExitStack() as stv:
                sbv = maker(stv)
                nb2 = sbv("nb2", [P, 4, W])
                nT2 = sbv("nT2", [P, 2, W])
                gf = sbv("gf", [P, 4, W])
        with ExitStack() as st:
            sb = maker(st)
            gH = sb("gH", [P, N], F32R)
            gL = sb("gL", [P, N], F32R)
            hi3 = sb("hi3", [P, 4, HALF], F32R)
            lo3 = sb("lo3", [P, 4, HALF], F32R)
            w_place = sb("w_place", [P, 4 * E * 2 * P])
            h1 = sb("h1", [P, 4, W])
            hH1 = sb("hH1", [P, 2, W], F32R)
            hL1 = sb("hL1", [P, 2, W], F32R)
            cb1 = sb("cb1", [P, 4, W])
            n3H = sb("n3H", [P, 2, W], F32R)
            n3L = sb("n3L", [P, 2, W], F32R)
            oT = sb("oT", [P, W])
            outb = oT
            yTb = sb("yTb", [P, W])
            x3 = sb("x3", [P, 2, W])
            nb3 = sb("nb3", [P, W])
            xbt = nb3
            ct1 = sb("ct1", [E, W])
            st3 = sb("st3", [P, BPP, 6])
            mv3 = sb("mv3", [P, BPP, 2])
            v3 = sb("v3", [P, BPP])
            r3 = sb("r3", [P, BPP])
            t3 = sb("t3", [P, BPP])
            lg3 = sb("lg3", [P, BPP, E])
            mx3 = sb("mx3", [P, BPP, E])
            ix3 = sb("ix3", [P, BPP, E], U32)
            if3 = sb("if3", [P, BPP, E])
            m13 = sb("m13", [P, BPP, E])
            m23 = sb("m23", [P, BPP, E])
            ex3 = sb("ex3", [P, BPP])
            c3 = sb("c3", [P, BPP, E])

        small_in = sem("small_in")
        experts_in = sem("experts_in")
        x_in = [sem(f"x_in{c}") for c in range(4)]
        ident_zero = sem("ident_zero")
        consts_done = sem("consts_done")
        iota_done = sem("iota_done")
        dve = sem("dve")
        dve_count = [0]
        stats_ready = sem("stats_ready")
        n0_ready = sem("n0_ready")
        n0_ready_act = sem("n0_ready_act")
        smallH_done = sem("smallH_done")
        weightsH_done = sem("weightsH_done")
        weights_done = sem("weights_done")
        g0_done = sem("g0_done")
        acc_zero = sem("acc_zero")

        SHARE = 36

        def setup_sync(sp):
            for c in range(4):
                sp.dma_start(accT[:, c * 4 * W:(c + 1) * 4 * W].rearrange("p (b d) -> p b d", d=P),
                             x[c * 4 * W:(c + 1) * 4 * W, :].rearrange("(b p) d -> p b d", p=P)
                             ).then_inc(x_in[c], 16)

        def setup_scalar(act, first_split):
            loads = [(w_self, w_gnn0[0:P, :]), (w_last_self, w_gnn0[P - 1, :].partition_broadcast(P)), (w_nbr, w_gnn0[P:2 * P, :]),
                     (w_last, w_gnn0[2 * P - 1, :].partition_broadcast(P)),
                     (w_edge, w_gnn0[2 * P, :].partition_broadcast(P)),
                     (bias0, bias_gnn0.partition_broadcast(P)), (bias1, bias_gnn1.partition_broadcast(P)),
                     (w_l1, w_gnn1), (router, router_t), (gate, gate_w),
                     (gate_row, gate_b.partition_broadcast(P)), (gate_row2, gate_bias.partition_broadcast(P)),
                     (b1s0, b1_0), (b2s0, b2_0), (b1s1, b1_1), (b2s1, b2_1)]
            for dst, src in loads:
                act.dma_start(dst[:], src).then_inc(small_in, 16)
            for s, w in enumerate((w1_0, w2_0)):
                act.dma_start(stage[:, s, :].rearrange("p (e n) -> p e n", e=E), w.rearrange("e k n -> k e n")
                              ).then_inc(experts_in, 16)
            first_split()
            act.wait_ge(stats_ready, 1)
            for b in range(SHARE, BLOCKS):
                ins = nc.scalar.activation(g0[:, b, :], accT[:, b * P:(b + 1) * P], ACT.Identity,
                                           bias=shift0[:, b:b + 1], scale=rstd[:, b:b + 1])
                if b % BPP == BPP - 1:
                    ins.then_inc(n0_ready_act, 1)
            act.wait_ge(small_in, 16 * len(loads))
            nc.scalar.activation(routerHL[:, 0:E], router[:], ACT.Copy).then_inc(smallH_done, 1)
            nc.scalar.activation(gateHL[:, 0:E], gate[:], ACT.Copy).then_inc(smallH_done, 1)

        def setup_gpsimd(pool):
            nc.gpsimd.memset(ident[:], 0.0).then_inc(ident_zero, 1)
            nc.gpsimd.iota(iota_i[:], [[1, E]], base=0, channel_multiplier=0).then_inc(iota_done, 1)
            pool.wait_ge(ident_zero, 1)
            nc.gpsimd.affine_select(out=ident[:], in_=ident[:], compare_op=ALU.not_equal, fill=1.0, base=0,
                                    pattern=[[-1, P]], channel_multiplier=1).then_inc(consts_done, 1)
            nc.gpsimd.memset(ones[:], 1.0).then_inc(consts_done, 1)
            nc.gpsimd.memset(scrap_v[:], 0.0).then_inc(consts_done, 1)
            nc.gpsimd.memset(scrap_p[:], 0.0).then_inc(consts_done, 1)
            nc.gpsimd.memset(e_rows[:], 0.0).then_inc(consts_done, 1)
            for c in range(4):
                pool.wait_ge(n0_ready, min(4 * (c + 1), SHARE // BPP))
                if 4 * (c + 1) > SHARE // BPP:
                    pool.wait_ge(n0_ready_act, 4 * (c + 1) - SHARE // BPP)
                nc.gpsimd.memset(accT[:, c * 4 * W:(c + 1) * 4 * W], 0.0).then_inc(acc_zero, 1)

        def setup_vector(v):
            ch = Chain(v, dve)
            v.wait_ge(iota_done, 1)
            ch.mark(nc.vector.tensor_copy(iota_f[:], iota_i[:]))
            for b in range(BLOCKS):
                if b % 16 == 0:
                    v.wait_ge(x_in[b // 16], 16)
                ch.mark(nc.vector.bn_stats(stats[:, b, :], accT[:, b * P:(b + 1) * P]))
            ch.sync()
            for b in range(BLOCKS):
                ch.mark(nc.vector.bn_aggr(mv[:, b, :], stats[:, b, :]))
            ch.sync()
            ch.mark(nc.vector.tensor_scalar(vpe[:], mv[:, :, 1], EPS, None, ALU.add))
            rsqrt_steps(nc, ch, vpe[:], rstd[:], tmp[:])
            ch.sync()
            nc.vector.scalar_tensor_tensor(out=shift0[:], in0=mv[:, :, 0], scalar=-1.0, in1=rstd[:],
                                           op0=ALU.mult, op1=ALU.mult).then_inc(stats_ready, 1)
            for b in range(SHARE):
                ins = nc.vector.tensor_scalar(g0[:, b, :], accT[:, b * P:(b + 1) * P], mv[:, b, 0:1],
                                              rstd[:, b:b + 1], ALU.subtract, ALU.mult)
                if b % BPP == BPP - 1:
                    ins.then_inc(n0_ready, 1)
            v.wait_ge(n0_ready, SHARE // BPP)
            v.wait_ge(n0_ready_act, PANELS - SHARE // BPP)
            nc.vector.memset(g0[:, :, P - 1:P], 1.0).then_inc(g0_done, 1)
            v.wait_ge(smallH_done, 2)
            ch.mark(nc.vector.tensor_tensor(routerHL[:, E:], router[:], routerHL[:, 0:E].bitcast(F32), ALU.subtract))
            ch.mark(nc.vector.tensor_tensor(gateHL[:, E:], gate[:], gateHL[:, 0:E].bitcast(F32), ALU.subtract))
            v.wait_ge(small_in, 16 * 16)
            ch.mark(nc.vector.tensor_tensor(w_self[:], w_self[:], w_last_self[:], ALU.subtract))
            ch.mark(nc.vector.tensor_tensor(w_nbr[:], w_nbr[:], w_last[:], ALU.subtract))
            ch.mark(nc.vector.tensor_tensor(gate_row[:], gate_row[:], gate_row2[:], ALU.add))
            dve_count[0] = ch.value()

        raw_in = [sem(f"raw_in{s}") for s in range(RING1)]
        hi_done = sem("hi_done")
        lo_done = sem("lo_done")
        split_used = sem("split_used")
        jwH_done = sem("jwH_done")
        jwL_done = sem("jwL_done")
        iwF_done = sem("iwF_done")
        iwH_done = sem("iwH_done")
        iwL_done = sem("iwL_done")
        turned = sem("turned")
        row_tile_done = sem("row_tile_done")
        product_done = sem("product_done")
        product_used = sem("product_used")
        outJ_added = sem("outJ_added")
        outI_added = sem("outI_added")
        acc_step = sem("acc_step")
        rows_kept = sem("rows_kept")
        columns_summed = sem("columns_summed")
        columns_copied = sem("columns_copied")
        PT = bank[0:4]
        OI = bank[4]
        OJ = bank[5:7]
        ES = bank[7]
        MAIN_TILES = PANELS * (2 * PAIRS + 1)
        MAIN_PAIRS = PANELS * PAIRS
        MAIN_RANKS = PANELS * RANKS
        TILES_I = 2 * PAIRS + 1
        USES_I = TILES_I // RING1
        STEPS_I = 2 + 3 * (PAIRS - 1)

        class Pair:

            def __init__(self, i, k):
                self.i, self.k = i, k
                if k <= PAIRS:
                    self.j = (i + k) % PANELS
                    self.q = i * PAIRS + (k - 1)
                    self.r = i * RANKS + (k - 1)
                    self.g = i
                    self.slotA, self.useA = (2 * k - 2) % RING1, i * USES_I + (2 * k - 2) // RING1
                    self.slotB, self.useB = (2 * k - 1) % RING1, i * USES_I + (2 * k - 1) // RING1
                else:
                    self.j = i + k
                    self.q = MAIN_PAIRS + i
                    self.r = MAIN_RANKS + i
                    self.g = PANELS + i
                    n = MAIN_TILES + 2 * i
                    self.slotA, self.useA = n % RING1, n // RING1
                    self.slotB, self.useB = (n + 1) % RING1, (n + 1) // RING1

            @property
            def iw(self):
                return 0 if self.k <= PAIRS else (self.i + 1) % 2

            @property
            def par(self):
                return self.k % 2 if self.k <= PAIRS else self.i % 2

        FAR = [Pair(i, PAIRS + 1) for i in range(PANELS // 2)]

        def next_pair(a):
            if a.k < PAIRS:
                return Pair(a.i, a.k + 1)
            if a.k == PAIRS:
                return Pair(a.i + 1, 1)
            return FAR[a.i + 1]

        with nc.Block() as block:
            @block.sync
            def _(sp):
                setup_sync(sp)

                def released(i, m):
                    if isinstance(i, int) and i == PANELS:
                        if m < RING1:
                            i, prev = PANELS - 1, m + TILES_I - RING1
                        else:
                            rank = MAIN_RANKS + (m - RING1) // 2
                            odd = (m - RING1) % 2
                            return rank, odd, not odd
                    elif m >= RING1:
                        prev = m - RING1
                    else:
                        prev = m + TILES_I - RING1
                        rank = i * RANKS + (prev // 2 - RANKS)
                        return (rank, True, True) if prev == TILES_I - 1 else (rank, prev % 2, not prev % 2)
                    rank = i * RANKS + prev // 2
                    return (rank, True, True) if prev == TILES_I - 1 else (rank, prev % 2, not prev % 2)

                def load(i, m, slot, col_panel, row_panel):
                    rank, by_pe, by_dve = released(i, m)
                    if by_pe:
                        sp.wait_ge(row_tile_done, rank + 1 + RANKS)
                    if by_dve:
                        sp.wait_ge(product_done, rank * 4 + 4 + 4 * RANKS)
                    sp.dma_start(raw[:, slot, :], adj_tile(col_panel, row_panel)).then_inc(raw_in[slot], 16)

                with sp.Fori(0, PANELS) as i:
                    for k in range(1, PAIRS + 1):
                        a = Pair(i, k)
                        load(i, 2 * k - 2, a.slotA, a.i, a.j)
                        load(i, 2 * k - 1, a.slotB, a.j, a.i)
                    load(i, TILES_I - 1, RING1 - 1, i, i)
                for a in FAR:
                    load(PANELS, 2 * a.i, a.slotA, a.i, a.j)
                    load(PANELS, 2 * a.i + 1, a.slotB, a.j, a.i)

            @block.scalar
            def _(act):
                act.sem_inc(columns_copied, 1)

                def weights_j(a):
                    act.wait_ge(split_used, a.q * 3 + (2 if a.k == 1 else -1))
                    nc.scalar.activation(jwH[:, a.par, :], g0_flat(a.j, 0, W), ACT.Copy).then_inc(jwH_done, 1)

                def weights_i(a):
                    act.wait_ge(row_tile_done, (a.r - (1 if a.k <= PAIRS else 2)) + 1 + RANKS)
                    nc.scalar.activation(iwF[:, a.iw, :], g0_flat(a.i, 0, W), ACT.Copy).then_inc(iwF_done, 1)
                    nc.scalar.activation(iwH[:, a.iw, :], g0_flat(a.i, 0, W // 2), ACT.Copy).then_inc(iwH_done, 1)

                def g0_flat(panel, start, n):
                    return g0[:].rearrange("p b d -> p (b d)")[:, bass.ds(panel * W + start, n)]

                def split(a):
                    for u, (slot, use, half) in enumerate(((a.slotA, a.useA, 0), (a.slotA, a.useA, 1),
                                                           (a.slotB, a.useB, 0))):
                        act.wait_ge(raw_in[slot], (use + 1) * 16)
                        act.wait_ge(split_used, a.q * 3 + (u + 1))
                        nc.scalar.activation(hi[:, u, :], raw[:, slot, half * HALF:(half + 1) * HALF], ACT.Copy
                                             ).then_inc(hi_done, 1)

                def column_sums(a, flush, dst):
                    act.wait_ge(columns_summed, flush + 1)
                    nc.scalar.activation(dst, ES[:, 0:BPP], ACT.Copy).then_inc(columns_copied, 1)

                setup_scalar(act, lambda: split(Pair(0, 1)))
                act.wait_ge(g0_done, 1)
                with act.Fori(0, PANELS) as i:
                    weights_j(Pair(i, 1))
                    weights_i(Pair(i, 1))
                    for k in range(1, PAIRS + 1):
                        a = Pair(i, k)
                        if k < PAIRS:
                            weights_j(next_pair(a))
                        split(next_pair(a))
                        if k == 1:
                            column_sums(a, i, e_cols[:, bass.ds(i * BPP, BPP)])
                weights_j(FAR[0])
                weights_i(FAR[0])
                column_sums(None, PANELS, e_cols[:, PANELS * BPP:(PANELS + 1) * BPP])
                for a in FAR:
                    if a.i + 1 < len(FAR):
                        weights_j(next_pair(a))
                        weights_i(next_pair(a))
                        split(next_pair(a))
                    if a.i >= 1:
                        column_sums(a, PANELS + a.i, e_cols8[:, (a.i - 1) * BPP:a.i * BPP])
                column_sums(None, PANELS + len(FAR), e_cols8[:, (len(FAR) - 1) * BPP:len(FAR) * BPP])

            @block.gpsimd
            def _(pool):
                setup_gpsimd(pool)
                nc.gpsimd.memset(accP[:], 0.0).then_inc(product_used, 1)

                def weights_j(a):
                    pool.wait_ge(jwH_done, a.q + 1)
                    nc.gpsimd.tensor_tensor(jwL[:, a.par, :], g0[:].rearrange("p b d -> p (b d)")[:, bass.ds(a.j * W, W)],
                                            jwH[:, a.par, :].bitcast(F32), ALU.subtract).then_inc(jwL_done, 1)

                def weights_i(a):
                    pool.wait_ge(iwH_done, a.g + 1)
                    nc.gpsimd.tensor_tensor(iwL[:, a.iw, :],
                                            g0[:].rearrange("p b d -> p (b d)")[:, bass.ds(a.i * W, W // 2)],
                                            iwH[:, a.iw, :].bitcast(F32), ALU.subtract).then_inc(iwL_done, 1)

                def add_products(par, base, fresh):
                    if fresh:
                        nc.gpsimd.tensor_tensor(accP[:], prod[:, par, 0:W], prod[:, par, W:2 * W], ALU.add
                                                ).then_inc(acc_step, 1)
                    else:
                        for m in range(2):
                            if m:
                                pool.wait_ge(acc_step, base + 1)
                            nc.gpsimd.tensor_tensor(accP[:], accP[:], prod[:, par, m * W:(m + 1) * W], ALU.add
                                                    ).then_inc(acc_step, 1)
                    steps = 1 if fresh else 2
                    pool.wait_ge(acc_step, base + steps)
                    nc.gpsimd.tensor_tensor(accP[:], accP[:], prod[:, par, 2 * W:3 * W], ALU.add).then_inc(acc_step, 1)
                    pool.wait_ge(acc_step, base + (steps + 1))
                    nc.gpsimd.tensor_tensor(accP[:], accP[:], prod[:, par, 3 * W:], ALU.add).then_inc(product_used, 1)

                with pool.Fori(0, PANELS) as i:
                    weights_j(Pair(i, 1))
                    weights_i(Pair(i, 1))
                    for k in range(1, PAIRS + 1):
                        a = Pair(i, k)
                        if k < PAIRS:
                            weights_j(next_pair(a))
                        pool.wait_ge(product_done, a.r * 4 + 4 + 4 * RANKS)
                        if k == 1:
                            pool.wait_ge(columns_summed, i + 1)
                            add_products(a.par, i * STEPS_I, True)
                        else:
                            pool.wait_ge(product_used, a.q + 1)
                            add_products(a.par, i * STEPS_I + (2 + 3 * (k - 2)), False)
                weights_j(FAR[0])
                weights_i(FAR[0])
                for a in FAR:
                    if a.i + 1 < len(FAR):
                        weights_j(next_pair(a))
                        weights_i(next_pair(a))
                    pool.wait_ge(product_done, a.r * 4 + 4 + 4 * RANKS)
                    pool.wait_ge(columns_summed, PANELS + 1 + a.i)
                    add_products(a.par, PANELS * STEPS_I + 2 * a.i, True)

            @block.vector
            def _(v):
                v.sem_inc(product_done, 4 * RANKS)
                v.sem_inc(outJ_added, 1)
                v.sem_inc(outI_added, 1)
                setup_vector(v)

                def products(r, k, j, tile, par):
                    for m in range(BPP):
                        v.wait_ge(turned, r * 4 + m + 1)
                        nc.vector.tensor_tensor_reduce(
                            prod[:, par, m * W:(m + 1) * W], PT[m][:], tile[:, m * W:(m + 1) * W], 1.0, 0.0,
                            ALU.mult, ALU.add, row_sums[:, par, m:m + 1]).then_inc(product_done, 1)

                def keep_rows(r, k, j, par):
                    v.wait_ge(product_done, r * 4 + 4 + 4 * RANKS)
                    nc.vector.tensor_copy(e_rows[:, bass.ds(j * BPP + k * BLOCKS, BPP)], row_sums[:, par, :]
                                          ).then_inc(rows_kept, 1)

                def split(a):
                    for u, (slot, half) in enumerate(((a.slotA, 0), (a.slotA, 1), (a.slotB, 0))):
                        v.wait_ge(hi_done, a.q * 3 + (u + 1))
                        nc.vector.tensor_tensor(lo[:, u, :], raw[:, slot, half * HALF:(half + 1) * HALF],
                                                hi[:, u, :].bitcast(F32), ALU.subtract).then_inc(lo_done, 1)

                def add_j(a):
                    v.wait_ge(row_tile_done, a.r + 1 + RANKS)
                    v.wait_ge(outJ_added, a.q + 1)
                    v.wait_ge(outI_added, a.g + 1)
                    dst = accT[:, bass.ds(a.j * W, W)]
                    nc.vector.tensor_tensor(dst, OJ[a.par][:], dst, ALU.add).then_inc(outJ_added, 1)

                def add_i(i, g, q_end):
                    v.wait_ge(outJ_added, q_end + 1)
                    dst = accT[:, bass.ds(i * W, W)]
                    nc.vector.tensor_tensor(dst, OI[:], dst, ALU.add).then_inc(outI_added, 1)

                split(Pair(0, 1))
                v.wait_ge(acc_zero, 4)
                v.wait_ge(consts_done, 5)
                with v.Fori(0, PANELS) as i:
                    for k in range(1, PAIRS + 1):
                        a = Pair(i, k)
                        v.wait_ge(product_used, a.q + (1 if k == 1 else 0))
                        products(a.r, k, a.j, raw[:, a.slotA, :], a.par)
                        split(next_pair(a))
                        keep_rows(a.r, k, a.j, a.par)
                        add_j(a)
                    v.wait_ge(product_used, i * PAIRS + PAIRS)
                    products(i * RANKS + PAIRS, 0, i, raw[:, RING1 - 1, :], 0)
                    keep_rows(i * RANKS + PAIRS, 0, i, 0)
                    v.wait_ge(row_tile_done, i * RANKS + RANKS + RANKS)
                    add_i(i, i, i * PAIRS + PAIRS)
                for a in FAR:
                    if a.i < 2:
                        v.wait_ge(product_used, MAIN_PAIRS + 1)
                    else:
                        v.wait_ge(product_used, MAIN_PAIRS + 1 + (a.i - 2) + 1)
                    v.wait_ge(rows_kept, a.r)
                    products(a.r, a.k, a.j, raw[:, a.slotA, :], a.par)
                    if a.i + 1 < len(FAR):
                        split(next_pair(a))
                    keep_rows(a.r, a.k, a.j, a.par)
                    add_j(a)
                    add_i(a.i, a.g, a.q + 1)

            @block.tensor
            def _(pe):
                pe.sem_inc(split_used, 3)
                pe.sem_inc(row_tile_done, RANKS)

                def turn(r, slot, use):
                    pe.wait_ge(raw_in[slot], (use + 1) * 16)
                    for m in range(BPP):
                        pe.wait_ge(product_done, r * 4 + (4 * RANKS - 4 + m + 1))
                        for b in range(BPP):
                            last = nc.tensor.transpose(PT[m][:, b * P:(b + 1) * P],
                                                       raw[:, slot, b * W + m * P:b * W + (m + 1) * P], ident[:])
                        last.then_inc(turned, 1)

                def split_half(dst, wh, wl, first_block, unit, start, stop):
                    for b in range(2):
                        blk = slice((first_block + b) * P, (first_block + b + 1) * P)
                        cols = slice(b * W, (b + 1) * W)
                        nc.tensor.matmul(dst[:], wh[:, blk], hi[:, unit, cols], start=start and b == 0, stop=False)
                        nc.tensor.matmul(dst[:], wh[:, blk], lo[:, unit, cols], start=False, stop=False)
                        last = nc.tensor.matmul(dst[:], wl[:, blk], hi[:, unit, cols], start=False,
                                                stop=stop and b == 1)
                    last.then_inc(split_used, 1)

                def plain(dst, iw, slot, blocks, start, stop):
                    for b in blocks:
                        last = nc.tensor.matmul(dst[:], iwF[:, iw, b * P:(b + 1) * P], raw[:, slot, b * W:(b + 1) * W],
                                                start=start and b == blocks[0], stop=stop and b == blocks[-1])
                    last.then_inc(row_tile_done, 1)

                def pair(a, only):
                    turn(a.r, a.slotB, a.useB)
                    pe.wait_ge(jwL_done, a.q + 1)
                    if a.k == 1 or only:
                        pe.wait_ge(outI_added, a.g + 1)
                    for u in range(2):
                        pe.wait_ge(lo_done, a.q * 3 + (u + 1))
                        split_half(OI, jwH[:, a.par, :], jwL[:, a.par, :], 2 * u, u, (a.k == 1 or only) and u == 0,
                                   only and u == 1)
                    pe.wait_ge(iwL_done, a.g + 1)
                    pe.wait_ge(iwF_done, a.g + 1)
                    pe.wait_ge(outJ_added, a.q + (1 if a.k == 1 else 0))
                    pe.wait_ge(lo_done, a.q * 3 + 3)
                    split_half(OJ[a.par], iwH[:, a.iw, :], iwL[:, a.iw, :], 0, 2, True, False)
                    plain(OJ[a.par], a.iw, a.slotB, [2, 3], False, True)

                def sum_columns(flush):
                    pe.wait_ge(columns_copied, flush + 1)
                    for c in range(BPP):
                        last = nc.tensor.matmul(ES[:, c:c + 1], accP[:, c * P:(c + 1) * P], ones[:, 0:1],
                                                start=True, stop=True)
                    last.then_inc(columns_summed, 1)

                pe.wait_ge(consts_done, 5)
                with pe.Fori(0, PANELS) as i:
                    for k in range(1, PAIRS + 1):
                        a = Pair(i, k)
                        pair(a, False)
                        if k == 1:
                            pe.wait_ge(product_used, i * PAIRS + 1)
                            sum_columns(i)
                    turn(i * RANKS + PAIRS, RING1 - 1, i * USES_I + USES_I - 1)
                    plain(OI, 0, RING1 - 1, [0, 1, 2, 3], False, True)
                pe.wait_ge(product_used, MAIN_PAIRS + 1)
                sum_columns(PANELS)
                for a in FAR:
                    pair(a, True)
                    if a.i >= 1:
                        pe.wait_ge(product_used, MAIN_PAIRS + 1 + a.i)
                        sum_columns(PANELS + a.i)
                pe.wait_ge(product_used, MAIN_PAIRS + 1 + len(FAR))
                sum_columns(PANELS + len(FAR))

        x_again = [sem(f"x_again{s}") for s in range(4)]
        x_biased = sem("x_biased")
        g0_turned = sem("g0_turned")
        nTa_ready = sem("nTa_ready")
        nbr_done = sem("nbr_done")
        sums_out = sem("sums_out")
        sums_in = sem("sums_in")
        sums_turned = sem("sums_turned")
        x1_summed = sem("x1_summed")
        n1_ready = sem("n1_ready")
        n1_turned = sem("n1_turned")
        n1H_done = sem("n1H_done")
        n1L_done = sem("n1L_done")
        xn_done = sem("xn_done")
        logits_done = sem("logits_done")
        shifted = sem("shifted")
        exp_done = sem("exp_done")
        root_in = sem("root_in")
        root_done = sem("root_done")
        c_ready = sem("c_ready")
        c_turned = sem("c_turned")
        ct_ready = sem("ct_ready")
        c_out = sem("c_out")
        stage_in = sem("stage_in")
        LAG = 2

        def bcast(col, n=BLOCKS, m=E):
            return col.to_broadcast([P, n, m])

        with nc.Block() as block:
            @block.sync
            def _(sp):
                for p in range(PANELS):
                    if p >= 4:
                        sp.wait_ge(x1_summed, p - 3)
                    sp.dma_start(bt[:, p % 4, :].rearrange("p (b d) -> p b d", d=P), rows(x, p)
                                 ).then_inc(x_again[p % 4], 16)
                sp.dma_start(sums_dram.rearrange("(o b) t -> o (b t)", o=1), accT[P - 1:P, :]).then_inc(sums_out, 16)
                sp.wait_ge(sums_out, 16)
                sp.dma_start(sums_by_block[:], sums_dram).then_inc(sums_in, 16)
                sp.wait_ge(weights_done, 2)
                sp.dma_start(stage[:].rearrange("p s n -> p (s n)").rearrange("p (e h) -> p e h", e=E),
                             w1_1.rearrange("e k h -> k e h")).then_inc(stage_in, 16)
                sp.wait_ge(ct_ready, 1)
                sp.dma_start(c0_dram.rearrange("(g q) t -> q g t", q=P), cwT[:].rearrange("q (g t) -> q g t", t=P)
                             ).then_inc(c_out, 16)
                sp.wait_ge(c_out, 16)

            @block.scalar
            def _(act):
                for p in range(PANELS):
                    act.wait_ge(g0_turned, p + 1)
                    if p >= 2:
                        act.wait_ge(nbr_done, p - 1)
                    nc.scalar.activation(nTa[:, p % 2, :], bank[4 + p % 2][:], ACT.Copy).then_inc(nTa_ready, 1)
                act.wait_ge(experts_in, 32)
                for s, wh in enumerate((w1H0, w2H0)):
                    nc.scalar.activation(wh[:].rearrange("p e n -> p (e n)"), stage[:, s, :], ACT.Copy
                                         ).then_inc(weightsH_done, 1)
                act.wait_ge(root_in, 1)
                nc.scalar.activation(dinv[:], rowsum[:], ACT.Sqrt).then_inc(root_done, 1)
                for p in range(PANELS):
                    act.wait_ge(n1_turned, p + 1)
                    nc.scalar.activation(n1H[:, p * W:(p + 1) * W], bank[2 + p % 4][:], ACT.Copy).then_inc(n1H_done, 1)
                act.wait_ge(shifted, 1)
                nc.scalar.activation(pr[:], pr[:], ACT.Exp).then_inc(exp_done, 1)
                act.wait_ge(c_turned, 1)
                nc.scalar.activation(cwT[:], bank[7][:], ACT.Copy).then_inc(ct_ready, 1)

            @block.gpsimd
            def _(pool):
                for p in range(PANELS):
                    pool.wait_ge(x_again[p % 4], 16 * (p // 4 + 1))
                    panel = bt[:, p % 4, :].rearrange("p (b d) -> p b d", d=P)
                    nc.gpsimd.tensor_tensor(panel, panel, bias0[:].unsqueeze(1).to_broadcast([P, BPP, P]), ALU.add
                                            ).then_inc(x_biased, 1)
                for s, (wh, wl) in enumerate(((w1H0, w1L0), (w2H0, w2L0))):
                    pool.wait_ge(weightsH_done, s + 1)
                    nc.gpsimd.tensor_tensor(wl[:].rearrange("p e n -> p (e n)"), stage[:, s, :],
                                            wh[:].rearrange("p e n -> p (e n)").bitcast(F32), ALU.subtract
                                            ).then_inc(weights_done, 1)
                for p in range(PANELS):
                    pool.wait_ge(n1_ready, p + 1)
                    panel = xn[:, p * BPP:(p + 1) * BPP, :].rearrange("p b d -> p (b d)")
                    nc.gpsimd.tensor_tensor(panel, panel, nb[:, p % 4, :], ALU.add).then_inc(xn_done, 1)

            @block.vector
            def _(v):
                ch = Chain(v, dve, dve_count[0])
                ch.mark(nc.vector.tensor_reduce(e_sum[:], e_rows[:].rearrange("p (k b) -> p b k", b=BLOCKS), AX_X, ALU.add))
                ch.sync()
                ch.mark(nc.vector.tensor_tensor(e_sum[:], e_sum[:], e_cols[:, BPP:], ALU.add))
                ch.sync()
                ch.mark(nc.vector.tensor_tensor(e_sum[:, 0:BLOCKS // 2], e_sum[:, 0:BLOCKS // 2], e_cols8[:], ALU.add))
                for p in range(PANELS + 1):
                    if p < PANELS:
                        v.wait_ge(x_biased, p + 1)
                        v.wait_ge(nbr_done, p + 1)
                        panel = xn[:, p * BPP:(p + 1) * BPP, :].rearrange("p b d -> p (b d)")
                        nc.vector.tensor_tensor(panel, bank[p % 2][:], bt[:, p % 4, :], ALU.add).then_inc(x1_summed, 1)
                    if p >= 1:
                        q = p - 1
                        v.wait_ge(x1_summed, q + 1)
                        if q == 0:
                            ch.sync()
                        for b in range(q * BPP, (q + 1) * BPP):
                            ch.mark(nc.vector.scalar_tensor_tensor(out=xn[:, b, :], in0=w_edge[:],
                                                                   scalar=e_sum[:, b:b + 1], in1=xn[:, b, :],
                                                                   op0=ALU.mult, op1=ALU.add))
                        ch.sync()
                        for b in range(q * BPP, (q + 1) * BPP):
                            ch.mark(nc.vector.bn_stats(stats2[:, b, :], xn[:, b, :]))
                ch.sync()
                v.wait_ge(sums_turned, 1)
                nc.vector.tensor_scalar(rowsum[:], bank[7][:, 0:BLOCKS], 1.0, None, ALU.add).then_inc(root_in, 1)
                for b in range(BLOCKS):
                    ch.mark(nc.vector.bn_aggr(mv[:, b, :], stats2[:, b, :]))
                ch.sync()
                ch.mark(nc.vector.tensor_scalar(vpe[:], mv[:, :, 1], EPS, None, ALU.add))
                rsqrt_steps(nc, ch, vpe[:], rstd[:], tmp[:])
                ch.sync()
                for p in range(PANELS + LAG):
                    if p < PANELS:
                        if p >= 4:
                            v.wait_ge(n1_turned, p - 3)
                            v.wait_ge(xn_done, p - 3)
                        for b in range(BPP):
                            blk = p * BPP + b
                            ins = nc.vector.tensor_scalar(nb[:, p % 4, b * P:(b + 1) * P], xn[:, blk, :],
                                                          mv[:, blk, 0:1], rstd[:, blk:blk + 1],
                                                          ALU.subtract, ALU.mult)
                        ins.then_inc(n1_ready, 1)
                    if p >= LAG:
                        q = p - LAG
                        v.wait_ge(n1H_done, q + 1)
                        nc.vector.tensor_tensor(n1L[:, q * W:(q + 1) * W], bank[2 + q % 4][:],
                                                n1H[:, q * W:(q + 1) * W].bitcast(F32), ALU.subtract
                                                ).then_inc(n1L_done, 1)
                v.wait_ge(root_done, 1)
                ch.mark(nc.vector.reciprocal(dinv[:], dinv[:]))
                newton_step(nc, ch, rowsum[:], dinv[:], tmp[:])
                v.wait_ge(logits_done, PANELS)
                for half in range(2):
                    blocks = lg[:, half * BLOCKS // 2:(half + 1) * BLOCKS // 2, :]
                    parts = bank[6 + half][:].rearrange("p (b s e) -> p b s e", s=2, e=E)
                    ch.mark(nc.vector.tensor_copy(blocks, parts[:, :, 0, :]))
                    ch.sync()
                    ch.mark(nc.vector.tensor_tensor(blocks, blocks, parts[:, :, 1, :], ALU.add))
                ch.sync()
                for b in range(BLOCKS):
                    ch.mark(nc.vector.max(mx[:, b, :], lg[:, b, :]))
                ch.sync()
                for b in range(BLOCKS):
                    ch.mark(nc.vector.max_index(ix[:, b, :], mx[:, b, :], lg[:, b, :]))
                nc.vector.tensor_tensor(pr[:], lg[:], bcast(mx[:, :, 0:1]), ALU.subtract).then_inc(shifted, 1)
                ch.sync()
                v.wait_ge(shifted, 1)
                ch.mark(nc.vector.tensor_copy(mx[:, :, 0:2], ix[:, :, 0:2]))
                ch.sync()
                iota3 = iota_f[:].unsqueeze(1).to_broadcast([P, BLOCKS, E])
                ch.mark(nc.vector.tensor_tensor(lg[:], iota3, bcast(mx[:, :, 0:1]), ALU.is_equal))
                ch.mark(nc.vector.tensor_tensor(cw[:], iota3, bcast(mx[:, :, 1:2]), ALU.is_equal))
                ch.sync()
                ch.mark(nc.vector.tensor_tensor(cw[:], cw[:], lg[:], ALU.add))
                v.wait_ge(exp_done, 1)
                ch.mark(nc.vector.tensor_reduce(vpe[:], pr[:], AX_X, ALU.add))
                ch.sync()
                ch.mark(nc.vector.reciprocal(vpe[:], vpe[:]))
                ch.sync()
                ch.mark(nc.vector.tensor_tensor(pr[:], pr[:], bcast(vpe[:].unsqueeze(2)), ALU.mult))
                ch.sync()
                ch.mark(nc.vector.tensor_tensor(cw[:], cw[:], pr[:], ALU.mult))
                ch.sync()
                ch.mark(nc.vector.tensor_reduce(tmp[:], cw[:], AX_X, ALU.add))
                ch.sync()
                ch.mark(nc.vector.tensor_scalar(tmp[:], tmp[:], 1e-12, None, ALU.max))
                ch.sync()
                ch.mark(nc.vector.reciprocal(tmp[:], tmp[:]))
                ch.sync()
                nc.vector.tensor_tensor(cw[:], cw[:], bcast(tmp[:].unsqueeze(2)), ALU.mult).then_inc(c_ready, 1)
                dve_count[0] = ch.value()

            @block.tensor
            def _(pe):
                for p in range(PANELS + 1):
                    if p < PANELS:
                        if p >= 2:
                            pe.wait_ge(nTa_ready, p - 1)
                        for b in range(BPP):
                            last = nc.tensor.transpose(bank[4 + p % 2][:, b * P:(b + 1) * P], g0[:, p * BPP + b, :],
                                                       ident[:])
                        last.then_inc(g0_turned, 1)
                    if p >= 1:
                        q = p - 1
                        pe.wait_ge(nTa_ready, q + 1)
                        if q >= 2:
                            pe.wait_ge(x1_summed, q - 1)
                        for b in range(BPP):
                            blk = q * BPP + b
                            agg = accT[:, blk * P:(blk + 1) * P]
                            dst = bank[q % 2][:, b * P:(b + 1) * P]
                            nc.tensor.matmul(dst, agg, w_nbr[:], start=True, stop=False)
                            last = nc.tensor.matmul(dst, nTa[:, q % 2, b * P:(b + 1) * P], w_self[:],
                                                    start=False, stop=True)
                        last.then_inc(nbr_done, 1)
                pe.wait_ge(sums_in, 16)
                nc.tensor.transpose(bank[7][:, 0:BLOCKS], sums_by_block[:], ident[0:BLOCKS, 0:BLOCKS]
                                    ).then_inc(sums_turned, 1)
                for p in range(PANELS + LAG):
                    if p < PANELS:
                        pe.wait_ge(n1_ready, p + 1)
                        if p >= 4:
                            pe.wait_ge(n1L_done, p - 3)
                        for b in range(BPP):
                            last = nc.tensor.transpose(bank[2 + p % 4][:, b * P:(b + 1) * P],
                                                       nb[:, p % 4, b * P:(b + 1) * P], ident[:])
                        last.then_inc(n1_turned, 1)
                    if p >= LAG:
                        q = p - LAG
                        pe.wait_ge(n1L_done, q + 1)
                        for blk in range(q * BPP, (q + 1) * BPP):
                            cols = slice(blk * P, (blk + 1) * P)
                            at = blk % (BLOCKS // 2) * 2 * E
                            dst = bank[6 + blk // (BLOCKS // 2)]
                            nc.tensor.matmul(dst[:, at:at + 2 * E], n1H[:, cols], routerHL[:], start=True, stop=False)
                            last = nc.tensor.matmul(dst[:, at:at + E], n1L[:, cols], routerHL[:, 0:E],
                                                    start=False, stop=True)
                        last.then_inc(logits_done, 1)
                pe.wait_ge(c_ready, 1)
                for g in range(BLOCKS * E // P):
                    last = nc.tensor.transpose(bank[7][:, g * P:(g + 1) * P],
                                               cw[:].rearrange("p b e -> p (b e)")[:, g * P:(g + 1) * P], ident[:])
                last.then_inc(c_turned, 1)

        W1RAW = stage[:].rearrange("p s n -> p (s n)")
        stageH_done = sem("stageH_done")
        stageL_done = sem("stageL_done")
        cb_in = [sem(f"cb_in{s}") for s in range(E)]
        ct_in = sem("ct_in")
        z_done = sem("z_done")
        gelu_done = sem("gelu_done")
        scaled = sem("scaled")
        hH_done = sem("hH_done")
        hL_done = sem("hL_done")
        y_done = sem("y_done")
        y_copied = sem("y_copied")
        yt_turned = sem("yt_turned")
        x2_summed = sem("x2_summed")
        stats3_done = sem("stats3_done")
        ZB = bank[0:4]
        YB = bank[4:6]
        TB = bank[6:8]

        with nc.Block() as block:
            @block.sync
            def _(sp):
                def panel(p):
                    c = c0_dram[bass.ds(p * BPP * E, BPP * E), :].rearrange("(b e) t -> e b t", e=E)
                    sp.wait_ge(y_done, p * E + 1)
                    sp.dma_start(ct0[:].rearrange("e (b t) -> e b t", b=BPP), c).then_inc(ct_in, 16)
                    for e in range(E):
                        sp.wait_ge(scaled, p * E + (e + 1))
                        sp.dma_start(cb0[:, e, :].rearrange("p (b t) -> p b t", b=BPP),
                                     c[e].partition_broadcast(P)).then_inc(cb_in[e], 16)

                with sp.Fori(0, PANELS) as p:
                    panel(p)
                sp.wait_ge(stageL_done, 1)
                sp.dma_start(W1RAW.rearrange("p (e q d) -> p e q d", e=E, q=2),
                             w2_1.rearrange("e (q h) d -> h e q d", q=2)).then_inc(stage_in, 16)

            @block.scalar
            def _(act):
                act.wait_ge(stage_in, 16)
                nc.scalar.activation(w1H1[:], W1RAW, ACT.Copy).then_inc(stageH_done, 1)

                def gelu(p, e):
                    act.wait_ge(z_done, p * E + (e + 1))
                    act.wait_ge(hL_done, p * E + (e + 1))
                    nc.scalar.activation(h0[:, e, :], ZB[e % 4][:], ACT.Gelu, bias=b1s0[:, e:e + 1]
                                         ).then_inc(gelu_done, 1)

                def round_h(p, e):
                    act.wait_ge(scaled, p * E + (e + 9))
                    act.wait_ge(y_done, p * E + (e + 7))
                    nc.scalar.activation(hH0[:, e % 2, :], h0[:, e, :], ACT.Copy).then_inc(hH_done, 1)

                def y_out(p, odd, step):
                    act.wait_ge(y_done, p * E + 16)
                    if not (isinstance(step, int) and step < 2):
                        act.wait_ge(yt_turned, step - 1)
                    nc.scalar.activation(yTa[:], YB[odd][:], ACT.Copy).then_inc(y_copied, 1)

                def panel(p, odd, first=False, last=False):
                    for e in range(E):
                        round_h(p, e)
                        if e < E - 3:
                            gelu(p, e + 3)
                        elif not last:
                            gelu(p + 1, e + 3 - E)
                        if e == 1 and not first:
                            y_out(p - 1, 1 - odd, p)

                act.sem_inc(gelu_done, 4)
                act.sem_inc(y_copied, 1)
                gelu(0, 0)
                gelu(0, 1)
                gelu(0, 2)
                panel(0, 0, first=True)
                panel(1, 1)
                panel(2, 0)
                with act.Fori(1, PANELS // 2 - 1) as g:
                    panel(g * 2 + 1, 1)
                    panel(g * 2 + 2, 0)
                panel(PANELS - 1, 1, last=True)
                y_out(PANELS - 1, 1, PANELS)
                act.wait_ge(stage_in, 32)
                nc.scalar.activation(w2H1[:], W1RAW, ACT.Copy).then_inc(stageH_done, 1)

            @block.gpsimd
            def _(pool):
                pool.sem_inc(scaled, 8)
                with pool.Fori(0, PANELS) as p:
                    for e in range(E):
                        pool.wait_ge(gelu_done, p * E + (e + 5))
                        pool.wait_ge(cb_in[e], p * 16 + 16)
                        nc.gpsimd.tensor_tensor(h0[:, e, :], h0[:, e, :], cb0[:, e, :], ALU.mult
                                                ).then_inc(scaled, 1)

            @block.vector
            def _(v):
                v.sem_inc(hL_done, 8)
                v.wait_ge(stageH_done, 1)
                nc.vector.tensor_tensor(w1L1[:], W1RAW, w1H1[:].bitcast(F32), ALU.subtract).then_inc(stageL_done, 1)

                def rows2(p, odd, turned):
                    v.wait_ge(yt_turned, turned)
                    panel = xn[:, bass.ds(p * BPP, BPP), :].rearrange("p b d -> p (b d)")
                    nc.vector.tensor_tensor(panel, TB[odd][:], panel, ALU.add).then_inc(x2_summed, 1)

                def stats_rows2(p, turned):
                    v.wait_ge(x2_summed, turned)
                    hold(nc.vector, scrap_v[:])
                    for b in range(BPP):
                        ins = nc.vector.bn_stats(stats3[:, bass.ds(p * BPP + b, 1), :].rearrange("p b s -> p (b s)"),
                                                 xn[:, bass.ds(p * BPP + b, 1), :].rearrange("p b d -> p (b d)"))
                    ins.then_inc(stats3_done, 1)

                def panel(p, odd, first=False):
                    for e in range(E):
                        v.wait_ge(hH_done, p * E + (e + 1))
                        nc.vector.tensor_tensor(hL0[:, e % 2, :], h0[:, e, :], hH0[:, e % 2, :].bitcast(F32),
                                                ALU.subtract).then_inc(hL_done, 1)
                        if e == 5 and not first:
                            rows2(p - 1, 1 - odd, p)
                        if e == 6 and not first:
                            stats_rows2(p - 1, p)

                panel(0, 0, first=True)
                with v.Fori(0, PANELS // 2 - 1) as g:
                    panel(g * 2 + 1, 1)
                    panel(g * 2 + 2, 0)
                panel(PANELS - 1, 1)
                rows2(PANELS - 1, 1, PANELS)
                stats_rows2(PANELS - 1, PANELS)
                v.wait_ge(stageH_done, 2)
                nc.vector.tensor_tensor(w2L1[:], W1RAW, w2H1[:].bitcast(F32), ALU.subtract).then_inc(stageL_done, 1)

            @block.tensor
            def _(pe):
                pe.sem_inc(y_done, 8)

                def z(p, e):
                    pe.wait_ge(gelu_done, p * E + (e + 1))
                    cols = bass.ds(p * W, W)
                    nc.tensor.matmul(ZB[e % 4][:], w1H0[:, e, :], n1H[:, cols], start=True, stop=False)
                    nc.tensor.matmul(ZB[e % 4][:], w1H0[:, e, :], n1L[:, cols], start=False, stop=False)
                    nc.tensor.matmul(ZB[e % 4][:], w1L0[:, e, :], n1H[:, cols], start=False, stop=True
                                     ).then_inc(z_done, 1)

                def y(p, e, odd):
                    if e == 0:
                        pe.wait_ge(ct_in, p * 16 + 16)
                        if not (isinstance(p, int) and p == 0):
                            pe.wait_ge(y_copied, p * 1)
                        nc.tensor.matmul(YB[odd][:], b2s0[:], ct0[:], start=True, stop=False)
                    pe.wait_ge(hL_done, p * E + (e + 9))
                    nc.tensor.matmul(YB[odd][:], w2H0[:, e, :], hH0[:, e % 2, :], start=False, stop=False)
                    nc.tensor.matmul(YB[odd][:], w2H0[:, e, :], hL0[:, e % 2, :], start=False, stop=False)
                    nc.tensor.matmul(YB[odd][:], w2L0[:, e, :], hH0[:, e % 2, :], start=False, stop=(e == E - 1)
                                     ).then_inc(y_done, 1)

                def turn_y(odd, step):
                    pe.wait_ge(y_copied, step + 1)
                    if not (isinstance(step, int) and step < 3):
                        pe.wait_ge(x2_summed, step - 2)
                    for b in range(BPP):
                        last = nc.tensor.transpose(TB[odd][:, b * P:(b + 1) * P], yTa[:, b * P:(b + 1) * P],
                                                   ident[:])
                    last.then_inc(yt_turned, 1)

                def panel(p, odd, last=False, first=False):
                    for e in range(E):
                        if e == 4 and not first:
                            turn_y(1 - odd, p)
                        if e + 4 < E:
                            z(p, e + 4)
                        elif not last:
                            z(p + 1, e + 4 - E)
                        y(p, e, odd)

                for e in range(4):
                    z(0, e)
                panel(0, 0, first=True)
                panel(1, 1)
                panel(2, 0)
                with pe.Fori(1, PANELS // 2 - 1) as g:
                    panel(g * 2 + 1, 1)
                    panel(g * 2 + 2, 0)
                panel(PANELS - 1, 1, last=True)
                turn_y(1, PANELS)

        n2_ready = sem("n2_ready")
        xb_biased = sem("xb_biased")
        n2_turned = sem("n2_turned")
        n2T_ready = sem("n2T_ready")
        support_done = sem("support_done")
        g_scaled = sem("g_scaled")
        gH_done = sem("gH_done")
        gL_done = sem("gL_done")
        xb_done = sem("xb_done")
        xb_out = sem("xb_out")
        LAG2 = 3
        raw3_in = [sem(f"raw3_in{s}") for s in range(RING3)]

        with nc.Block() as block:
            @block.sync
            def _(sp):
                sp.wait_ge(stageL_done, 2)
                for t in range(RING3 - 1):
                    sp.dma_start(raw3[:, t, :], adj_tile(0, t)).then_inc(raw3_in[t], 16)
                for p in range(PANELS):
                    sp.wait_ge(xb_done, p + 1)
                    sp.dma_start(rows(xb_dram, p), xn[:, p * BPP:(p + 1) * BPP, :]).then_inc(xb_out, 16)
                sp.wait_ge(xb_out, 16 * PANELS)

            @block.scalar
            def _(act):
                for p in range(PANELS + 1):
                    if p < PANELS:
                        act.wait_ge(n2_turned, p + 1)
                        if p >= 2:
                            act.wait_ge(support_done, p - 1)
                        nc.scalar.activation(nT2[:, p % 2, :], bank[2 + p % 2][:], ACT.Copy).then_inc(n2T_ready, 1)
                    if p >= 1:
                        q = p - 1
                        act.wait_ge(support_done, q + 1)
                        if q >= 4:
                            act.wait_ge(gL_done, q - 3)
                            act.wait_ge(xb_done, q - 3)
                        for b in range(BPP):
                            blk = q * BPP + b
                            ins = nc.scalar.activation(gf[:, q % 4, b * P:(b + 1) * P],
                                                       bank[4 + q % 2][:, b * P:(b + 1) * P], ACT.Copy,
                                                       scale=dinv[:, blk:blk + 1])
                        ins.then_inc(g_scaled, 1)
                        act.wait_ge(g_scaled, q + 1)
                        nc.scalar.activation(gH[:, q * W:(q + 1) * W], gf[:, q % 4, :], ACT.Copy).then_inc(gH_done, 1)

            @block.gpsimd
            def _(pool):
                for p in range(PANELS + 2):
                    if p < PANELS:
                        pool.wait_ge(n2_ready, p + 1)
                        panel = xn[:, p * BPP:(p + 1) * BPP, :]
                        nc.gpsimd.tensor_tensor(panel, panel, bias1[:].unsqueeze(1).to_broadcast([P, BPP, P]), ALU.add
                                                ).then_inc(xb_biased, 1)
                    if p >= 2:
                        q = p - 2
                        pool.wait_ge(gH_done, q + 1)
                        nc.gpsimd.tensor_tensor(gL[:, q * W:(q + 1) * W], gf[:, q % 4, :],
                                                gH[:, q * W:(q + 1) * W].bitcast(F32), ALU.subtract
                                                ).then_inc(gL_done, 1)

            @block.vector
            def _(v):
                ch = Chain(v, dve, dve_count[0])
                v.wait_ge(stats3_done, PANELS)
                for b in range(BLOCKS):
                    ch.mark(nc.vector.bn_aggr(mv[:, b, :], stats3[:, b, :]))
                ch.sync()
                ch.mark(nc.vector.tensor_scalar(vpe[:], mv[:, :, 1], EPS, None, ALU.add))
                rsqrt_steps(nc, ch, vpe[:], rstd[:], tmp[:])
                ch.sync()
                for p in range(PANELS + LAG2):
                    if p < PANELS:
                        if p >= 4:
                            v.wait_ge(n2_turned, p - 3)
                        for b in range(BPP):
                            blk = p * BPP + b
                            ins = nc.vector.tensor_scalar(nb2[:, p % 4, b * P:(b + 1) * P], xn[:, blk, :],
                                                          mv[:, blk, 0:1], rstd[:, blk:blk + 1],
                                                          ALU.subtract, ALU.mult)
                        ins.then_inc(n2_ready, 1)
                    if p >= LAG2:
                        q = p - LAG2
                        v.wait_ge(g_scaled, q + 1)
                        v.wait_ge(xb_biased, q + 1)
                        for b in range(BPP):
                            blk = q * BPP + b
                            ins = nc.vector.scalar_tensor_tensor(out=xn[:, blk, :], in0=gf[:, q % 4, b * P:(b + 1) * P],
                                                                 scalar=dinv[:, blk:blk + 1], in1=xn[:, blk, :],
                                                                 op0=ALU.mult, op1=ALU.add)
                        ins.then_inc(xb_done, 1)
                dve_count[0] = ch.value()

            @block.tensor
            def _(pe):
                for p in range(PANELS + 1):
                    if p < PANELS:
                        pe.wait_ge(n2_ready, p + 1)
                        if p >= 2:
                            pe.wait_ge(n2T_ready, p - 1)
                        for b in range(BPP):
                            last = nc.tensor.transpose(bank[2 + p % 2][:, b * P:(b + 1) * P],
                                                       nb2[:, p % 4, b * P:(b + 1) * P], ident[:])
                        last.then_inc(n2_turned, 1)
                    if p >= 1:
                        q = p - 1
                        pe.wait_ge(n2T_ready, q + 1)
                        if q >= 2:
                            pe.wait_ge(g_scaled, q - 1)
                        for b in range(BPP):
                            last = nc.tensor.matmul(bank[4 + q % 2][:, b * P:(b + 1) * P],
                                                    nT2[:, q % 2, b * P:(b + 1) * P], w_l1[:], start=True, stop=True)
                        last.then_inc(support_done, 1)

        hi3_done = sem("hi3_done")
        lo3_done = sem("lo3_done")
        split3_used = sem("split3_used")
        o_copied = sem("o_copied")
        o_turned = sem("o_turned")
        xb3_in = sem("xb3_in")
        x3_done = sem("x3_done")
        n3_ready = sem("n3_ready")
        n3_turned = sem("n3_turned")
        n3H_done = sem("n3H_done")
        n3L_done = sem("n3L_done")
        logits3_done = sem("logits3_done")
        shifted3 = sem("shifted3")
        exp3_done = sem("exp3_done")
        c3_ready = sem("c3_ready")
        c3_turned = sem("c3_turned")
        ct3_ready = sem("ct3_ready")
        c3_out = sem("c3_out")
        cb3_in = [sem(f"cb3_in{s}") for s in range(4)]
        z3_done = sem("z3_done")
        relu_done = sem("relu_done")
        scaled3 = sem("scaled3")
        hH3_done = sem("hH3_done")
        hL3_done = sem("hL3_done")
        y3_done = sem("y3_done")
        y3_copied = sem("y3_copied")
        y3_turned = sem("y3_turned")
        out_ready = sem("out_ready")
        out_stored = sem("out_stored")
        dve3 = sem("dve3")
        ZB = bank[0:2]
        YB = bank[2:4]
        OG = bank[4:6]
        M1 = bank[6]
        M2 = bank[7]
        S = 2 * E
        CHAIN3 = 38
        LAST = PANELS + 2
        assert S == PANELS

        def chains(p):
            return min(p, PANELS) if isinstance(p, int) else p

        def active(p):
            return dict(tiles=p < PANELS, chain=1 <= p <= PANELS, ffn=2 <= p <= PANELS + 1, fin=3 <= p,
                        ahead=p < PANELS - 1)

        def over_panels(eng, panel):
            for p in range(4):
                panel(p, p % 2, **active(p))
            with eng.Fori(4, PANELS - 2, 2) as p:
                panel(p, 0, **active(4))
                panel(p + 1, 1, **active(5))
            for p in range(PANELS - 2, LAST + 1):
                panel(p, p % 2, **active(p))

        with nc.Block() as block:
            @block.sync
            def _(sp):
                def load_c(c, e):
                    if e == 0:
                        sp.wait_ge(c3_out, (c + 1) * 16)
                    else:
                        sp.wait_ge(scaled3, c * S + (2 * (e - 4) + 2 + 8))
                    sp.dma_start(cb1[:, e % 4, :], c1_dram[bass.ds(c * E + e, 1), :].to_broadcast([P, W])
                                 ).then_inc(cb3_in[e % 4], 16)

                def panel(p, odd, tiles, chain, ffn, fin, ahead):
                    for t in range(PANELS):
                        if tiles and not (isinstance(p, int) and p == 0 and t < RING3 - 1):
                            sp.wait_ge(lo3_done, p * (2 * PANELS) + (2 * t + 2))
                            sp.dma_start(raw3[:, t % RING3, :], adj_tile(p, t)).then_inc(raw3_in[t % RING3], 16)
                        if ffn and t == 1:
                            sp.wait_ge(ct3_ready, p - 1)
                            sp.dma_start(c1_dram[bass.ds((p - 2) * E, E), :], ct1[:]).then_inc(c3_out, 16)
                        if ffn and t == 2:
                            load_c(p - 2, 0)
                        if ffn and t % 2 and t >= 3:
                            load_c(p - 2, (t - 1) // 2)
                        if fin and t == 6:
                            sp.wait_ge(out_ready, p - 2)
                            sp.dma_start(rows(out, p - 3), outb[:].rearrange("p (b d) -> p b d", d=P)
                                         ).then_inc(out_stored, 16)
                        if tiles and t == 12:
                            if not (isinstance(p, int) and p == 0):
                                sp.wait_ge(n3_turned, p * 1)
                            sp.dma_start(xbt[:].rearrange("p (b d) -> p b d", d=P), rows(xb_dram, p)
                                         ).then_inc(xb3_in, 16)

                over_panels(sp, panel)
                sp.wait_ge(out_stored, 16 + 16 * PANELS)

            @block.scalar
            def _(act):
                def split(p, t):
                    for h in range(2):
                        act.wait_ge(raw3_in[t % RING3], (p * 4 + (t // RING3 + 1)) * 16)
                        act.wait_ge(split3_used, p * 32 + (2 * t + h + 1))
                        nc.scalar.activation(hi3[:, (2 * t + h) % 4, :], raw3[:, t % RING3, h * HALF:(h + 1) * HALF],
                                             ACT.Copy).then_inc(hi3_done, 1)

                def relu(c, s):
                    act.wait_ge(z3_done, c * S + (s + 1))
                    act.wait_ge(hL3_done, c * S + (s + 1))
                    nc.scalar.activation(h1[:, s % 4, :], ZB[s % 2][:], ACT.Relu, bias=b1s1[:, s // 2, s % 2:s % 2 + 1]
                                         ).then_inc(relu_done, 1)

                def round_h(c, s):
                    act.wait_ge(scaled3, c * S + (s + 9))
                    act.wait_ge(y3_done, c * S + (s + 1))
                    nc.scalar.activation(hH1[:, s % 2, :], h1[:, s % 4, :], ACT.Copy).then_inc(hH3_done, 1)

                def panel(p, odd, tiles, chain, ffn, fin, ahead):
                    c = p - 1
                    for t in range(PANELS):
                        if chain and t == 8:
                            act.wait_ge(n3_turned, p * 1)
                            nc.scalar.activation(n3H[:, 1 - odd, :], M1[:], ACT.Copy).then_inc(n3H_done, 1)
                        if chain and t == 13:
                            act.wait_ge(c3_turned, p * 1)
                            nc.scalar.activation(ct1[:], M2[0:E, :], ACT.Copy).then_inc(ct3_ready, 1)
                        if tiles and t < PANELS - 1:
                            split(p, t + 1)
                        if ahead and t == PANELS - 1:
                            split(p + 1, 0)
                        if chain and t == 11:
                            act.wait_ge(shifted3, p * 1)
                            nc.scalar.activation(ex3[:], ex3[:], ACT.Exp).then_inc(exp3_done, 1)
                        if ffn:
                            round_h(p - 2, t)
                        if ffn and t + 2 < S:
                            relu(p - 2, t + 2)
                        if chain and t + 2 >= S:
                            relu(c, t + 2 - S)
                        if chain and t == 0:
                            act.wait_ge(split3_used, p * 32 + 4)
                            if fin:
                                act.wait_ge(out_stored, (p - 2) * 16)
                            nc.scalar.activation(oT[:], OG[1 - odd][:], ACT.Copy).then_inc(o_copied, 1)
                        if fin and t == 0:
                            act.wait_ge(y3_done, (p - 2) * S + 2)
                            nc.scalar.activation(yTb[:], YB[1 - odd][:], ACT.Copy).then_inc(y3_copied, 1)

                act.sem_inc(o_copied, 1)
                act.sem_inc(y3_copied, 1)
                act.sem_inc(relu_done, 4)
                split(0, 0)
                over_panels(act, panel)

            @block.gpsimd
            def _(pool):
                pool.sem_inc(scaled3, 8)
                with pool.Fori(0, PANELS) as c:
                    for s in range(S):
                        pool.wait_ge(relu_done, c * S + (s + 5))
                        pool.wait_ge(cb3_in[(s // 2) % 4], (c * 2 + (s // 8 + 1)) * 16)
                        nc.gpsimd.tensor_tensor(h1[:, s % 4, :], h1[:, s % 4, :], cb1[:, (s // 2) % 4, :], ALU.mult
                                                ).then_inc(scaled3, 1)

            @block.vector
            def _(v):
                ch = Chain(v, dve3)

                def split(p, t):
                    for h in range(2):
                        v.wait_ge(hi3_done, p * 32 + (2 * t + h + 1))
                        slot = (2 * t + h) % 4
                        nc.vector.tensor_tensor(lo3[:, slot, :], raw3[:, t % RING3, h * HALF:(h + 1) * HALF],
                                                hi3[:, slot, :].bitcast(F32), ALU.subtract).then_inc(lo3_done, 1)

                def rest_h(c, s):
                    v.wait_ge(hH3_done, c * S + (s + 1))
                    nc.vector.tensor_tensor(hL1[:, s % 2, :], h1[:, s % 4, :], hH1[:, s % 2, :].bitcast(F32),
                                            ALU.subtract).then_inc(hL3_done, 1)

                def finish(p, f, odd):
                    v.wait_ge(y3_turned, f + 1)
                    v.wait_ge(o_turned, chains(p))
                    if isinstance(p, int) and p > PANELS:
                        v.wait_ge(out_stored, (p - 2) * 16)
                    nc.vector.tensor_tensor(outb[:], M2[:], x3[:, 1 - odd, :], ALU.add).then_inc(out_ready, 1)

                def rows3(p, c, odd, fin):
                    v.wait_ge(o_turned, p * 1)
                    v.wait_ge(xb3_in, p * 16)
                    if fin:
                        v.wait_ge(out_ready, p - 2)
                    for b in range(BPP):
                        blk = slice(b * P, (b + 1) * P)
                        ins = nc.vector.scalar_tensor_tensor(out=x3[:, 1 - odd, blk], in0=M1[:, blk],
                                                             scalar=dinv[:, bass.ds(c * BPP + b, 1)],
                                                             in1=xbt[:, blk], op0=ALU.mult, op1=ALU.add)
                    ins.then_inc(x3_done, 1)

                def stats_rows3(p, odd):
                    v.wait_ge(x3_done, p * 1)
                    hold(nc.vector, scrap_v[:])
                    for b in range(BPP):
                        ch.mark(nc.vector.bn_stats(st3[:, b, :], x3[:, 1 - odd, b * P:(b + 1) * P]))
                    ch.sync()
                    hold(nc.vector, scrap_v[:])
                    for b in range(BPP):
                        ch.mark(nc.vector.bn_aggr(mv3[:, b, :], st3[:, b, :]))
                    ch.sync()
                    ch.mark(nc.vector.tensor_scalar(v3[:], mv3[:, :, 1], EPS, None, ALU.add))

                def norm3(c, odd):
                    ch.sync()
                    for b in range(BPP):
                        blk = slice(b * P, (b + 1) * P)
                        ins = nc.vector.tensor_scalar(nb3[:, blk], x3[:, 1 - odd, blk], mv3[:, b, 0:1], r3[:, b:b + 1],
                                                      ALU.subtract, ALU.mult)
                    ins.then_inc(n3_ready, 1)

                def gates(p):
                    v.wait_ge(logits3_done, p * 1)
                    parts = M2[:, 0:BPP * 2 * E].rearrange("p (b s e) -> p b s e", s=2, e=E)
                    ch.mark(nc.vector.tensor_tensor(lg3[:], parts[:, :, 0, :],
                                                    gate_row[:].unsqueeze(1).to_broadcast([P, BPP, E]), ALU.add))
                    ch.sync()
                    ch.mark(nc.vector.tensor_tensor(lg3[:], lg3[:], parts[:, :, 1, :], ALU.add))
                    ch.sync()
                    hold(nc.vector, scrap_v[:])
                    for b in range(BPP):
                        ch.mark(nc.vector.max(mx3[:, b, :], lg3[:, b, :]))
                    ch.sync()
                    nc.vector.tensor_tensor(ex3[:], mx3[:, :, 1], mx3[:, :, 0], ALU.subtract).then_inc(shifted3, 1)
                    for b in range(BPP):
                        ins = nc.vector.max_index(ix3[:, b, :], mx3[:, b, :], lg3[:, b, :])
                    ch.mark(ins)

                def weights(p):
                    ch.sync()
                    ch.mark(nc.vector.tensor_copy(if3[:, :, 0:2], ix3[:, :, 0:2]))
                    v.wait_ge(exp3_done, p * 1)
                    ch.mark(nc.vector.tensor_scalar(t3[:], ex3[:], 1.0, None, ALU.add))
                    ch.sync()
                    ch.mark(nc.vector.reciprocal(t3[:], t3[:]))
                    ch.sync()
                    ch.mark(nc.vector.tensor_tensor(v3[:], t3[:], ex3[:], ALU.mult))
                    iota3 = iota_f[:].unsqueeze(1).to_broadcast([P, BPP, E])
                    ch.mark(nc.vector.tensor_tensor(m13[:], iota3, bcast(if3[:, :, 0:1], BPP), ALU.is_equal))
                    ch.mark(nc.vector.tensor_tensor(m23[:], iota3, bcast(if3[:, :, 1:2], BPP), ALU.is_equal))
                    ch.sync()
                    ch.mark(nc.vector.tensor_tensor(m13[:], m13[:], bcast(t3[:].unsqueeze(2), BPP), ALU.mult))
                    ch.mark(nc.vector.tensor_tensor(m23[:], m23[:], bcast(v3[:].unsqueeze(2), BPP), ALU.mult))
                    ch.sync()
                    nc.vector.tensor_tensor(c3[:], m13[:], m23[:], ALU.add).then_inc(c3_ready, 1)

                def panel(p, odd, tiles, chain, ffn, fin, ahead):
                    c = p - 1
                    if chain:
                        ch.rebase(c * CHAIN3)
                    for t in range(PANELS):
                        if tiles and t < PANELS - 1:
                            split(p, t + 1)
                        if ahead and t == PANELS - 1:
                            split(p + 1, 0)
                        if ffn:
                            rest_h(p - 2, t)
                        if fin and t == 2:
                            finish(p, p - 3, odd)
                        if chain and t == 2:
                            rows3(p, c, odd, fin)
                        if chain and t == 3:
                            stats_rows3(p, odd)
                        if chain and t == 4:
                            rsqrt_start(nc, ch, v3[:], r3[:], t3[:])
                            newton_step(nc, ch, v3[:], r3[:], t3[:])
                        if chain and t == 5:
                            newton_step(nc, ch, v3[:], r3[:], t3[:])
                            newton_step(nc, ch, v3[:], r3[:], t3[:])
                        if chain and t == 6:
                            norm3(c, odd)
                        if chain and t == 8:
                            v.wait_ge(n3H_done, p * 1)
                            nc.vector.tensor_tensor(n3L[:, 1 - odd, :], M1[:], n3H[:, 1 - odd, :].bitcast(F32),
                                                    ALU.subtract).then_inc(n3L_done, 1)
                        if chain and t == 10:
                            gates(p)
                        if chain and t == 11:
                            weights(p)
                    if chain:
                        assert ch.n == CHAIN3, ch.n

                v.sem_inc(lo3_done, 8)
                v.sem_inc(hL3_done, 4)
                v.sem_inc(out_stored, 16)
                v.wait_ge(gL_done, PANELS)
                split(0, 0)
                over_panels(v, panel)

            @block.tensor
            def _(pe):
                def gnn(p, t, odd):
                    for h in range(2):
                        unit = (2 * t + h) % 4
                        pe.wait_ge(lo3_done, p * 32 + (2 * t + h + 9))
                        if t == 0 and h == 0 and not (isinstance(p, int) and p < 2):
                            pe.wait_ge(o_copied, p * 1)
                        for b in range(2):
                            blk = slice((t * BPP + 2 * h + b) * P, (t * BPP + 2 * h + b + 1) * P)
                            cols = slice(b * W, (b + 1) * W)
                            first = t == 0 and h == 0 and b == 0
                            end = t == PANELS - 1 and h == 1 and b == 1
                            nc.tensor.matmul(OG[odd][:], gH[:, blk], hi3[:, unit, cols], start=first, stop=False)
                            nc.tensor.matmul(OG[odd][:], gH[:, blk], lo3[:, unit, cols], start=False, stop=False)
                            last = nc.tensor.matmul(OG[odd][:], gL[:, blk], hi3[:, unit, cols], start=False, stop=end)
                        last.then_inc(split3_used, 1)

                def z(c, s, par):
                    pe.wait_ge(relu_done, c * S + (s + 3))
                    pe.wait_ge(n3L_done, c + 1)
                    blk = slice(s * P, (s + 1) * P)
                    nc.tensor.matmul(ZB[s % 2][:], w1H1[:, blk], n3H[:, par, :], start=True, stop=False)
                    nc.tensor.matmul(ZB[s % 2][:], w1H1[:, blk], n3L[:, par, :], start=False, stop=False)
                    nc.tensor.matmul(ZB[s % 2][:], w1L1[:, blk], n3H[:, par, :], start=False, stop=True
                                     ).then_inc(z3_done, 1)

                def y(c, s, par):
                    blk = slice(s * P, (s + 1) * P)
                    if s == 0:
                        pe.wait_ge(ct3_ready, c + 1)
                        if not (isinstance(c, int) and c < 1):
                            pe.wait_ge(y3_copied, c * 1)
                        nc.tensor.matmul(YB[par][:], b2s1[:], ct1[:], start=True, stop=False)
                    pe.wait_ge(hL3_done, c * S + (s + 5))
                    nc.tensor.matmul(YB[par][:], w2H1[:, blk], hH1[:, s % 2, :], start=False, stop=False)
                    nc.tensor.matmul(YB[par][:], w2H1[:, blk], hL1[:, s % 2, :], start=False, stop=False)
                    nc.tensor.matmul(YB[par][:], w2L1[:, blk], hH1[:, s % 2, :], start=False, stop=(s == S - 1)
                                     ).then_inc(y3_done, 1)

                def turn(src, dst):
                    for b in range(BPP):
                        last = nc.tensor.transpose(dst[:, b * P:(b + 1) * P], src[:, b * P:(b + 1) * P], ident[:])
                    return last

                def panel(p, odd, tiles, chain, ffn, fin, ahead):
                    c = p - 1
                    for t in range(PANELS):
                        if tiles:
                            gnn(p, t, odd)
                        if fin and t == 1:
                            pe.wait_ge(y3_copied, p - 1)
                            pe.wait_ge(ct3_ready, chains(p - 1))
                            turn(yTb, M2).then_inc(y3_turned, 1)
                        if chain and t == 1:
                            pe.wait_ge(o_copied, p + 1)
                            turn(oT, M1).then_inc(o_turned, 1)
                        if chain and t == 7:
                            pe.wait_ge(n3_ready, p * 1)
                            turn(nb3, M1).then_inc(n3_turned, 1)
                        if chain and t == 9:
                            pe.wait_ge(n3L_done, p * 1)
                            if not (isinstance(p, int) and p < 3):
                                pe.wait_ge(out_ready, p - 2)
                            for b in range(BPP):
                                blk = slice(b * P, (b + 1) * P)
                                at = b * 2 * E
                                nc.tensor.matmul(M2[:, at:at + 2 * E], n3H[:, 1 - odd, blk], gateHL[:],
                                                 start=True, stop=False)
                                last = nc.tensor.matmul(M2[:, at:at + E], n3L[:, 1 - odd, blk], gateHL[:, 0:E],
                                                        start=False, stop=True)
                            last.then_inc(logits3_done, 1)
                        if chain and t == 12:
                            pe.wait_ge(c3_ready, p * 1)
                            for b in range(BPP):
                                last = nc.tensor.transpose(M2[0:E, b * P:(b + 1) * P], c3[:, b, :], ident[:])
                            last.then_inc(c3_turned, 1)
                        if ffn and t + 3 < S:
                            z(p - 2, t + 3, odd)
                        if chain and t + 3 >= S:
                            z(c, t + 3 - S, 1 - odd)
                        if ffn:
                            y(p - 2, t, odd)

                pe.sem_inc(split3_used, 4)
                pe.sem_inc(y3_done, 2)
                over_panels(pe, panel)


_OUT = (N, P)


def kernel(**inputs):
    import numpy as _np
    import concourse.bacc as _bacc
    from concourse import mybir as _mybir
    from concourse.bass_utils import run_bass_kernel_spmd as _run

    a = {k: _np.asarray(v) for k, v in inputs.items()}
    tiles = a["adj"].reshape(PANELS, W, PANELS, BPP, P).transpose(0, 2, 4, 3, 1)
    laid = [
        ("x", a["x"]), ("adj_tiles", tiles), ("w_gnn0", a["L0_gnn_weight"]), ("bias_gnn0", a["L0_gnn_bias"]),
        ("router_t", a["L0_ffn_router_w"].T), ("w1_0", a["L0_ffn_w1"]), ("b1_0", a["L0_ffn_b1"].T),
        ("w2_0", a["L0_ffn_w2"]), ("b2_0", a["L0_ffn_b2"]), ("w_gnn1", a["L1_gnn_weight"]),
        ("bias_gnn1", a["L1_gnn_bias"]), ("gate_w", a["L1_ffn_Wg"]), ("gate_b", a["L1_ffn_bg"]),
        ("gate_bias", a["L1_ffn_bias"]), ("w1_1", a["L1_ffn_W1"]),
        ("b1_1", a["L1_ffn_b1"].reshape(E, 2, P).transpose(2, 0, 1)), ("w2_1", a["L1_ffn_W2"]),
        ("b2_1", a["L1_ffn_b2"]),
    ]
    nc = _bacc.Bacc("TRN2", target_bir_lowering=False, num_devices=1)
    arrays, args = {}, []
    for name, v in laid:
        v = _np.ascontiguousarray(v)
        if name == "adj_tiles":
            v = v.reshape(PANELS * PANELS * P, TILE)
        arrays[name] = v
        args.append(nc.dram_tensor(name, v.shape, _mybir.dt.from_np(v.dtype), kind="ExternalInput").ap())
    args.append(nc.dram_tensor("out", _OUT, F32, kind="ExternalOutput").ap())
    program(nc, *args)
    r = _run(nc, [arrays], core_ids=[0])
    return r.results[0]["out"]
```
